# Optimizing a Trainium2 kernel written in Bass

```python
import numpy as np
import jax
import jax.numpy as jnp

def _softmax(x, axis=-1):
    return jax.nn.softmax(x, axis=axis)

def _gelu(x):
    return jax.nn.gelu(x, approximate=True)

def _silu(x):
    return jax.nn.silu(x)

def _sigmoid(x):
    return jax.nn.sigmoid(x)

def _layernorm(x, axis=-1, eps=1e-05):
    m = jnp.mean(x, axis=axis, keepdims=True)
    v = jnp.var(x, axis=axis, keepdims=True)
    return (x - m) / jnp.sqrt(v + eps)

def _scatter_add(tgt, idx, src, axis=0):
    return tgt.at[idx].add(src)

def _segment_sum(src, seg, n):
    return jax.ops.segment_sum(src, seg, n)
kernel_name = 'mk_adaln_attn_ffn_d4_seqx_r8_a2a9c1'

def setup_inputs(seed: int=0):
    np.random.seed(seed)
    _w = jnp.asarray

    def _rec_inputs():
        import jax
        import jax.numpy as jnp
        _rk = jax.random.key(seed)
        x = -0.000125 + 0.9999 * jax.random.normal(jax.random.fold_in(_rk, 1), (4, 256, 256), jnp.float32)
        _lenS = 256 - jax.random.randint(jax.random.fold_in(_rk, 7), (4,), 0, max(1, 256 // 4) + 1, jnp.int32)
        _lenS2 = 256 - jax.random.randint(jax.random.fold_in(_rk, 8), (4,), 0, max(1, 256 // 4) + 1, jnp.int32)
        fside_BxSxS_0 = -1.52775e-05 + 0.999936 * jax.random.normal(jax.random.fold_in(_rk, 11), (4, 256, 256), jnp.float32)
        cond_512 = -5.03954e-05 + 1.00559 * jax.random.normal(jax.random.fold_in(_rk, 12), (4, 64), jnp.float32)
        return (x, fside_BxSxS_0, cond_512)
    x, fside_BxSxS_0, cond_512 = _rec_inputs()

    def _L0_cond_setup():
        import jax, jax.numpy as jnp
        from jax import lax
        import numpy as np
        B, T, C, TD = (8, 256, 256, 64)

        def _bi_wkv(r, k, v, w, u, time_emb):
            tf = jax.nn.sigmoid(jnp.sum(time_emb, axis=-1))[:, None, None]
            decay = jnp.exp(-jnp.exp(w.astype(jnp.float32)))[None, :] * (0.5 + 0.5 * tf[:, :, 0])
            kf = k.astype(jnp.float32)
            vf = v.astype(jnp.float32)
            ek = jnp.exp(jnp.minimum(kf, 30.0))
            ekv = ek * vf

            def step(carry, x):
                a, b = carry
                ekv_t, ek_t = x
                a = a * decay + ekv_t
                b = b * decay + ek_t
                return ((a, b), (a, b))
            ekv_t = jnp.swapaxes(ekv, 0, 1)
            ek_t = jnp.swapaxes(ek, 0, 1)
            init = (jnp.zeros_like(decay), jnp.zeros_like(decay))
            _, (nf, df) = lax.scan(step, init, (ekv_t, ek_t))
            _, (nb, db) = lax.scan(step, init, (ekv_t, ek_t), reverse=True)
            nf = jnp.swapaxes(nf, 0, 1)
            df = jnp.swapaxes(df, 0, 1)
            nb = jnp.swapaxes(nb, 0, 1)
            db = jnp.swapaxes(db, 0, 1)
            euk = jnp.exp(jnp.minimum(u.astype(jnp.float32)[None, None, :] + kf, 30.0))
            num = nf + nb - ekv + euk * vf
            den = df + db - ek + euk
            base = jax.nn.sigmoid(r.astype(jnp.float32)) * (num / jnp.maximum(den, 1e-08))
            out = base * (0.8 + 0.2 * tf)
            return out.astype(r.dtype)
        key = jax.random.key(seed)
        ks = jax.random.split(key, 6)
        return {'r': jax.random.normal(ks[0], (B, T, C), dtype=jnp.float32), 'k': jax.random.normal(ks[1], (B, T, C), dtype=jnp.float32), 'v': jax.random.normal(ks[2], (B, T, C), dtype=jnp.float32), 'w': jax.random.normal(ks[3], (C,), dtype=jnp.float32), 'u': jax.random.normal(ks[4], (C,), dtype=jnp.float32), 'time_emb': jax.random.normal(ks[5], (B, TD), dtype=jnp.float32)}
    _L0_cond_all = _L0_cond_setup()
    _L0_cond_in = {k: v for k, v in _L0_cond_all.items() if k in ('w', 'u')}
    del _L0_cond_all

    def _L0_attn_setup():
        import jax, jax.numpy as jnp
        import numpy as np
        NUM_HEADS = 16
        HIDDEN = 256
        HEAD_DIM = HIDDEN // NUM_HEADS
        ROTARY_DIM = HEAD_DIM // 4
        ROPE_BASE = 10000.0

        def _rope_angles(seq_len, dtype=jnp.float32):
            inv_freq = 1.0 / ROPE_BASE ** (jnp.arange(0, ROTARY_DIM, 2, dtype=dtype) / ROTARY_DIM)
            t = jnp.arange(seq_len, dtype=dtype)
            freqs = jnp.einsum('s,d->sd', t, inv_freq)
            emb = jnp.concatenate([freqs, freqs], axis=-1)
            return (jnp.cos(emb), jnp.sin(emb))

        def _rotate_half(x):
            x1, x2 = jnp.split(x, 2, axis=-1)
            return jnp.concatenate([-x2, x1], axis=-1)
        key = jax.random.key(seed)
        k1, k2, k3 = jax.random.split(key, 3)
        B, S = (2, 256)
        scale_qkv = 1.0 / np.sqrt(HIDDEN)
        return {'hidden_states': jax.random.normal(k1, (B, S, HIDDEN), dtype=jnp.float32), 'w_qkv': jax.random.normal(k2, (HIDDEN, 3 * HIDDEN), dtype=jnp.float32) * scale_qkv, 'b_qkv': jnp.zeros((3 * HIDDEN,), dtype=jnp.float32), 'w_out': jax.random.normal(k3, (HIDDEN, HIDDEN), dtype=jnp.float32) * scale_qkv, 'b_out': jnp.zeros((HIDDEN,), dtype=jnp.float32)}
    _L0_attn_all = _L0_attn_setup()
    _L0_attn_in = {k: v for k, v in _L0_attn_all.items() if k in ('w_qkv', 'b_qkv', 'w_out', 'b_out')}
    del _L0_attn_all

    def _L0_cond2_setup():
        import jax, jax.numpy as jnp
        from jax import lax
        import numpy as np
        B, T, C, TD = (8, 256, 256, 64)

        def _bi_wkv(r, k, v, w, u, time_emb):
            tf = jax.nn.sigmoid(jnp.sum(time_emb, axis=-1))[:, None, None]
            decay = jnp.exp(-jnp.exp(w.astype(jnp.float32)))[None, :] * (0.5 + 0.5 * tf[:, :, 0])
            kf = k.astype(jnp.float32)
            vf = v.astype(jnp.float32)
            ek = jnp.exp(jnp.minimum(kf, 30.0))
            ekv = ek * vf

            def step(carry, x):
                a, b = carry
                ekv_t, ek_t = x
                a = a * decay + ekv_t
                b = b * decay + ek_t
                return ((a, b), (a, b))
            ekv_t = jnp.swapaxes(ekv, 0, 1)
            ek_t = jnp.swapaxes(ek, 0, 1)
            init = (jnp.zeros_like(decay), jnp.zeros_like(decay))
            _, (nf, df) = lax.scan(step, init, (ekv_t, ek_t))
            _, (nb, db) = lax.scan(step, init, (ekv_t, ek_t), reverse=True)
            nf = jnp.swapaxes(nf, 0, 1)
            df = jnp.swapaxes(df, 0, 1)
            nb = jnp.swapaxes(nb, 0, 1)
            db = jnp.swapaxes(db, 0, 1)
            euk = jnp.exp(jnp.minimum(u.astype(jnp.float32)[None, None, :] + kf, 30.0))
            num = nf + nb - ekv + euk * vf
            den = df + db - ek + euk
            base = jax.nn.sigmoid(r.astype(jnp.float32)) * (num / jnp.maximum(den, 1e-08))
            out = base * (0.8 + 0.2 * tf)
            return out.astype(r.dtype)
        key = jax.random.key(seed)
        ks = jax.random.split(key, 6)
        return {'r': jax.random.normal(ks[0], (B, T, C), dtype=jnp.float32), 'k': jax.random.normal(ks[1], (B, T, C), dtype=jnp.float32), 'v': jax.random.normal(ks[2], (B, T, C), dtype=jnp.float32), 'w': jax.random.normal(ks[3], (C,), dtype=jnp.float32), 'u': jax.random.normal(ks[4], (C,), dtype=jnp.float32), 'time_emb': jax.random.normal(ks[5], (B, TD), dtype=jnp.float32)}
    _L0_cond2_all = _L0_cond2_setup()
    _L0_cond2_in = {k: v for k, v in _L0_cond2_all.items() if k in ('w', 'u')}
    del _L0_cond2_all

    def _L0_ffn_setup():
        import jax, jax.numpy as jnp
        import numpy as np
        from jax import lax
        H = 256
        I = 176
        E = 16
        TOP_K = 6
        IS = 2 * I

        def _swiglu(x, w13_, w2_):
            gu = x @ w13_.T
            g, u = jnp.split(gu, 2, axis=-1)
            return jax.nn.silu(g) * u @ w2_.T
        key = jax.random.key(seed)
        ks = jax.random.split(key, 6)
        return {'hidden_states': jax.random.normal(ks[0], (1, 256, H), jnp.float32), 'gate_w': jax.random.normal(ks[1], (E, H), jnp.float32) * 0.02, 'w13': jax.random.normal(ks[2], (E, 2 * I, H), jnp.float32) * 0.02, 'w2': jax.random.normal(ks[3], (E, H, I), jnp.float32) * 0.02, 'sw13': jax.random.normal(ks[4], (2 * IS, H), jnp.float32) * 0.02, 'sw2': jax.random.normal(ks[5], (H, IS), jnp.float32) * 0.02}
    _L0_ffn_all = _L0_ffn_setup()
    _L0_ffn_in = {k: v for k, v in _L0_ffn_all.items() if k in ('gate_w', 'w13', 'w2', 'sw13', 'sw2')}
    del _L0_ffn_all

    def _L1_cond_setup():
        import jax, jax.numpy as jnp
        from jax import lax
        import numpy as np
        B, T, C, TD = (8, 256, 256, 64)

        def _bi_wkv(r, k, v, w, u, time_emb):
            tf = jax.nn.sigmoid(jnp.sum(time_emb, axis=-1))[:, None, None]
            decay = jnp.exp(-jnp.exp(w.astype(jnp.float32)))[None, :] * (0.5 + 0.5 * tf[:, :, 0])
            kf = k.astype(jnp.float32)
            vf = v.astype(jnp.float32)
            ek = jnp.exp(jnp.minimum(kf, 30.0))
            ekv = ek * vf

            def step(carry, x):
                a, b = carry
                ekv_t, ek_t = x
                a = a * decay + ekv_t
                b = b * decay + ek_t
                return ((a, b), (a, b))
            ekv_t = jnp.swapaxes(ekv, 0, 1)
            ek_t = jnp.swapaxes(ek, 0, 1)
            init = (jnp.zeros_like(decay), jnp.zeros_like(decay))
            _, (nf, df) = lax.scan(step, init, (ekv_t, ek_t))
            _, (nb, db) = lax.scan(step, init, (ekv_t, ek_t), reverse=True)
            nf = jnp.swapaxes(nf, 0, 1)
            df = jnp.swapaxes(df, 0, 1)
            nb = jnp.swapaxes(nb, 0, 1)
            db = jnp.swapaxes(db, 0, 1)
            euk = jnp.exp(jnp.minimum(u.astype(jnp.float32)[None, None, :] + kf, 30.0))
            num = nf + nb - ekv + euk * vf
            den = df + db - ek + euk
            base = jax.nn.sigmoid(r.astype(jnp.float32)) * (num / jnp.maximum(den, 1e-08))
            out = base * (0.8 + 0.2 * tf)
            return out.astype(r.dtype)
        key = jax.random.key(seed)
        ks = jax.random.split(key, 6)
        return {'r': jax.random.normal(ks[0], (B, T, C), dtype=jnp.float32), 'k': jax.random.normal(ks[1], (B, T, C), dtype=jnp.float32), 'v': jax.random.normal(ks[2], (B, T, C), dtype=jnp.float32), 'w': jax.random.normal(ks[3], (C,), dtype=jnp.float32), 'u': jax.random.normal(ks[4], (C,), dtype=jnp.float32), 'time_emb': jax.random.normal(ks[5], (B, TD), dtype=jnp.float32)}
    _L1_cond_all = _L1_cond_setup()
    _L1_cond_in = {k: v for k, v in _L1_cond_all.items() if k in ('w', 'u')}
    del _L1_cond_all

    def _L1_attn_setup():
        import jax, jax.numpy as jnp
        import numpy as np
        B, SQ, H = (2, 256, 256)
        NH = 16
        HN = H // NH
        key = jax.random.key(seed)
        ks = jax.random.split(key, 6)
        query = jax.random.normal(ks[0], (B, SQ, H), dtype=jnp.float32)
        k_in = jax.random.normal(ks[1], (B, SQ, H), dtype=jnp.float32)
        v_in = jax.random.normal(ks[2], (B, SQ, H), dtype=jnp.float32)
        Wqkv = jax.random.normal(ks[3], (3 * H, H), dtype=jnp.float32) * (1.0 / np.sqrt(H))
        Wproj = jax.random.normal(ks[4], (H, H), dtype=jnp.float32) * (1.0 / np.sqrt(H))
        bproj = jnp.zeros((H,), dtype=jnp.float32)
        return {'query': query, 'key': k_in, 'value': v_in, 'Wqkv': Wqkv, 'Wproj': Wproj, 'bproj': bproj}
    _L1_attn_all = _L1_attn_setup()
    _L1_attn_in = {k: v for k, v in _L1_attn_all.items() if k in ('key', 'value', 'Wqkv', 'Wproj', 'bproj')}
    del _L1_attn_all

    def _L1_cond2_setup():
        import jax, jax.numpy as jnp
        from jax import lax
        import numpy as np
        B, T, C, TD = (8, 256, 256, 64)

        def _bi_wkv(r, k, v, w, u, time_emb):
            tf = jax.nn.sigmoid(jnp.sum(time_emb, axis=-1))[:, None, None]
            decay = jnp.exp(-jnp.exp(w.astype(jnp.float32)))[None, :] * (0.5 + 0.5 * tf[:, :, 0])
            kf = k.astype(jnp.float32)
            vf = v.astype(jnp.float32)
            ek = jnp.exp(jnp.minimum(kf, 30.0))
            ekv = ek * vf

            def step(carry, x):
                a, b = carry
                ekv_t, ek_t = x
                a = a * decay + ekv_t
                b = b * decay + ek_t
                return ((a, b), (a, b))
            ekv_t = jnp.swapaxes(ekv, 0, 1)
            ek_t = jnp.swapaxes(ek, 0, 1)
            init = (jnp.zeros_like(decay), jnp.zeros_like(decay))
            _, (nf, df) = lax.scan(step, init, (ekv_t, ek_t))
            _, (nb, db) = lax.scan(step, init, (ekv_t, ek_t), reverse=True)
            nf = jnp.swapaxes(nf, 0, 1)
            df = jnp.swapaxes(df, 0, 1)
            nb = jnp.swapaxes(nb, 0, 1)
            db = jnp.swapaxes(db, 0, 1)
            euk = jnp.exp(jnp.minimum(u.astype(jnp.float32)[None, None, :] + kf, 30.0))
            num = nf + nb - ekv + euk * vf
            den = df + db - ek + euk
            base = jax.nn.sigmoid(r.astype(jnp.float32)) * (num / jnp.maximum(den, 1e-08))
            out = base * (0.8 + 0.2 * tf)
            return out.astype(r.dtype)
        key = jax.random.key(seed)
        ks = jax.random.split(key, 6)
        return {'r': jax.random.normal(ks[0], (B, T, C), dtype=jnp.float32), 'k': jax.random.normal(ks[1], (B, T, C), dtype=jnp.float32), 'v': jax.random.normal(ks[2], (B, T, C), dtype=jnp.float32), 'w': jax.random.normal(ks[3], (C,), dtype=jnp.float32), 'u': jax.random.normal(ks[4], (C,), dtype=jnp.float32), 'time_emb': jax.random.normal(ks[5], (B, TD), dtype=jnp.float32)}
    _L1_cond2_all = _L1_cond2_setup()
    _L1_cond2_in = {k: v for k, v in _L1_cond2_all.items() if k in ('w', 'u')}
    del _L1_cond2_all

    def _L1_ffn_setup():
        import jax, jax.numpy as jnp
        import numpy as np
        B, S, H, I, E = (2, 256, 256, 176, 8)
        TOP_K = 2
        key = jax.random.key(seed)
        k0, k1, k2, k3, k4 = jax.random.split(key, 5)
        scale = float(np.sqrt(2.0 / (H + I)))
        return {'hidden_states': jax.random.normal(k0, (B, S, H), dtype=jnp.float32), 'router_w': jax.random.normal(k1, (E, H), dtype=jnp.float32) * H ** (-0.5), 'gate_w': jax.random.normal(k2, (E, I, H), dtype=jnp.float32) * scale, 'up_w': jax.random.normal(k3, (E, I, H), dtype=jnp.float32) * scale, 'down_w': jax.random.normal(k4, (E, H, I), dtype=jnp.float32) * scale}
    _L1_ffn_all = _L1_ffn_setup()
    _L1_ffn_in = {k: v for k, v in _L1_ffn_all.items() if k in ('router_w', 'gate_w', 'up_w', 'down_w')}
    del _L1_ffn_all

    def _L2_cond_setup():
        import jax, jax.numpy as jnp
        from jax import lax
        import numpy as np
        B, T, C, TD = (8, 256, 256, 64)

        def _bi_wkv(r, k, v, w, u, time_emb):
            tf = jax.nn.sigmoid(jnp.sum(time_emb, axis=-1))[:, None, None]
            decay = jnp.exp(-jnp.exp(w.astype(jnp.float32)))[None, :] * (0.5 + 0.5 * tf[:, :, 0])
            kf = k.astype(jnp.float32)
            vf = v.astype(jnp.float32)
            ek = jnp.exp(jnp.minimum(kf, 30.0))
            ekv = ek * vf

            def step(carry, x):
                a, b = carry
                ekv_t, ek_t = x
                a = a * decay + ekv_t
                b = b * decay + ek_t
                return ((a, b), (a, b))
            ekv_t = jnp.swapaxes(ekv, 0, 1)
            ek_t = jnp.swapaxes(ek, 0, 1)
            init = (jnp.zeros_like(decay), jnp.zeros_like(decay))
            _, (nf, df) = lax.scan(step, init, (ekv_t, ek_t))
            _, (nb, db) = lax.scan(step, init, (ekv_t, ek_t), reverse=True)
            nf = jnp.swapaxes(nf, 0, 1)
            df = jnp.swapaxes(df, 0, 1)
            nb = jnp.swapaxes(nb, 0, 1)
            db = jnp.swapaxes(db, 0, 1)
            euk = jnp.exp(jnp.minimum(u.astype(jnp.float32)[None, None, :] + kf, 30.0))
            num = nf + nb - ekv + euk * vf
            den = df + db - ek + euk
            base = jax.nn.sigmoid(r.astype(jnp.float32)) * (num / jnp.maximum(den, 1e-08))
            out = base * (0.8 + 0.2 * tf)
            return out.astype(r.dtype)
        key = jax.random.key(seed)
        ks = jax.random.split(key, 6)
        return {'r': jax.random.normal(ks[0], (B, T, C), dtype=jnp.float32), 'k': jax.random.normal(ks[1], (B, T, C), dtype=jnp.float32), 'v': jax.random.normal(ks[2], (B, T, C), dtype=jnp.float32), 'w': jax.random.normal(ks[3], (C,), dtype=jnp.float32), 'u': jax.random.normal(ks[4], (C,), dtype=jnp.float32), 'time_emb': jax.random.normal(ks[5], (B, TD), dtype=jnp.float32)}
    _L2_cond_all = _L2_cond_setup()
    _L2_cond_in = {k: v for k, v in _L2_cond_all.items() if k in ('w', 'u')}
    del _L2_cond_all

    def _L2_attn_setup():
        import jax, jax.numpy as jnp
        import numpy as np
        B_SZ, T, D, N = (4, 256, 256, 64)

        def _reference_tuple_inner(x, A, B, C_w, C_b, D_w, D_b, log_delta):
            A_diag = jnp.exp(-jax.nn.softplus(log_delta))
            x_proj = (x @ C_w.T + C_b) * jax.nn.sigmoid(x @ D_w.T + D_b)
            xp_t = jnp.transpose(x_proj, (1, 0, 2))

            def step(g, xt):
                g = g * A_diag + xt
                return (g, g)
            g_last, gs = jax.lax.scan(step, jnp.zeros((x.shape[0], x.shape[2]), x.dtype), xp_t)
            gs = jnp.transpose(gs, (1, 0, 2))
            AB = jnp.sum(A * B, axis=-1)
            output = gs * AB
            h = g_last[:, :, None] * B[None, :, :]
            return (output, h)
        key = jax.random.key(seed)
        ks = jax.random.split(key, 8)
        s = 1.0 / np.sqrt(D)
        return {'x': jax.random.normal(ks[0], (B_SZ, T, D), dtype=jnp.float32), 'A': jax.random.normal(ks[1], (D, N), dtype=jnp.float32), 'B': jax.random.normal(ks[2], (D, N), dtype=jnp.float32), 'C_w': jax.random.uniform(ks[3], (D, D), jnp.float32, -s, s), 'C_b': jax.random.uniform(ks[4], (D,), jnp.float32, -s, s), 'D_w': jax.random.uniform(ks[5], (D, D), jnp.float32, -s, s), 'D_b': jax.random.uniform(ks[6], (D,), jnp.float32, -s, s), 'log_delta': jnp.zeros((D,), dtype=jnp.float32)}
    _L2_attn_all = _L2_attn_setup()
    _L2_attn_in = {k: v for k, v in _L2_attn_all.items() if k in ('A', 'B', 'C_w', 'C_b', 'D_w', 'D_b', 'log_delta')}
    del _L2_attn_all

    def _L2_cond2_setup():
        import jax, jax.numpy as jnp
        from jax import lax
        import numpy as np
        B, T, C, TD = (8, 256, 256, 64)

        def _bi_wkv(r, k, v, w, u, time_emb):
            tf = jax.nn.sigmoid(jnp.sum(time_emb, axis=-1))[:, None, None]
            decay = jnp.exp(-jnp.exp(w.astype(jnp.float32)))[None, :] * (0.5 + 0.5 * tf[:, :, 0])
            kf = k.astype(jnp.float32)
            vf = v.astype(jnp.float32)
            ek = jnp.exp(jnp.minimum(kf, 30.0))
            ekv = ek * vf

            def step(carry, x):
                a, b = carry
                ekv_t, ek_t = x
                a = a * decay + ekv_t
                b = b * decay + ek_t
                return ((a, b), (a, b))
            ekv_t = jnp.swapaxes(ekv, 0, 1)
            ek_t = jnp.swapaxes(ek, 0, 1)
            init = (jnp.zeros_like(decay), jnp.zeros_like(decay))
            _, (nf, df) = lax.scan(step, init, (ekv_t, ek_t))
            _, (nb, db) = lax.scan(step, init, (ekv_t, ek_t), reverse=True)
            nf = jnp.swapaxes(nf, 0, 1)
            df = jnp.swapaxes(df, 0, 1)
            nb = jnp.swapaxes(nb, 0, 1)
            db = jnp.swapaxes(db, 0, 1)
            euk = jnp.exp(jnp.minimum(u.astype(jnp.float32)[None, None, :] + kf, 30.0))
            num = nf + nb - ekv + euk * vf
            den = df + db - ek + euk
            base = jax.nn.sigmoid(r.astype(jnp.float32)) * (num / jnp.maximum(den, 1e-08))
            out = base * (0.8 + 0.2 * tf)
            return out.astype(r.dtype)
        key = jax.random.key(seed)
        ks = jax.random.split(key, 6)
        return {'r': jax.random.normal(ks[0], (B, T, C), dtype=jnp.float32), 'k': jax.random.normal(ks[1], (B, T, C), dtype=jnp.float32), 'v': jax.random.normal(ks[2], (B, T, C), dtype=jnp.float32), 'w': jax.random.normal(ks[3], (C,), dtype=jnp.float32), 'u': jax.random.normal(ks[4], (C,), dtype=jnp.float32), 'time_emb': jax.random.normal(ks[5], (B, TD), dtype=jnp.float32)}
    _L2_cond2_all = _L2_cond2_setup()
    _L2_cond2_in = {k: v for k, v in _L2_cond2_all.items() if k in ('w', 'u')}
    del _L2_cond2_all

    def _L2_ffn_setup():
        import jax, jax.numpy as jnp
        import numpy as np
        EPS = 1e-05
        RMS_EPS = 1e-06

        def activation_quant(x, num_bits=8):
            qn = -2 ** (num_bits - 1)
            qp = 2 ** (num_bits - 1) - 1
            xf = x.astype(jnp.float32)
            s = qp / jnp.clip(jnp.max(jnp.abs(xf), axis=-1, keepdims=True), EPS, None)
            return (jnp.clip(jnp.round(xf * s), qn, qp) / s).astype(x.dtype)

        def weight_quant(w):
            wf = w.astype(jnp.float32)
            s = 1.0 / jnp.clip(jnp.mean(jnp.abs(wf)), EPS, None)
            return (jnp.clip(jnp.round(wf * s), -1.0, 1.0) / s).astype(w.dtype)

        def bit_linear(x, w):
            qx = x + jax.lax.stop_gradient(activation_quant(x) - x)
            qw = w + jax.lax.stop_gradient(weight_quant(w) - w)
            return jnp.einsum('bsh,oh->bso', qx, qw)

        def rms_norm(x, weight, eps=RMS_EPS):
            xf = x.astype(jnp.float32)
            var = jnp.mean(xf * xf, axis=-1, keepdims=True)
            return weight * (xf * jax.lax.rsqrt(var + eps)).astype(x.dtype)
        key = jax.random.key(seed)
        k1, k2, k3, k4 = jax.random.split(key, 4)
        B, S, H, I = (2, 256, 256, 1024)
        scale = 1.0 / np.sqrt(H)
        return {'x': jax.random.normal(k1, (B, S, H), dtype=jnp.float32), 'w_gate': jax.random.normal(k2, (I, H), dtype=jnp.float32) * scale, 'w_up': jax.random.normal(k3, (I, H), dtype=jnp.float32) * scale, 'w_down': jax.random.normal(k4, (H, I), dtype=jnp.float32) * (1.0 / np.sqrt(I)), 'ln_weight': jnp.ones((I,), dtype=jnp.float32)}
    _L2_ffn_all = _L2_ffn_setup()
    _L2_ffn_in = {k: v for k, v in _L2_ffn_all.items() if k in ('w_gate', 'w_up', 'w_down', 'ln_weight')}
    del _L2_ffn_all

    def _L3_cond_setup():
        import jax, jax.numpy as jnp
        from jax import lax
        import numpy as np
        B, T, C, TD = (8, 256, 256, 64)

        def _bi_wkv(r, k, v, w, u, time_emb):
            tf = jax.nn.sigmoid(jnp.sum(time_emb, axis=-1))[:, None, None]
            decay = jnp.exp(-jnp.exp(w.astype(jnp.float32)))[None, :] * (0.5 + 0.5 * tf[:, :, 0])
            kf = k.astype(jnp.float32)
            vf = v.astype(jnp.float32)
            ek = jnp.exp(jnp.minimum(kf, 30.0))
            ekv = ek * vf

            def step(carry, x):
                a, b = carry
                ekv_t, ek_t = x
                a = a * decay + ekv_t
                b = b * decay + ek_t
                return ((a, b), (a, b))
            ekv_t = jnp.swapaxes(ekv, 0, 1)
            ek_t = jnp.swapaxes(ek, 0, 1)
            init = (jnp.zeros_like(decay), jnp.zeros_like(decay))
            _, (nf, df) = lax.scan(step, init, (ekv_t, ek_t))
            _, (nb, db) = lax.scan(step, init, (ekv_t, ek_t), reverse=True)
            nf = jnp.swapaxes(nf, 0, 1)
            df = jnp.swapaxes(df, 0, 1)
            nb = jnp.swapaxes(nb, 0, 1)
            db = jnp.swapaxes(db, 0, 1)
            euk = jnp.exp(jnp.minimum(u.astype(jnp.float32)[None, None, :] + kf, 30.0))
            num = nf + nb - ekv + euk * vf
            den = df + db - ek + euk
            base = jax.nn.sigmoid(r.astype(jnp.float32)) * (num / jnp.maximum(den, 1e-08))
            out = base * (0.8 + 0.2 * tf)
            return out.astype(r.dtype)
        key = jax.random.key(seed)
        ks = jax.random.split(key, 6)
        return {'r': jax.random.normal(ks[0], (B, T, C), dtype=jnp.float32), 'k': jax.random.normal(ks[1], (B, T, C), dtype=jnp.float32), 'v': jax.random.normal(ks[2], (B, T, C), dtype=jnp.float32), 'w': jax.random.normal(ks[3], (C,), dtype=jnp.float32), 'u': jax.random.normal(ks[4], (C,), dtype=jnp.float32), 'time_emb': jax.random.normal(ks[5], (B, TD), dtype=jnp.float32)}
    _L3_cond_all = _L3_cond_setup()
    _L3_cond_in = {k: v for k, v in _L3_cond_all.items() if k in ('w', 'u')}
    del _L3_cond_all

    def _L3_attn_setup():
        import jax, jax.numpy as jnp
        import numpy as np
        B, T, C = (2, 256, 256)
        NH, NKV, HD = (16, 8, 32)
        SOFTCAP = 50.0
        ROPE_BASE = 10000.0

        def _rotate_half(x):
            x1, x2 = (x[..., :x.shape[-1] // 2], x[..., x.shape[-1] // 2:])
            return jnp.concatenate((-x2, x1), axis=-1)

        def _rope_cos_sin(t, head_dim, dtype):
            inv_freq = 1.0 / ROPE_BASE ** (jnp.arange(0, head_dim, 2, dtype=jnp.int32).astype(jnp.float32) / head_dim)
            pos = jnp.arange(t, dtype=jnp.float32)
            freqs = pos[:, None] * inv_freq[None, :]
            emb = jnp.concatenate((freqs, freqs), axis=-1)
            return (jnp.cos(emb).astype(dtype)[None, None], jnp.sin(emb).astype(dtype)[None, None])
        key = jax.random.key(seed)
        ks = jax.random.split(key, 5)
        s = 0.02
        return {'X': jax.random.normal(ks[0], (B, T, C), dtype=jnp.float32), 'Wq': jax.random.normal(ks[1], (C, NH * HD), dtype=jnp.float32) * s, 'Wk': jax.random.normal(ks[2], (C, NKV * HD), dtype=jnp.float32) * s, 'Wv': jax.random.normal(ks[3], (C, NKV * HD), dtype=jnp.float32) * s, 'Wo': jax.random.normal(ks[4], (NH * HD, C), dtype=jnp.float32) * s}
    _L3_attn_all = _L3_attn_setup()
    _L3_attn_in = {k: v for k, v in _L3_attn_all.items() if k in ('Wq', 'Wk', 'Wv', 'Wo')}
    del _L3_attn_all

    def _L3_cond2_setup():
        import jax, jax.numpy as jnp
        from jax import lax
        import numpy as np
        B, T, C, TD = (8, 256, 256, 64)

        def _bi_wkv(r, k, v, w, u, time_emb):
            tf = jax.nn.sigmoid(jnp.sum(time_emb, axis=-1))[:, None, None]
            decay = jnp.exp(-jnp.exp(w.astype(jnp.float32)))[None, :] * (0.5 + 0.5 * tf[:, :, 0])
            kf = k.astype(jnp.float32)
            vf = v.astype(jnp.float32)
            ek = jnp.exp(jnp.minimum(kf, 30.0))
            ekv = ek * vf

            def step(carry, x):
                a, b = carry
                ekv_t, ek_t = x
                a = a * decay + ekv_t
                b = b * decay + ek_t
                return ((a, b), (a, b))
            ekv_t = jnp.swapaxes(ekv, 0, 1)
            ek_t = jnp.swapaxes(ek, 0, 1)
            init = (jnp.zeros_like(decay), jnp.zeros_like(decay))
            _, (nf, df) = lax.scan(step, init, (ekv_t, ek_t))
            _, (nb, db) = lax.scan(step, init, (ekv_t, ek_t), reverse=True)
            nf = jnp.swapaxes(nf, 0, 1)
            df = jnp.swapaxes(df, 0, 1)
            nb = jnp.swapaxes(nb, 0, 1)
            db = jnp.swapaxes(db, 0, 1)
            euk = jnp.exp(jnp.minimum(u.astype(jnp.float32)[None, None, :] + kf, 30.0))
            num = nf + nb - ekv + euk * vf
            den = df + db - ek + euk
            base = jax.nn.sigmoid(r.astype(jnp.float32)) * (num / jnp.maximum(den, 1e-08))
            out = base * (0.8 + 0.2 * tf)
            return out.astype(r.dtype)
        key = jax.random.key(seed)
        ks = jax.random.split(key, 6)
        return {'r': jax.random.normal(ks[0], (B, T, C), dtype=jnp.float32), 'k': jax.random.normal(ks[1], (B, T, C), dtype=jnp.float32), 'v': jax.random.normal(ks[2], (B, T, C), dtype=jnp.float32), 'w': jax.random.normal(ks[3], (C,), dtype=jnp.float32), 'u': jax.random.normal(ks[4], (C,), dtype=jnp.float32), 'time_emb': jax.random.normal(ks[5], (B, TD), dtype=jnp.float32)}
    _L3_cond2_all = _L3_cond2_setup()
    _L3_cond2_in = {k: v for k, v in _L3_cond2_all.items() if k in ('w', 'u')}
    del _L3_cond2_all

    def _L3_ffn_setup():
        import jax, jax.numpy as jnp
        import numpy as np
        import math
        GOLDEN_CENTER = 1.0 / math.e
        GOLDEN_LOWER = 0.5 - math.log(4.0 / 3.0)
        GOLDEN_UPPER = 0.5
        B, T, D = (4, 128, 256)
        E = 8
        F = 1024 // (E // 2)
        R = 64
        NL = 2

        def _router_weights(x, Wr, temperature):
            logits = jnp.einsum('btd,de->bte', x, Wr)
            inhibition = jax.nn.sigmoid(logits / temperature)
            in_zone = (inhibition >= GOLDEN_LOWER) & (inhibition <= GOLDEN_UPPER)
            distance = jnp.abs(inhibition - GOLDEN_CENTER)
            w = jnp.exp(-distance / 0.1) * in_zone.astype(x.dtype)
            wsum = w.sum(axis=-1, keepdims=True)
            no_expert = wsum < 1e-08
            fb = jnp.exp(-distance / 0.3)
            _, top2 = jax.lax.top_k(fb, 2)
            fb_mask = jax.nn.one_hot(top2, E, dtype=x.dtype).sum(axis=-2)
            fb_w = fb * fb_mask
            fb_w = fb_w / jnp.clip(fb_w.sum(axis=-1, keepdims=True), 1e-08)
            w = jnp.where(no_expert, fb_w, w)
            return w / jnp.clip(w.sum(axis=-1, keepdims=True), 1e-08)
        key = jax.random.key(seed)
        ks = jax.random.split(key, 13)
        s = 0.02
        x = jax.random.normal(ks[0], (B, T, D), dtype=jnp.float32)
        Wg = jax.random.normal(ks[1], (E, D, F), dtype=jnp.float32) * s
        Wu = jax.random.normal(ks[2], (E, D, F), dtype=jnp.float32) * s
        Wd = jax.random.normal(ks[3], (E, F, D), dtype=jnp.float32) * s
        Ga = jax.random.normal(ks[4], (NL, D, R), dtype=jnp.float32) * s
        Gb = jax.random.normal(ks[5], (NL, R, F), dtype=jnp.float32) * s
        Ua = jax.random.normal(ks[6], (NL, D, R), dtype=jnp.float32) * s
        Ub = jax.random.normal(ks[7], (NL, R, F), dtype=jnp.float32) * s
        Da = jax.random.normal(ks[8], (NL, F, R), dtype=jnp.float32) * s
        Db = jax.random.normal(ks[9], (NL, R, D), dtype=jnp.float32) * s
        Wr = jax.random.normal(ks[10], (D, E), dtype=jnp.float32) * s
        temperature = jnp.ones((1,), dtype=jnp.float32)
        return {'x': x, 'Wg': Wg, 'Wu': Wu, 'Wd': Wd, 'Ga': Ga, 'Gb': Gb, 'Ua': Ua, 'Ub': Ub, 'Da': Da, 'Db': Db, 'Wr': Wr, 'temperature': temperature}
    _L3_ffn_all = _L3_ffn_setup()
    _L3_ffn_in = {k: v for k, v in _L3_ffn_all.items() if k in ('Wg', 'Wu', 'Wd', 'Ga', 'Gb', 'Ua', 'Ub', 'Da', 'Db', 'Wr', 'temperature')}
    del _L3_ffn_all
    return {'x': x, 'fside_BxSxS_0': fside_BxSxS_0, 'cond_512': cond_512, 'L0_cond_w': _L0_cond_in['w'], 'L0_cond_u': _L0_cond_in['u'], 'L0_attn_w_qkv': _L0_attn_in['w_qkv'], 'L0_attn_b_qkv': _L0_attn_in['b_qkv'], 'L0_attn_w_out': _L0_attn_in['w_out'], 'L0_attn_b_out': _L0_attn_in['b_out'], 'L0_cond2_w': _L0_cond2_in['w'], 'L0_cond2_u': _L0_cond2_in['u'], 'L0_ffn_gate_w': _L0_ffn_in['gate_w'], 'L0_ffn_w13': _L0_ffn_in['w13'], 'L0_ffn_w2': _L0_ffn_in['w2'], 'L0_ffn_sw13': _L0_ffn_in['sw13'], 'L0_ffn_sw2': _L0_ffn_in['sw2'], 'L1_cond_w': _L1_cond_in['w'], 'L1_cond_u': _L1_cond_in['u'], 'L1_attn_key': _L1_attn_in['key'], 'L1_attn_value': _L1_attn_in['value'], 'L1_attn_Wqkv': _L1_attn_in['Wqkv'], 'L1_attn_Wproj': _L1_attn_in['Wproj'], 'L1_attn_bproj': _L1_attn_in['bproj'], 'L1_cond2_w': _L1_cond2_in['w'], 'L1_cond2_u': _L1_cond2_in['u'], 'L1_ffn_router_w': _L1_ffn_in['router_w'], 'L1_ffn_gate_w': _L1_ffn_in['gate_w'], 'L1_ffn_up_w': _L1_ffn_in['up_w'], 'L1_ffn_down_w': _L1_ffn_in['down_w'], 'L2_cond_w': _L2_cond_in['w'], 'L2_cond_u': _L2_cond_in['u'], 'L2_attn_A': _L2_attn_in['A'], 'L2_attn_B': _L2_attn_in['B'], 'L2_attn_C_w': _L2_attn_in['C_w'], 'L2_attn_C_b': _L2_attn_in['C_b'], 'L2_attn_D_w': _L2_attn_in['D_w'], 'L2_attn_D_b': _L2_attn_in['D_b'], 'L2_attn_log_delta': _L2_attn_in['log_delta'], 'L2_cond2_w': _L2_cond2_in['w'], 'L2_cond2_u': _L2_cond2_in['u'], 'L2_ffn_w_gate': _L2_ffn_in['w_gate'], 'L2_ffn_w_up': _L2_ffn_in['w_up'], 'L2_ffn_w_down': _L2_ffn_in['w_down'], 'L2_ffn_ln_weight': _L2_ffn_in['ln_weight'], 'L3_cond_w': _L3_cond_in['w'], 'L3_cond_u': _L3_cond_in['u'], 'L3_attn_Wq': _L3_attn_in['Wq'], 'L3_attn_Wk': _L3_attn_in['Wk'], 'L3_attn_Wv': _L3_attn_in['Wv'], 'L3_attn_Wo': _L3_attn_in['Wo'], 'L3_cond2_w': _L3_cond2_in['w'], 'L3_cond2_u': _L3_cond2_in['u'], 'L3_ffn_Wg': _L3_ffn_in['Wg'], 'L3_ffn_Wu': _L3_ffn_in['Wu'], 'L3_ffn_Wd': _L3_ffn_in['Wd'], 'L3_ffn_Ga': _L3_ffn_in['Ga'], 'L3_ffn_Gb': _L3_ffn_in['Gb'], 'L3_ffn_Ua': _L3_ffn_in['Ua'], 'L3_ffn_Ub': _L3_ffn_in['Ub'], 'L3_ffn_Da': _L3_ffn_in['Da'], 'L3_ffn_Db': _L3_ffn_in['Db'], 'L3_ffn_Wr': _L3_ffn_in['Wr'], 'L3_ffn_temperature': _L3_ffn_in['temperature']}

def reference(x, fside_BxSxS_0, cond_512, L0_cond_w, L0_cond_u, L0_attn_w_qkv, L0_attn_b_qkv, L0_attn_w_out, L0_attn_b_out, L0_cond2_w, L0_cond2_u, L0_ffn_gate_w, L0_ffn_w13, L0_ffn_w2, L0_ffn_sw13, L0_ffn_sw2, L1_cond_w, L1_cond_u, L1_attn_key, L1_attn_value, L1_attn_Wqkv, L1_attn_Wproj, L1_attn_bproj, L1_cond2_w, L1_cond2_u, L1_ffn_router_w, L1_ffn_gate_w, L1_ffn_up_w, L1_ffn_down_w, L2_cond_w, L2_cond_u, L2_attn_A, L2_attn_B, L2_attn_C_w, L2_attn_C_b, L2_attn_D_w, L2_attn_D_b, L2_attn_log_delta, L2_cond2_w, L2_cond2_u, L2_ffn_w_gate, L2_ffn_w_up, L2_ffn_w_down, L2_ffn_ln_weight, L3_cond_w, L3_cond_u, L3_attn_Wq, L3_attn_Wk, L3_attn_Wv, L3_attn_Wo, L3_cond2_w, L3_cond2_u, L3_ffn_Wg, L3_ffn_Wu, L3_ffn_Wd, L3_ffn_Ga, L3_ffn_Gb, L3_ffn_Ua, L3_ffn_Ub, L3_ffn_Da, L3_ffn_Db, L3_ffn_Wr, L3_ffn_temperature):
    import jax
    import jax.numpy as jnp

    def _L0_cond_ref(r, k, v, w, u, time_emb):
        import jax, jax.numpy as jnp
        from jax import lax
        import numpy as np
        B, T, C, TD = (8, 256, 256, 64)

        def _bi_wkv(r, k, v, w, u, time_emb):
            tf = jax.nn.sigmoid(jnp.sum(time_emb, axis=-1))[:, None, None]
            decay = jnp.exp(-jnp.exp(w.astype(jnp.float32)))[None, :] * (0.5 + 0.5 * tf[:, :, 0])
            kf = k.astype(jnp.float32)
            vf = v.astype(jnp.float32)
            ek = jnp.exp(jnp.minimum(kf, 30.0))
            ekv = ek * vf

            def step(carry, x):
                a, b = carry
                ekv_t, ek_t = x
                a = a * decay + ekv_t
                b = b * decay + ek_t
                return ((a, b), (a, b))
            ekv_t = jnp.swapaxes(ekv, 0, 1)
            ek_t = jnp.swapaxes(ek, 0, 1)
            init = (jnp.zeros_like(decay), jnp.zeros_like(decay))
            _, (nf, df) = lax.scan(step, init, (ekv_t, ek_t))
            _, (nb, db) = lax.scan(step, init, (ekv_t, ek_t), reverse=True)
            nf = jnp.swapaxes(nf, 0, 1)
            df = jnp.swapaxes(df, 0, 1)
            nb = jnp.swapaxes(nb, 0, 1)
            db = jnp.swapaxes(db, 0, 1)
            euk = jnp.exp(jnp.minimum(u.astype(jnp.float32)[None, None, :] + kf, 30.0))
            num = nf + nb - ekv + euk * vf
            den = df + db - ek + euk
            base = jax.nn.sigmoid(r.astype(jnp.float32)) * (num / jnp.maximum(den, 1e-08))
            out = base * (0.8 + 0.2 * tf)
            return out.astype(r.dtype)
        return _bi_wkv(r, k, v, w, u, time_emb)

    def _L0_attn_ref(hidden_states, w_qkv, b_qkv, w_out, b_out):
        import jax, jax.numpy as jnp
        import numpy as np
        NUM_HEADS = 16
        HIDDEN = 256
        HEAD_DIM = HIDDEN // NUM_HEADS
        ROTARY_DIM = HEAD_DIM // 4
        ROPE_BASE = 10000.0

        def _rope_angles(seq_len, dtype=jnp.float32):
            inv_freq = 1.0 / ROPE_BASE ** (jnp.arange(0, ROTARY_DIM, 2, dtype=dtype) / ROTARY_DIM)
            t = jnp.arange(seq_len, dtype=dtype)
            freqs = jnp.einsum('s,d->sd', t, inv_freq)
            emb = jnp.concatenate([freqs, freqs], axis=-1)
            return (jnp.cos(emb), jnp.sin(emb))

        def _rotate_half(x):
            x1, x2 = jnp.split(x, 2, axis=-1)
            return jnp.concatenate([-x2, x1], axis=-1)
        B, S, H = hidden_states.shape
        qkv = jnp.einsum('bsh,hf->bsf', hidden_states, w_qkv) + b_qkv
        qkv = qkv.reshape(B, S, NUM_HEADS, 3 * HEAD_DIM)
        q = jnp.transpose(qkv[..., :HEAD_DIM], (0, 2, 1, 3))
        k = jnp.transpose(qkv[..., HEAD_DIM:2 * HEAD_DIM], (0, 2, 1, 3))
        v = jnp.transpose(qkv[..., 2 * HEAD_DIM:], (0, 2, 1, 3))
        cos, sin = _rope_angles(S, q.dtype)
        q_rot, q_pass = (q[..., :ROTARY_DIM], q[..., ROTARY_DIM:])
        k_rot, k_pass = (k[..., :ROTARY_DIM], k[..., ROTARY_DIM:])
        q_rot = q_rot * cos + _rotate_half(q_rot) * sin
        k_rot = k_rot * cos + _rotate_half(k_rot) * sin
        q = jnp.concatenate([q_rot, q_pass], axis=-1)
        k = jnp.concatenate([k_rot, k_pass], axis=-1)
        scores = jnp.einsum('bhqd,bhkd->bhqk', q, k)
        causal = jnp.tril(jnp.ones((S, S), dtype=bool))
        scores = jnp.where(causal, scores, jnp.float32(-jnp.inf).astype(scores.dtype))
        probs = jax.nn.softmax(scores, axis=-1)
        attn = jnp.einsum('bhqk,bhkd->bhqd', probs, v)
        attn = jnp.transpose(attn, (0, 2, 1, 3)).reshape(B, S, H)
        return jnp.einsum('bsh,hf->bsf', attn, w_out) + b_out

    def _L0_cond2_ref(r, k, v, w, u, time_emb):
        import jax, jax.numpy as jnp
        from jax import lax
        import numpy as np
        B, T, C, TD = (8, 256, 256, 64)

        def _bi_wkv(r, k, v, w, u, time_emb):
            tf = jax.nn.sigmoid(jnp.sum(time_emb, axis=-1))[:, None, None]
            decay = jnp.exp(-jnp.exp(w.astype(jnp.float32)))[None, :] * (0.5 + 0.5 * tf[:, :, 0])
            kf = k.astype(jnp.float32)
            vf = v.astype(jnp.float32)
            ek = jnp.exp(jnp.minimum(kf, 30.0))
            ekv = ek * vf

            def step(carry, x):
                a, b = carry
                ekv_t, ek_t = x
                a = a * decay + ekv_t
                b = b * decay + ek_t
                return ((a, b), (a, b))
            ekv_t = jnp.swapaxes(ekv, 0, 1)
            ek_t = jnp.swapaxes(ek, 0, 1)
            init = (jnp.zeros_like(decay), jnp.zeros_like(decay))
            _, (nf, df) = lax.scan(step, init, (ekv_t, ek_t))
            _, (nb, db) = lax.scan(step, init, (ekv_t, ek_t), reverse=True)
            nf = jnp.swapaxes(nf, 0, 1)
            df = jnp.swapaxes(df, 0, 1)
            nb = jnp.swapaxes(nb, 0, 1)
            db = jnp.swapaxes(db, 0, 1)
            euk = jnp.exp(jnp.minimum(u.astype(jnp.float32)[None, None, :] + kf, 30.0))
            num = nf + nb - ekv + euk * vf
            den = df + db - ek + euk
            base = jax.nn.sigmoid(r.astype(jnp.float32)) * (num / jnp.maximum(den, 1e-08))
            out = base * (0.8 + 0.2 * tf)
            return out.astype(r.dtype)
        return _bi_wkv(r, k, v, w, u, time_emb)

    def _L0_ffn_ref(hidden_states, gate_w, w13, w2, sw13, sw2):
        import jax, jax.numpy as jnp
        import numpy as np
        from jax import lax
        H = 256
        I = 176
        E = 16
        TOP_K = 6
        IS = 2 * I

        def _swiglu(x, w13_, w2_):
            gu = x @ w13_.T
            g, u = jnp.split(gu, 2, axis=-1)
            return jax.nn.silu(g) * u @ w2_.T
        B, S, Hd = hidden_states.shape
        x = hidden_states.reshape(-1, Hd)
        T = x.shape[0]
        scores = jax.nn.softmax(x @ gate_w.T, axis=-1)
        topk_w, topk_ids = lax.top_k(scores, TOP_K)
        topk_w = topk_w / (topk_w.sum(-1, keepdims=True) + 1e-20)
        combine = jnp.einsum('tk,tke->te', topk_w, jax.nn.one_hot(topk_ids, E, dtype=topk_w.dtype))

        def body(acc, ew):
            w13_e, w2_e, c_e = ew
            y = _swiglu(x, w13_e, w2_e)
            return (acc + c_e[:, None] * y, None)
        out, _ = lax.scan(body, jnp.zeros_like(x), (w13, w2, combine.T))
        out = out + _swiglu(x, sw13, sw2)
        return out.reshape(B, S, Hd)

    def _L1_cond_ref(r, k, v, w, u, time_emb):
        import jax, jax.numpy as jnp
        from jax import lax
        import numpy as np
        B, T, C, TD = (8, 256, 256, 64)

        def _bi_wkv(r, k, v, w, u, time_emb):
            tf = jax.nn.sigmoid(jnp.sum(time_emb, axis=-1))[:, None, None]
            decay = jnp.exp(-jnp.exp(w.astype(jnp.float32)))[None, :] * (0.5 + 0.5 * tf[:, :, 0])
            kf = k.astype(jnp.float32)
            vf = v.astype(jnp.float32)
            ek = jnp.exp(jnp.minimum(kf, 30.0))
            ekv = ek * vf

            def step(carry, x):
                a, b = carry
                ekv_t, ek_t = x
                a = a * decay + ekv_t
                b = b * decay + ek_t
                return ((a, b), (a, b))
            ekv_t = jnp.swapaxes(ekv, 0, 1)
            ek_t = jnp.swapaxes(ek, 0, 1)
            init = (jnp.zeros_like(decay), jnp.zeros_like(decay))
            _, (nf, df) = lax.scan(step, init, (ekv_t, ek_t))
            _, (nb, db) = lax.scan(step, init, (ekv_t, ek_t), reverse=True)
            nf = jnp.swapaxes(nf, 0, 1)
            df = jnp.swapaxes(df, 0, 1)
            nb = jnp.swapaxes(nb, 0, 1)
            db = jnp.swapaxes(db, 0, 1)
            euk = jnp.exp(jnp.minimum(u.astype(jnp.float32)[None, None, :] + kf, 30.0))
            num = nf + nb - ekv + euk * vf
            den = df + db - ek + euk
            base = jax.nn.sigmoid(r.astype(jnp.float32)) * (num / jnp.maximum(den, 1e-08))
            out = base * (0.8 + 0.2 * tf)
            return out.astype(r.dtype)
        return _bi_wkv(r, k, v, w, u, time_emb)

    def _L1_attn_ref(query, key, value, Wqkv, Wproj, bproj):
        import jax, jax.numpy as jnp
        import numpy as np
        B, SQ, H = (2, 256, 256)
        NH = 16
        HN = H // NH
        b, sq, h = query.shape
        nh, hn = (NH, HN)
        norm = 1.0 / jnp.sqrt(jnp.asarray(hn, query.dtype))
        x = jnp.transpose(query, (1, 0, 2)).reshape(sq * b, h)
        mixed = x @ Wqkv.T
        mixed = mixed.reshape(sq, b, nh, 3, hn)
        q = mixed[..., 0, :]
        k = mixed[..., 1, :]
        v = mixed[..., 2, :]
        q = q.reshape(sq, b * nh, hn).transpose(1, 0, 2)
        k = k.reshape(sq, b * nh, hn).transpose(1, 0, 2)
        v = v.reshape(sq, b * nh, hn).transpose(1, 0, 2)
        attn = jnp.einsum('gqd,gkd->gqk', q, k) * norm
        attn = jax.nn.softmax(attn, axis=-1)
        ctx = jnp.einsum('gqk,gkd->gqd', attn, v)
        ctx = ctx.reshape(nh, b, sq, hn)
        ctx = jnp.transpose(ctx, (2, 1, 0, 3)).reshape(sq * b, h)
        out = ctx @ Wproj.T + bproj
        out = out.reshape(sq, b, h)
        return jnp.transpose(out, (1, 0, 2))

    def _L1_cond2_ref(r, k, v, w, u, time_emb):
        import jax, jax.numpy as jnp
        from jax import lax
        import numpy as np
        B, T, C, TD = (8, 256, 256, 64)

        def _bi_wkv(r, k, v, w, u, time_emb):
            tf = jax.nn.sigmoid(jnp.sum(time_emb, axis=-1))[:, None, None]
            decay = jnp.exp(-jnp.exp(w.astype(jnp.float32)))[None, :] * (0.5 + 0.5 * tf[:, :, 0])
            kf = k.astype(jnp.float32)
            vf = v.astype(jnp.float32)
            ek = jnp.exp(jnp.minimum(kf, 30.0))
            ekv = ek * vf

            def step(carry, x):
                a, b = carry
                ekv_t, ek_t = x
                a = a * decay + ekv_t
                b = b * decay + ek_t
                return ((a, b), (a, b))
            ekv_t = jnp.swapaxes(ekv, 0, 1)
            ek_t = jnp.swapaxes(ek, 0, 1)
            init = (jnp.zeros_like(decay), jnp.zeros_like(decay))
            _, (nf, df) = lax.scan(step, init, (ekv_t, ek_t))
            _, (nb, db) = lax.scan(step, init, (ekv_t, ek_t), reverse=True)
            nf = jnp.swapaxes(nf, 0, 1)
            df = jnp.swapaxes(df, 0, 1)
            nb = jnp.swapaxes(nb, 0, 1)
            db = jnp.swapaxes(db, 0, 1)
            euk = jnp.exp(jnp.minimum(u.astype(jnp.float32)[None, None, :] + kf, 30.0))
            num = nf + nb - ekv + euk * vf
            den = df + db - ek + euk
            base = jax.nn.sigmoid(r.astype(jnp.float32)) * (num / jnp.maximum(den, 1e-08))
            out = base * (0.8 + 0.2 * tf)
            return out.astype(r.dtype)
        return _bi_wkv(r, k, v, w, u, time_emb)

    def _L1_ffn_ref(hidden_states, router_w, gate_w, up_w, down_w):
        import jax, jax.numpy as jnp
        import numpy as np
        B, S, H, I, E = (2, 256, 256, 176, 8)
        TOP_K = 2
        b, s, h = hidden_states.shape
        e = router_w.shape[0]
        x = hidden_states.reshape(-1, h)
        logits = jnp.einsum('th,eh->te', x, router_w)
        top_vals, top_idx = jax.lax.top_k(logits, TOP_K)
        top_w = jax.nn.softmax(top_vals, axis=-1)
        expert = top_idx[:, 0]
        weight = top_w[:, 0]
        gate = jnp.einsum('th,eih->eti', x, gate_w)
        up = jnp.einsum('th,eih->eti', x, up_w)
        act = jax.nn.silu(gate) * up
        out_e = jnp.einsum('eti,ehi->eth', act, down_w)
        combine = jax.nn.one_hot(expert, e, dtype=x.dtype) * weight[:, None]
        out = jnp.einsum('eth,te->th', out_e, combine)
        return out.reshape(b, s, h)

    def _L2_cond_ref(r, k, v, w, u, time_emb):
        import jax, jax.numpy as jnp
        from jax import lax
        import numpy as np
        B, T, C, TD = (8, 256, 256, 64)

        def _bi_wkv(r, k, v, w, u, time_emb):
            tf = jax.nn.sigmoid(jnp.sum(time_emb, axis=-1))[:, None, None]
            decay = jnp.exp(-jnp.exp(w.astype(jnp.float32)))[None, :] * (0.5 + 0.5 * tf[:, :, 0])
            kf = k.astype(jnp.float32)
            vf = v.astype(jnp.float32)
            ek = jnp.exp(jnp.minimum(kf, 30.0))
            ekv = ek * vf

            def step(carry, x):
                a, b = carry
                ekv_t, ek_t = x
                a = a * decay + ekv_t
                b = b * decay + ek_t
                return ((a, b), (a, b))
            ekv_t = jnp.swapaxes(ekv, 0, 1)
            ek_t = jnp.swapaxes(ek, 0, 1)
            init = (jnp.zeros_like(decay), jnp.zeros_like(decay))
            _, (nf, df) = lax.scan(step, init, (ekv_t, ek_t))
            _, (nb, db) = lax.scan(step, init, (ekv_t, ek_t), reverse=True)
            nf = jnp.swapaxes(nf, 0, 1)
            df = jnp.swapaxes(df, 0, 1)
            nb = jnp.swapaxes(nb, 0, 1)
            db = jnp.swapaxes(db, 0, 1)
            euk = jnp.exp(jnp.minimum(u.astype(jnp.float32)[None, None, :] + kf, 30.0))
            num = nf + nb - ekv + euk * vf
            den = df + db - ek + euk
            base = jax.nn.sigmoid(r.astype(jnp.float32)) * (num / jnp.maximum(den, 1e-08))
            out = base * (0.8 + 0.2 * tf)
            return out.astype(r.dtype)
        return _bi_wkv(r, k, v, w, u, time_emb)

    def _L2_attn_ref(x, A, B, C_w, C_b, D_w, D_b, log_delta):
        import jax, jax.numpy as jnp
        import numpy as np
        B_SZ, T, D, N = (4, 256, 256, 64)

        def _reference_tuple_inner(x, A, B, C_w, C_b, D_w, D_b, log_delta):
            A_diag = jnp.exp(-jax.nn.softplus(log_delta))
            x_proj = (x @ C_w.T + C_b) * jax.nn.sigmoid(x @ D_w.T + D_b)
            xp_t = jnp.transpose(x_proj, (1, 0, 2))

            def step(g, xt):
                g = g * A_diag + xt
                return (g, g)
            g_last, gs = jax.lax.scan(step, jnp.zeros((x.shape[0], x.shape[2]), x.dtype), xp_t)
            gs = jnp.transpose(gs, (1, 0, 2))
            AB = jnp.sum(A * B, axis=-1)
            output = gs * AB
            h = g_last[:, :, None] * B[None, :, :]
            return (output, h)
        return _reference_tuple_inner(x, A, B, C_w, C_b, D_w, D_b, log_delta)[0]

    def _L2_cond2_ref(r, k, v, w, u, time_emb):
        import jax, jax.numpy as jnp
        from jax import lax
        import numpy as np
        B, T, C, TD = (8, 256, 256, 64)

        def _bi_wkv(r, k, v, w, u, time_emb):
            tf = jax.nn.sigmoid(jnp.sum(time_emb, axis=-1))[:, None, None]
            decay = jnp.exp(-jnp.exp(w.astype(jnp.float32)))[None, :] * (0.5 + 0.5 * tf[:, :, 0])
            kf = k.astype(jnp.float32)
            vf = v.astype(jnp.float32)
            ek = jnp.exp(jnp.minimum(kf, 30.0))
            ekv = ek * vf

            def step(carry, x):
                a, b = carry
                ekv_t, ek_t = x
                a = a * decay + ekv_t
                b = b * decay + ek_t
                return ((a, b), (a, b))
            ekv_t = jnp.swapaxes(ekv, 0, 1)
            ek_t = jnp.swapaxes(ek, 0, 1)
            init = (jnp.zeros_like(decay), jnp.zeros_like(decay))
            _, (nf, df) = lax.scan(step, init, (ekv_t, ek_t))
            _, (nb, db) = lax.scan(step, init, (ekv_t, ek_t), reverse=True)
            nf = jnp.swapaxes(nf, 0, 1)
            df = jnp.swapaxes(df, 0, 1)
            nb = jnp.swapaxes(nb, 0, 1)
            db = jnp.swapaxes(db, 0, 1)
            euk = jnp.exp(jnp.minimum(u.astype(jnp.float32)[None, None, :] + kf, 30.0))
            num = nf + nb - ekv + euk * vf
            den = df + db - ek + euk
            base = jax.nn.sigmoid(r.astype(jnp.float32)) * (num / jnp.maximum(den, 1e-08))
            out = base * (0.8 + 0.2 * tf)
            return out.astype(r.dtype)
        return _bi_wkv(r, k, v, w, u, time_emb)

    def _L2_ffn_ref(x, w_gate, w_up, w_down, ln_weight):
        import jax, jax.numpy as jnp
        import numpy as np
        EPS = 1e-05
        RMS_EPS = 1e-06

        def activation_quant(x, num_bits=8):
            qn = -2 ** (num_bits - 1)
            qp = 2 ** (num_bits - 1) - 1
            xf = x.astype(jnp.float32)
            s = qp / jnp.clip(jnp.max(jnp.abs(xf), axis=-1, keepdims=True), EPS, None)
            return (jnp.clip(jnp.round(xf * s), qn, qp) / s).astype(x.dtype)

        def weight_quant(w):
            wf = w.astype(jnp.float32)
            s = 1.0 / jnp.clip(jnp.mean(jnp.abs(wf)), EPS, None)
            return (jnp.clip(jnp.round(wf * s), -1.0, 1.0) / s).astype(w.dtype)

        def bit_linear(x, w):
            qx = x + jax.lax.stop_gradient(activation_quant(x) - x)
            qw = w + jax.lax.stop_gradient(weight_quant(w) - w)
            return jnp.einsum('bsh,oh->bso', qx, qw)

        def rms_norm(x, weight, eps=RMS_EPS):
            xf = x.astype(jnp.float32)
            var = jnp.mean(xf * xf, axis=-1, keepdims=True)
            return weight * (xf * jax.lax.rsqrt(var + eps)).astype(x.dtype)
        h = jax.nn.silu(bit_linear(x, w_gate)) * bit_linear(x, w_up)
        h = rms_norm(h, ln_weight)
        return bit_linear(h, w_down)

    def _L3_cond_ref(r, k, v, w, u, time_emb):
        import jax, jax.numpy as jnp
        from jax import lax
        import numpy as np
        B, T, C, TD = (8, 256, 256, 64)

        def _bi_wkv(r, k, v, w, u, time_emb):
            tf = jax.nn.sigmoid(jnp.sum(time_emb, axis=-1))[:, None, None]
            decay = jnp.exp(-jnp.exp(w.astype(jnp.float32)))[None, :] * (0.5 + 0.5 * tf[:, :, 0])
            kf = k.astype(jnp.float32)
            vf = v.astype(jnp.float32)
            ek = jnp.exp(jnp.minimum(kf, 30.0))
            ekv = ek * vf

            def step(carry, x):
                a, b = carry
                ekv_t, ek_t = x
                a = a * decay + ekv_t
                b = b * decay + ek_t
                return ((a, b), (a, b))
            ekv_t = jnp.swapaxes(ekv, 0, 1)
            ek_t = jnp.swapaxes(ek, 0, 1)
            init = (jnp.zeros_like(decay), jnp.zeros_like(decay))
            _, (nf, df) = lax.scan(step, init, (ekv_t, ek_t))
            _, (nb, db) = lax.scan(step, init, (ekv_t, ek_t), reverse=True)
            nf = jnp.swapaxes(nf, 0, 1)
            df = jnp.swapaxes(df, 0, 1)
            nb = jnp.swapaxes(nb, 0, 1)
            db = jnp.swapaxes(db, 0, 1)
            euk = jnp.exp(jnp.minimum(u.astype(jnp.float32)[None, None, :] + kf, 30.0))
            num = nf + nb - ekv + euk * vf
            den = df + db - ek + euk
            base = jax.nn.sigmoid(r.astype(jnp.float32)) * (num / jnp.maximum(den, 1e-08))
            out = base * (0.8 + 0.2 * tf)
            return out.astype(r.dtype)
        return _bi_wkv(r, k, v, w, u, time_emb)

    def _L3_attn_ref(X, Wq, Wk, Wv, Wo):
        import jax, jax.numpy as jnp
        import numpy as np
        B, T, C = (2, 256, 256)
        NH, NKV, HD = (16, 8, 32)
        SOFTCAP = 50.0
        ROPE_BASE = 10000.0

        def _rotate_half(x):
            x1, x2 = (x[..., :x.shape[-1] // 2], x[..., x.shape[-1] // 2:])
            return jnp.concatenate((-x2, x1), axis=-1)

        def _rope_cos_sin(t, head_dim, dtype):
            inv_freq = 1.0 / ROPE_BASE ** (jnp.arange(0, head_dim, 2, dtype=jnp.int32).astype(jnp.float32) / head_dim)
            pos = jnp.arange(t, dtype=jnp.float32)
            freqs = pos[:, None] * inv_freq[None, :]
            emb = jnp.concatenate((freqs, freqs), axis=-1)
            return (jnp.cos(emb).astype(dtype)[None, None], jnp.sin(emb).astype(dtype)[None, None])
        b, t, c = X.shape
        n_rep = NH // NKV
        q = (X @ Wq).reshape(b, t, NH, HD).transpose(0, 2, 1, 3)
        k = (X @ Wk).reshape(b, t, NKV, HD).transpose(0, 2, 1, 3)
        v = (X @ Wv).reshape(b, t, NKV, HD).transpose(0, 2, 1, 3)
        cos, sin = _rope_cos_sin(t, HD, X.dtype)
        q = q * cos + _rotate_half(q) * sin
        k = k * cos + _rotate_half(k) * sin
        k = jnp.repeat(k, n_rep, axis=1)
        v = jnp.repeat(v, n_rep, axis=1)
        scale = 256.0 ** (-0.5)
        att = jnp.einsum('bhqd,bhkd->bhqk', q, k) * scale
        att = SOFTCAP * jnp.tanh(att / SOFTCAP)
        causal = jnp.tril(jnp.ones((t, t), dtype=bool))
        att = jnp.where(causal[None, None], att, -jnp.inf)
        att = jax.nn.softmax(att, axis=-1)
        y = jnp.einsum('bhqk,bhkd->bhqd', att, v)
        y = y.transpose(0, 2, 1, 3).reshape(b, t, NH * HD)
        return y @ Wo

    def _L3_cond2_ref(r, k, v, w, u, time_emb):
        import jax, jax.numpy as jnp
        from jax import lax
        import numpy as np
        B, T, C, TD = (8, 256, 256, 64)

        def _bi_wkv(r, k, v, w, u, time_emb):
            tf = jax.nn.sigmoid(jnp.sum(time_emb, axis=-1))[:, None, None]
            decay = jnp.exp(-jnp.exp(w.astype(jnp.float32)))[None, :] * (0.5 + 0.5 * tf[:, :, 0])
            kf = k.astype(jnp.float32)
            vf = v.astype(jnp.float32)
            ek = jnp.exp(jnp.minimum(kf, 30.0))
            ekv = ek * vf

            def step(carry, x):
                a, b = carry
                ekv_t, ek_t = x
                a = a * decay + ekv_t
                b = b * decay + ek_t
                return ((a, b), (a, b))
            ekv_t = jnp.swapaxes(ekv, 0, 1)
            ek_t = jnp.swapaxes(ek, 0, 1)
            init = (jnp.zeros_like(decay), jnp.zeros_like(decay))
            _, (nf, df) = lax.scan(step, init, (ekv_t, ek_t))
            _, (nb, db) = lax.scan(step, init, (ekv_t, ek_t), reverse=True)
            nf = jnp.swapaxes(nf, 0, 1)
            df = jnp.swapaxes(df, 0, 1)
            nb = jnp.swapaxes(nb, 0, 1)
            db = jnp.swapaxes(db, 0, 1)
            euk = jnp.exp(jnp.minimum(u.astype(jnp.float32)[None, None, :] + kf, 30.0))
            num = nf + nb - ekv + euk * vf
            den = df + db - ek + euk
            base = jax.nn.sigmoid(r.astype(jnp.float32)) * (num / jnp.maximum(den, 1e-08))
            out = base * (0.8 + 0.2 * tf)
            return out.astype(r.dtype)
        return _bi_wkv(r, k, v, w, u, time_emb)

    def _L3_ffn_ref(x, Wg, Wu, Wd, Ga, Gb, Ua, Ub, Da, Db, Wr, temperature):
        import jax, jax.numpy as jnp
        import numpy as np
        import math
        GOLDEN_CENTER = 1.0 / math.e
        GOLDEN_LOWER = 0.5 - math.log(4.0 / 3.0)
        GOLDEN_UPPER = 0.5
        B, T, D = (4, 128, 256)
        E = 8
        F = 1024 // (E // 2)
        R = 64
        NL = 2

        def _router_weights(x, Wr, temperature):
            logits = jnp.einsum('btd,de->bte', x, Wr)
            inhibition = jax.nn.sigmoid(logits / temperature)
            in_zone = (inhibition >= GOLDEN_LOWER) & (inhibition <= GOLDEN_UPPER)
            distance = jnp.abs(inhibition - GOLDEN_CENTER)
            w = jnp.exp(-distance / 0.1) * in_zone.astype(x.dtype)
            wsum = w.sum(axis=-1, keepdims=True)
            no_expert = wsum < 1e-08
            fb = jnp.exp(-distance / 0.3)
            _, top2 = jax.lax.top_k(fb, 2)
            fb_mask = jax.nn.one_hot(top2, E, dtype=x.dtype).sum(axis=-2)
            fb_w = fb * fb_mask
            fb_w = fb_w / jnp.clip(fb_w.sum(axis=-1, keepdims=True), 1e-08)
            w = jnp.where(no_expert, fb_w, w)
            return w / jnp.clip(w.sum(axis=-1, keepdims=True), 1e-08)
        weights = _router_weights(x, Wr, temperature)
        gate = jnp.einsum('btd,edf->ebtf', x, Wg)
        up = jnp.einsum('btd,edf->ebtf', x, Wu)
        gate = gate.at[:NL].add(jnp.einsum('btd,edr,erf->ebtf', x, Ga, Gb))
        up = up.at[:NL].add(jnp.einsum('btd,edr,erf->ebtf', x, Ua, Ub))
        mid = jax.nn.silu(gate) * up
        out = jnp.einsum('ebtf,efd->ebtd', mid, Wd)
        out = out.at[:NL].add(jnp.einsum('ebtf,efr,erd->ebtd', mid[:NL], Da, Db))
        return jnp.einsum('bte,ebtd->btd', weights, out)
    x = x + _L0_attn_ref(_L0_cond_ref(x, fside_BxSxS_0, fside_BxSxS_0, L0_cond_w, L0_cond_u, cond_512), L0_attn_w_qkv, L0_attn_b_qkv, L0_attn_w_out, L0_attn_b_out)
    x = x + _L0_ffn_ref(_L0_cond2_ref(x, fside_BxSxS_0, fside_BxSxS_0, L0_cond2_w, L0_cond2_u, cond_512), L0_ffn_gate_w, L0_ffn_w13, L0_ffn_w2, L0_ffn_sw13, L0_ffn_sw2)
    x = x + _L1_attn_ref(_L1_cond_ref(x, fside_BxSxS_0, fside_BxSxS_0, L1_cond_w, L1_cond_u, cond_512), L1_attn_key, L1_attn_value, L1_attn_Wqkv, L1_attn_Wproj, L1_attn_bproj)
    x = x + _L1_ffn_ref(_L1_cond2_ref(x, fside_BxSxS_0, fside_BxSxS_0, L1_cond2_w, L1_cond2_u, cond_512), L1_ffn_router_w, L1_ffn_gate_w, L1_ffn_up_w, L1_ffn_down_w)
    x = x + _L2_attn_ref(_L2_cond_ref(x, fside_BxSxS_0, fside_BxSxS_0, L2_cond_w, L2_cond_u, cond_512), L2_attn_A, L2_attn_B, L2_attn_C_w, L2_attn_C_b, L2_attn_D_w, L2_attn_D_b, L2_attn_log_delta)
    x = x + _L2_ffn_ref(_L2_cond2_ref(x, fside_BxSxS_0, fside_BxSxS_0, L2_cond2_w, L2_cond2_u, cond_512), L2_ffn_w_gate, L2_ffn_w_up, L2_ffn_w_down, L2_ffn_ln_weight)
    x = x + _L3_attn_ref(_L3_cond_ref(x, fside_BxSxS_0, fside_BxSxS_0, L3_cond_w, L3_cond_u, cond_512), L3_attn_Wq, L3_attn_Wk, L3_attn_Wv, L3_attn_Wo)
    x = x + _L3_ffn_ref(_L3_cond2_ref(x, fside_BxSxS_0, fside_BxSxS_0, L3_cond2_w, L3_cond2_u, cond_512), L3_ffn_Wg, L3_ffn_Wu, L3_ffn_Wd, L3_ffn_Ga, L3_ffn_Gb, L3_ffn_Ua, L3_ffn_Ub, L3_ffn_Da, L3_ffn_Db, L3_ffn_Wr, L3_ffn_temperature)
    return x

_drawn_inputs = setup_inputs


def setup_inputs(seed=0):
    import zlib

    import numpy as np

    out = dict(_drawn_inputs(seed))
    spreads = {'L0_attn_b_qkv': (0.0, 0.1),
     'L0_attn_b_out': (0.0, 0.1),
     'L1_attn_bproj': (0.0, 0.1),
     'L2_attn_log_delta': (0.0, 0.1),
     'L2_ffn_ln_weight': (1.0, 0.2)}
    factors = {'L0_cond_u': 2.923,
     'L0_cond2_w': 8.0,
     'L0_cond2_u': 8.0,
     'L0_ffn_gate_w': 8.0,
     'L0_ffn_w13': 8.0,
     'L0_ffn_w2': 8.0,
     'L0_ffn_sw13': 8.0,
     'L0_ffn_sw2': 8.0,
     'L1_cond_u': 3.205,
     'L1_cond2_u': 4.009,
     'L2_attn_D_b': 3.144,
     'L3_cond_w': 6.876,
     'L3_cond_u': 8.0,
     'L3_attn_Wq': 8.0,
     'L3_attn_Wk': 8.0,
     'L3_attn_Wv': 3.032,
     'L3_attn_Wo': 2.761,
     'L3_cond2_w': 8.0,
     'L3_cond2_u': 8.0,
     'L3_ffn_Wg': 8.0,
     'L3_ffn_Wu': 8.0,
     'L3_ffn_Wd': 8.0,
     'L3_ffn_Ga': 8.0,
     'L3_ffn_Gb': 8.0,
     'L3_ffn_Ua': 8.0,
     'L3_ffn_Ub': 8.0,
     'L3_ffn_Da': 8.0,
     'L3_ffn_Db': 8.0,
     'L3_ffn_Wr': 8.0}
    for name, (base, spread) in spreads.items():
        noise = np.random.default_rng([zlib.crc32(name.encode()), seed]).standard_normal(out[name].shape)
        drawn = base * np.exp(spread * noise) if base else spread * noise
        out[name] = jnp.asarray(drawn.astype(out[name].dtype))
    for name, factor in factors.items():
        out[name] = (out[name] * factor).astype(out[name].dtype)
    return out
```

```python
from contextlib import ExitStack

import numpy as np

import concourse.bass as bass
from concourse import mybir

F32 = mybir.dt.float32
F32R = mybir.dt.float32r
BF16 = mybir.dt.bfloat16
ALU = mybir.AluOpType
ACT = mybir.ActivationFunctionType
AX = mybir.AxisListType

P = 128
B, T, C = 4, 256, 256
N = B * T
KC = C // P
HALF = N // 2
HEADS, SLOT = 16, 32
GROUPS = HEADS * SLOT // P
CONDS = 8
EXPERT_ROWS = 16
GRANULES = P // EXPERT_ROWS
E30 = float(np.exp(np.float32(30.0)))
MAGIC = float(1.5 * 2 ** 23)
NEG = -1.0e30
CAP = 50.0
L2I = 1024
TILES = N // P

ATTN_COLS = 2 * GROUPS * P + C
G_SLOT = (0, 3, 0, 1, 2, 3, 0, 1)
DSZ = bass.ds


def build(nc, io, out):
    ctx = ExitStack()
    with ctx:
        def sb(name, shape, dt=F32):
            return ctx.enter_context(nc.sbuf_tensor(name, shape, dt))

        def sem(name):
            return ctx.enter_context(nc.semaphore(name))

        bank = [ctx.enter_context(nc.psum_tensor(f"bank{i}", [P, 512], F32)) for i in range(8)]

        x = sb("x", [P, KC, N])
        h = sb("h", [P, KC, N])
        h_hi = sb("h_hi", [P, KC, N], F32R)
        h_lo = sb("h_lo", [P, KC, N], F32R)
        G = sb("G", [P, 4, KC, N])
        side = sb("side", [P, KC, N])
        ek = sb("ek", [P, KC, N])
        wkv_in = sb("wkv_in", [P, 2, KC, T])
        wu = sb("wu", [P, 2, KC, CONDS])
        cond_bc = sb("cond_bc", [P, B, 64])
        tf4 = sb("tf4", [P, 4, B])
        ew = sb("ew", [P, 2, KC * CONDS])
        decay = sb("decay", [P, KC, CONDS * B])
        gscale = sb("gscale", [P, B])
        scan_f = sb("scan_f", [P, 2, KC, T])
        scan_b = sb("scan_b", [P, 2, KC, T])
        euk = sb("euk", [P, KC, T])
        wkv_num = sb("wkv_num", [P, KC, T])
        wkv_rec = sb("wkv_rec", [P, KC, T])
        ident = sb("ident", [P, P])
        ident_bf = sb("ident_bf", [P, P], BF16)
        negmask = sb("negmask", [P, P], BF16)
        capmask = sb("capmask", [P, P])
        zeros_bf = sb("zeros_bf", [P, 512], BF16)
        ones = sb("ones", [P, P])
        earlier = sb("earlier", [P, 16, 16])
        rope = sb("rope", [P, 4, T])
        w_attn = sb("w_attn", [P, KC, ATTN_COLS])
        w_out = sb("w_out", [P, 4, C])
        bias_attn = sb("bias_attn", [P, 8 + KC + KC])
        bias_v = sb("bias_v", [P, C])
        hb = sb("hb", [P, KC, T])
        v_sb = sb("v_sb", [P, 2, C])
        probs = sb("probs", [P, 2, 512])
        probs_t = sb("probs_t", [P, 2, 512])
        row_max = sb("row_max", [P, 2 * HEADS])
        row_sum = sb("row_sum", [P, 2 * HEADS])
        row_inv = sb("row_inv", [P, 2 * HEADS])
        attn_t = sb("attn_t", [P, 4, T])
        w_raw = sb("w_raw", [P, 2, 768])
        w_gu_hi = sb("w_gu_hi", [P, 2, 512], F32R)
        w_gu_lo = sb("w_gu_lo", [P, 2, 512], F32R)
        w_d_hi = sb("w_d_hi", [P, 2, 256], F32R)
        w_d_lo = sb("w_d_lo", [P, 2, 256], F32R)
        c_rows = sb("c_rows", [P, 2, N])
        act_s = sb("act_s", [P, 2, 512])
        act_m = sb("act_m", [P, 2, 512])
        act_a = sb("act_a", [P, 2, 512])
        act_hi = sb("act_hi", [P, 2, 512], F32R)
        act_lo = sb("act_lo", [P, 2, 512], F32R)
        w_route = sb("w_route", [P, 3, KC, 16])
        route = sb("route", [P, 7, TILES * 16])
        route_s = sb("route_s", [P, 6, TILES])
        temp = sb("temp", [P, 2])
        scan_c = sb("scan_c", [P, 4 * KC + 2 * KC])
        ab_in = sb("ab_in", [P, 2, KC, 64])
        wq_g = sb("wq_g", [P, KC, L2I], BF16)
        wq_u = sb("wq_u", [P, KC, L2I], BF16)
        wq_d = sb("wq_d", [P, L2I // P, C], BF16)
        wq_stat = sb("wq_stat", [P, 3, 4])
        bstat = sb("bstat", [P, 13, TILES])
        half_c = sb("half_c", [P, 2])
        qk = c_rows[:, :, :].rearrange("p a (b t) -> p (a b) t", t=T)
        rope_a = act_s[:, 0, :].rearrange("p (g t) -> p g t", g=2)
        rope_b = act_s[:, 1, :].rearrange("p (g t) -> p g t", g=2)
        attn = act_a
        c_t = act_a[0:16, :, :].rearrange("p a b -> p (a b)")
        ln_bc = attn_t[:, :, :].rearrange("p a b -> p (a b)")
        hq_bf = probs[:, :, :].rearrange("p a b -> p (a b)").bitcast(BF16).rearrange("p (t c) -> p t c", c=C)
        hq_t = probs_t[:, :, :].rearrange("p a b -> p (a b)").bitcast(BF16).rearrange("p (k t) -> p k t", k=KC)
        h2_bf = probs[:, 0, :].bitcast(BF16)
        h2_t = probs[:, 1, :].bitcast(BF16).rearrange("p (c t) -> p c t", t=P)
        y_sb = v_sb[:, 0, :]

        c_dram = {l: nc.dram_tensor(f"c_granules_{l}", (g, N), F32).ap() for l, g in (("L0", 200), ("L1", 88), ("L3", 128))}
        lora_dram = nc.dram_tensor("lora_chunks", (4, P, 768), F32).ap()

        side_in = sem("side_in")
        cond_in = sem("cond_in")
        x_in = sem("x_in")
        wkv_put = sem("wkv_put")
        scan_done = sem("scan_done")
        euk_done = sem("euk_done")
        wkv_step = sem("wkv_step")
        wkv_inv = sem("wkv_inv")
        g_done = sem("g_done")
        setup_v = sem("setup_v")
        setup_a = sem("setup_a")
        const_p = sem("const_p")

        def gate_dve(dve, part, n, b):
            s = n * 4 + b
            tok = DSZ(b * T, T)
            if part in (0, 1):
                ch = part
                if part == 0:
                    dve.wait_ge(g_done, s + 1)
                    dve.wait_ge(wkv_put, s + 1)
                d = decay[:, ch, DSZ(s, 1)]
                for i in range(2):
                    dve.tensor_tensor_scan(scan_f[:, i, ch, :], d.to_broadcast([P, T]), wkv_in[:, i, ch, :], 0.0,
                                           ALU.mult, ALU.add)
                    last = dve.tensor_tensor_scan(scan_b[:, i, ch, 0:T - 1][:, ::-1],
                                                  wkv_in[:, i, ch, 1:T][:, ::-1],
                                                  d.to_broadcast([P, T - 1]), 0.0, ALU.add, ALU.mult)
                if part == 1:
                    last.then_inc(scan_done, 1)
            if part == 2:
                dve.wait_ge(scan_done, s + 2)
                dve.tensor_tensor(scan_f[:, :, :, :], scan_f[:, :, :, :], scan_b[:, :, :, :], ALU.add).then_inc(wkv_step, 1)
                dve.wait_ge(euk_done, s + 1)
                dve.scalar_tensor_tensor(out=wkv_num[:, :, :], in0=euk[:, :, :], scalar=E30, in1=side[:, :, tok],
                                         op0=ALU.min, op1=ALU.mult).then_inc(wkv_step, 1)
            if part == 3:
                dve.wait_ge(wkv_step, s * 5 + 2)
                dve.scalar_tensor_tensor(out=scan_f[:, 1, :, :], in0=euk[:, :, :], scalar=E30, in1=scan_f[:, 1, :, :],
                                         op0=ALU.min, op1=ALU.add).then_inc(wkv_step, 1)
                dve.tensor_tensor(wkv_num[:, :, :], wkv_num[:, :, :], scan_f[:, 0, :, :], ALU.add).then_inc(wkv_step, 1)
            if part == 4:
                dve.wait_ge(wkv_step, s * 5 + 3)
                dve.tensor_scalar(scan_f[:, 1, :, :], scan_f[:, 1, :, :], 1e-8, None, ALU.max).then_inc(wkv_step, 1)
                dve.wait_ge(wkv_step, s * 5 + 5)
                dve.reciprocal(wkv_rec[:, :, :], scan_f[:, 1, :, :]).then_inc(wkv_inv, 1)

        def gate_finish(dve, n, b, slot):
            s = n * 4 + b
            dve.wait_ge(wkv_inv, s + 1)
            dve.scalar_tensor_tensor(out=G[:, slot, :, DSZ(b * T, T)], in0=wkv_num[:, :, :], scalar=gscale[:, DSZ(b, 1)],
                                     in1=wkv_rec[:, :, :], op0=ALU.mult, op1=ALU.mult).then_inc(g_done, 1)

        def gate_pool(pool, n, b):
            s = n * 4 + b
            tok = DSZ(b * T, T)
            pool.wait_ge(scan_done, s + 1)
            pool.tensor_tensor(wkv_in[:, 0, :, :], ek[:, :, tok], side[:, :, tok], ALU.mult)
            pool.tensor_tensor(wkv_in[:, 1, :, :], ek[:, :, tok], ones[:, 0:1].unsqueeze(2).to_broadcast([P, KC, T]), ALU.mult).then_inc(wkv_put, 1)

        def gate_act(act, n, b):
            s = n * 4 + b
            act.wait_ge(scan_done, s + 2)
            act.wait_ge(side_in, 16)
            for ch in range(KC):
                last = act.activation(euk[:, ch, :], side[:, ch, DSZ(b * T, T)], ACT.Exp, bias=wu[:, 1, ch, DSZ(n, 1)])
            last.then_inc(euk_done, 1)

        lora_in = sem("lora_in")
        lora_raw = [sem("lora_raw0"), sem("lora_raw1")]
        lora_mm = sem("lora_mm")
        lora_add = sem("lora_add")
        lora_out = sem("lora_out")
        ones_out = sem("ones_out")
        wq_in = [sem(f"wq_in{i}") for i in range(3)]
        wq_abs = sem("wq_abs")
        wq_sum = sem("wq_sum")
        wq_scale = sem("wq_scale")
        wq_step = sem("wq_step")
        wq_done = sem("wq_done")
        misc_in = sem("misc_in")
        lora_sb = c_rows[0:64, :, 0:768]
        wq_raw = (h[:, :, :], G[:, 1, :, :], G[:, 2, :, :])

        def setup_sp(sp):
            sp.dma_start(side[:, :, :], io["side"]).then_inc(side_in, 16)
            sp.dma_start(wu[:, :, :, :], io["wu"]).then_inc(cond_in, 16)
            sp.dma_start(cond_bc[:, :, :], io["cond"].unsqueeze(0).to_broadcast([P, B, 64])).then_inc(cond_in, 16)
            sp.dma_start(x[:, :, :], io["x"]).then_inc(x_in, 16)
            sp.dma_start(w_attn[:, :, :], io["L0_w_attn"]).then_inc(attn_w["L0"], 16)
            sp.dma_start(w_out[:, 0:KC, :], io["L0_w_out"]).then_inc(attn_w["L0"], 16)
            sp.dma_start(bias_attn[:, :], io["attn_bias"]).then_inc(misc_in, 16)
            sp.dma_start(bias_v[:, :], io["L0_bias_v"].unsqueeze(0).to_broadcast([P, C])).then_inc(misc_in, 16)
            sp.dma_start(rope[:, :, :], io["rope"]).then_inc(misc_in, 16)
            sp.dma_start(earlier[:, :, :], io["earlier"]).then_inc(misc_in, 16)
            sp.dma_start(w_route[:, :, :, :], io["w_route"]).then_inc(misc_in, 16)
            sp.dma_start(temp[:, 0:1], io["temp"].unsqueeze(0).to_broadcast([P, 1])).then_inc(misc_in, 16)
            sp.dma_start(scan_c[:, 0:3 * KC], io["scan_c"]).then_inc(misc_in, 16)
            sp.dma_start(ab_in[:, :, :, :], io["scan_ab"]).then_inc(misc_in, 16)
            for i, name in enumerate(("L2_w_gate", "L2_w_up", "L2_w_down")):
                sp.dma_start(wq_raw[i], io[name]).then_inc(wq_in[i], 16)
            sp.wait_ge(const_p, 3)
            sp.dma_start(c_dram["L0"][176:200, :].rearrange("g (a n) -> g a n", a=8), ones[0:24, :].unsqueeze(1).to_broadcast([24, 8, P])).then_inc(ones_out, 16)
            for e in range(2):
                if e:
                    sp.wait_ge(lora_mm, 6)
                    sp.wait_ge(lora_out, 32)
                sp.dma_start(lora_sb, io["lora"][e]).then_inc(lora_in, 16)
                for f in range(2):
                    sp.dma_start(w_raw[:, f, :], io["L3_w"][2 * e + f]).then_inc(lora_raw[f], 16)
                sp.wait_ge(lora_add, 10 * e + 10)
                for f in range(2):
                    sp.dma_start(lora_dram[2 * e + f], w_raw[:, f, :]).then_inc(lora_out, 16)

        def setup_pool(pool):
            pool.memset(ident[:, :], 0.0).then_inc(const_p, 1)
            pool.memset(ident_bf[:, :], 0.0).then_inc(const_p, 1)
            pool.memset(ones[:, :], 1.0).then_inc(const_p, 1)
            pool.memset(negmask[:, :], 0.0).then_inc(const_p, 1)
            pool.memset(capmask[:, :], 0.0).then_inc(const_p, 1)
            pool.memset(zeros_bf[:, :], 0.0).then_inc(const_p, 1)
            pool.memset(half_c[:, :], -0.5).then_inc(const_p, 1)
            pool.wait_ge(const_p, 7)
            for m in (ident, ident_bf):
                pool.affine_select(out=m[:, :], in_=m[:, :], compare_op=ALU.not_equal, fill=1.0, base=0,
                                   pattern=[[-1, P]], channel_multiplier=1).then_inc(const_p, 1)
            for m, fill in ((negmask, NEG), (capmask, -1000.0)):
                pool.affine_select(out=m[:, :], in_=m[:, :], compare_op=ALU.is_ge, fill=fill, base=0,
                                   pattern=[[-1, P]], channel_multiplier=1).then_inc(const_p, 1)
            pool.wait_ge(side_in, 16)
            pool.wait_ge(setup_a, 4)
            with pool.Fori(0, B) as b:
                gate_pool(pool, 0, b)
            for b in range(B):
                gate_pool(pool, 1, b)
                if b < 3:
                    ternary_pool(pool, b, (wq_g, wq_u, wq_d)[b])

        def ternary_pool(pool, i, dst):
            raw = wq_raw[i].rearrange("p a b -> p (a b)")
            pool.wait_ge(wq_scale, 3 * i + 3)
            pool.tensor_scalar(raw, raw, wq_stat[:, i, 2:3], MAGIC, ALU.mult, ALU.add).then_inc(wq_step, 1)
            pool.wait_ge(wq_step, 2 * i + 1)
            pool.tensor_scalar(raw, raw, -MAGIC, 1.0, ALU.add, ALU.min).then_inc(wq_step, 1)
            pool.wait_ge(wq_step, 2 * i + 2)
            pool.tensor_scalar(dst[:, :, :].rearrange("p a b -> p (a b)"), raw, -1.0, None, ALU.max).then_inc(wq_done, 1)

        def setup_act(act):
            act.wait_ge(cond_in, 32)
            act.activation(ew[:, 0, :], wu[:, 0, :, :].rearrange("p c n -> p (c n)"), ACT.Exp).then_inc(setup_a, 1)
            act.wait_ge(setup_a, 1)
            act.activation(ew[:, 1, :], ew[:, 0, :], ACT.Exp, scale=-1.0).then_inc(setup_a, 1)
            act.wait_ge(setup_v, 1)
            act.activation(tf4[:, 1, :], tf4[:, 0, :], ACT.Tanh, scale=0.5).then_inc(setup_a, 1)
            act.wait_ge(setup_v, 2)
            act.activation(ek[:, :, :], ek[:, :, :], ACT.Exp).then_inc(setup_a, 1)
            with act.Fori(0, B) as b:
                gate_act(act, 0, b)

        def setup_dve(dve):
            dve.memset(scan_b[:, :, :, T - 1:T], 0.0).then_inc(g_done, 1)
            dve.memset(row_sum[:, :], 0.0).then_inc(scan_done, 1)
            dve.wait_ge(cond_in, 32)
            dve.tensor_reduce(tf4[:, 0, :], cond_bc[:, :, :], AX.X, ALU.add).then_inc(setup_v, 1)
            dve.wait_ge(side_in, 16)
            dve.tensor_scalar(ek[:, :, :], side[:, :, :], 30.0, None, ALU.min).then_inc(setup_v, 1)
            dve.wait_ge(setup_a, 3)
            dve.tensor_scalar(tf4[:, 2, :], tf4[:, 1, :], 0.25, 0.75, ALU.mult, ALU.add).then_inc(setup_v, 1)
            dve.tensor_scalar(gscale[:, :], tf4[:, 1, :], 0.05, 0.45, ALU.mult, ALU.add).then_inc(setup_v, 1)
            dve.wait_ge(setup_v, 4)
            dve.tensor_tensor(decay[:, :, :].rearrange("p c (n b) -> p (c n) b", b=B),
                              ew[:, 1, :].unsqueeze(2).to_broadcast([P, KC * CONDS, B]),
                              tf4[:, 2, :].unsqueeze(1).to_broadcast([P, KC * CONDS, B]), ALU.mult).then_inc(setup_v, 1)
            dve.wait_ge(setup_v, 5)
            with dve.Fori(0, B) as b:
                for part in range(5):
                    gate_dve(dve, part, 0, b)
                gate_finish(dve, 0, b, 0)
            for e in range(2):
                for f in range(2):
                    dve.wait_ge(lora_raw[f], 16 * (e + 1))
                dve.wait_ge(lora_mm, 6 * e + 6)
                for half in range(2):
                    for kc in range(KC):
                        for f in range(2):
                            o = w_raw[:, f, half * 256 + kc * P:half * 256 + kc * P + P]
                            dve.tensor_tensor(o, bank[2 * half + kc][:, f * P:f * P + P], o, ALU.add).then_inc(lora_add, 1)
                for f in range(2):
                    o = w_raw[:, f, 512:768]
                    dve.tensor_tensor(o, bank[4 + f][:, 0:C], o, ALU.add).then_inc(lora_add, 1)
            for i in range(3):
                dve.wait_ge(wq_in[i], 16)
                dve.tensor_reduce(wq_stat[:, i, 0:1], wq_raw[i].rearrange("p a b -> p (a b)"), AX.X, ALU.add,
                                  apply_absolute_value=True).then_inc(wq_abs, 1)
                dve.wait_ge(wq_sum, i + 1)
                dve.tensor_scalar(wq_stat[:, i, 1:2], bank[6][:, i:i + 1], 1.0 / (C * L2I), 1e-5, ALU.mult, ALU.max)\
                   .then_inc(wq_scale, 1)
                dve.wait_ge(wq_scale, 3 * i + 1)
                dve.reciprocal(wq_stat[:, i, 2:3], wq_stat[:, i, 1:2]).then_inc(wq_scale, 2)

        def setup_pe(pe):
            for e in range(2):
                pe.wait_ge(lora_in, 16 * (e + 1))
                if e:
                    pe.wait_ge(lora_add, 10)
                for half in range(2):
                    for kc in range(KC):
                        a, bcol = 2 * half * 256, (2 * half + 1) * 256
                        pe.matmul(bank[2 * half + kc][:, 0:C], lora_at(a + kc * P, P), lora_at(bcol, C),
                                  start=True, stop=True).then_inc(lora_mm, 1)
                for f in range(2):
                    pe.matmul(bank[4 + f][:, 0:C], lora_at(4 * 256 + f * P, P), lora_at(5 * 256, C),
                              start=True, stop=True).then_inc(lora_mm, 1)
            pe.wait_ge(const_p, 3)
            for i in range(3):
                pe.wait_ge(wq_abs, i + 1)
                pe.matmul(bank[6][:, i:i + 1], ones[:, :], wq_stat[:, i, 0:1], start=True, stop=True).then_inc(wq_sum, 1)

        def lora_at(col, width):
            return lora_sb[:, col // 768, col % 768:col % 768 + width]

        attn_w = {l: sem(f"{l}_attn_w") for l in ("L0", "L1", "L3")}

        attn_sems = [
            sem("attn_tanh"),
            sem("attn_gated"),
            sem("attn_proj"),
            sem("attn_copied"),
            sem("attn_v_ready"),
            sem("attn_scores"),
            sem("attn_negmax"),
            sem("attn_probs"),
            sem("attn_turned"),
            sem("attn_even"),
            sem("attn_odd"),
            sem("attn_mixed"),
            sem("attn_norm"),
            sem("attn_turned_out"),
            sem("attn_out_copied"),
            sem("attn_out"),
            sem("attn_x_done"),
        ]
        attn_cap = sem("attn_cap")

        class Attention:
            def __init__(self, name, gate, next_gate, causal, q_scale, capped, ropes, biased, bias, d, v_heads, scrambled, x_ready, x_value, first, rope_step):
                self.name, self.gate, self.next_gate, self.bias = name, gate, next_gate, bias
                self.causal, self.q_scale, self.capped, self.ropes = causal, q_scale, capped, ropes
                self.biased, self.d, self.v_heads, self.scrambled = biased, d, v_heads, scrambled
                self.x_ready, self.x_value = x_ready, x_value
                self.chunks = HEADS * d // P
                self.first = first
                (self.tanh, self.gated, self.proj, self.copied, self.v_ready, self.scores, self.negmax, self.probs,
                 self.turned, self.even, self.odd, self.mixed, self.norm, self.turned_out, self.out_copied, self.out,
                 self.x_done) = attn_sems
                self.rope_step = rope_step
                self.cap = attn_cap

            def blocks(self):
                return [(0, 0, P), (1, P, T)] if self.causal else [(0, 0, T), (1, T, T)]

            def width(self):
                return 384 if self.causal else 512

            def corners(self):
                at, out = 0, []
                for q, col, keys in self.blocks():
                    for k in range(keys // P):
                        out.append((q, k, at, col + k * P))
                        at += P
                return out

            def front_pe(self, pe, it):
                L = self
                pe.wait_ge(L.gated, (it + self.first) + 1)
                for tt in range(2):
                    for kc in range(KC):
                        mm = pe.matmul(bank[4][:, tt * C:tt * C + C], hb[:, kc, tt * P:tt * P + P],
                                       w_attn[:, kc, 2 * GROUPS * P:ATTN_COLS], start=(kc == 0), stop=(kc == KC - 1))
                mm.then_inc(L.proj, 1)
                for n, pair in enumerate((0, 2, 1, 3)):
                    if n == 1:
                        pe.wait_ge(L.v_ready, (it + self.first) + 1)
                    if n >= 2:
                        pe.wait_ge(L.copied, (it + self.first) * 4 + n - 1)
                    for g in range(2):
                        for kc in range(KC):
                            mm = pe.matmul(bank[5 - n % 2][:, g * T:g * T + T],
                                           w_attn[:, kc, (pair * 2 + g) * P:(pair * 2 + g + 1) * P], hb[:, kc, :],
                                           start=(kc == 0), stop=(kc == KC - 1))
                    mm.then_inc(L.proj, 1)

            def qk_ready(self, eng, it, pairs):
                if self.ropes is not None:
                    eng.wait_ge(self.rope_step, it * 16 + 4 * pairs)
                else:
                    eng.wait_ge(self.copied, (it + self.first) * 4 + pairs)

            def scores_pe(self, pe, it, hd):
                L, g, j = self, hd // 4, hd % 4
                if hd in (0, HEADS // 2):
                    L.qk_ready(pe, it, 2 if hd == 0 else 4)
                rows = slice(SLOT * j, SLOT * j + SLOT)
                for q, col, keys in L.blocks():
                    mm = pe.matmul(bank[hd % 2][:, col:col + keys], qk[rows, g, q * P:q * P + P],
                                   qk[rows, GROUPS + g, 0:keys], start=True, stop=not (L.causal and not L.capped),
                                   tile_position=(SLOT * j, 0))
                    if L.causal and not L.capped:
                        mm = pe.matmul(bank[hd % 2][:, col + keys - P:col + keys], ident_bf[:, :], negmask[:, :],
                                       start=False, stop=True)
                mm.then_inc(L.scores, 1)

            def turn_pe(self, pe, it, hd):
                L = self
                pe.wait_ge(L.probs, (it + self.first) * HEADS + hd + 1)
                if hd >= 2:
                    pe.wait_ge(L.odd if hd % 2 else L.even, (it + self.first) * 8 + hd // 2)
                for q, k, at, col in L.corners():
                    mm = pe.transpose(bank[2 + hd % 2][:, at:at + P], probs[:, hd % 2, col:col + P], ident[:, :])
                mm.then_inc(L.turned, 1)

            def mix_pe(self, pe, it, hd):
                L, d = self, self.d
                pe.wait_ge(L.odd if hd % 2 else L.even, (it + self.first) * 8 + hd // 2 + 1)
                vh = hd * L.v_heads // HEADS
                for q, k, at, col in L.corners():
                    o = bank[6][:, q * C + hd * d:q * C + hd * d + d] if d == 16 else bank[6 + q][:, hd * d:hd * d + d]
                    mm = pe.matmul(o, probs_t[:, hd % 2, at:at + P], v_sb[:, k, vh * d:vh * d + d],
                                   start=(k == 0), stop=(k == (q if L.causal else 1)))
                if hd == HEADS - 1:
                    mm.then_inc(L.mixed, 1)

            def heads_pe(self, pe, it):
                self.scores_pe(pe, it, 0)
                self.scores_pe(pe, it, 1)
                for hd in range(HEADS):
                    self.turn_pe(pe, it, hd)
                    if hd >= 1:
                        self.mix_pe(pe, it, hd - 1)
                    if hd + 2 < HEADS:
                        self.scores_pe(pe, it, hd + 2)
                self.mix_pe(pe, it, HEADS - 1)

            def tail_pe(self, pe, it, src, ahead):
                L = self
                pe.wait_ge(L.norm, self.first * 2 + 2 * B if L.scrambled else (it + self.first) * 2 + 2)
                if ahead:
                    pe.wait_ge(L.copied, (it + self.first) * 4 + 8)
                if L.scrambled and it:
                    pe.wait_ge(L.x_done, (it + self.first))
                for ch in range(L.chunks):
                    for q in range(2):
                        mm = pe.transpose(bank[5 - ch // 2][:, (ch % 2) * T + q * P:(ch % 2) * T + q * P + P],
                                          src(q, ch), ident[:, :])
                mm.then_inc(L.turned_out, 1)
                pe.wait_ge(L.out_copied, (it + self.first) + 1)
                for m in range(KC):
                    for ch in range(L.chunks):
                        mm = pe.matmul(bank[6][:, m * T:m * T + T], w_out[:, ch, m * P:m * P + P], attn_t[:, ch, :],
                                       start=(ch == 0), stop=(ch == L.chunks - 1))
                mm.then_inc(L.out, 1)

            def gate_act(self, act, it):
                act.wait_ge(self.x_ready, self.x_value)
                act.activation(hb[:, :, :], x[:, :, DSZ(it * T, T)], ACT.Tanh, scale=0.5).then_inc(self.tanh, 1)

            def front_act(self, act, it):
                L = self
                for n, pair in enumerate((0, 2, 1, 3)):
                    act.wait_ge(L.proj, (it + self.first) * 5 + n + 2)
                    src = bank[5 - n % 2]
                    dst = qk[:, pair * 2:pair * 2 + 2, :]
                    if L.biased:
                        for g in range(2):
                            a = act.activation(dst[:, g, :], src[:, g * T:g * T + T], ACT.Identity,
                                               bias=bias_attn[:, pair * 2 + g:pair * 2 + g + 1])
                    else:
                        a = act.activation(dst, src[:, :].rearrange("p (g t) -> p g t", g=2), ACT.Copy,
                                           scale=L.q_scale if pair < 2 else 1.0)
                    a.then_inc(L.copied, 1)

            def softmax_act(self, act, it, hd):
                L = self
                if L.capped:
                    act.wait_ge(L.scores, (it + self.first) * HEADS + hd + 1)
                    act.activation(probs[:, hd % 2, 0:L.width()], bank[hd % 2][:, 0:L.width()], ACT.Tanh,
                                   scale=1.0 / (16.0 * CAP)).then_inc(L.cap, 1)
                    act.wait_ge(L.negmax, (it + self.first) * HEADS + hd + 1)
                else:
                    act.wait_ge(L.negmax, (it + self.first) * HEADS + hd + 1)
                for q, col, keys in L.blocks():
                    src = probs[:, hd % 2, col:col + keys] if L.capped else bank[hd % 2][:, col:col + keys]
                    a = act.activation(probs[:, hd % 2, col:col + keys], src, ACT.Exp, scale=CAP if L.capped else 1.0,
                                       bias=0.0 if L.capped else row_max[:, q * HEADS + hd:q * HEADS + hd + 1],
                                       accum_out=row_sum[:, q * HEADS + hd:q * HEADS + hd + 1])
                a.then_inc(L.probs, 1)

            def copy_act(self, act, it, hd):
                act.wait_ge(self.turned, (it + self.first) * HEADS + hd + 1)
                act.activation(probs_t[:, hd % 2, 0:self.width()], bank[2 + hd % 2][:, 0:self.width()], ACT.Copy)\
                   .then_inc(self.even, 1)

            def heads_act(self, act, it, last):
                for hd in range(HEADS):
                    self.softmax_act(act, it, hd)
                    if hd >= 1 and (hd - 1) % 2 == 0:
                        self.copy_act(act, it, hd - 1)
                    if hd == 2 and self.next_gate is not None:
                        gate_act(act, self.next_gate, it)
                    if hd == 8 and not last:
                        act.wait_ge(self.proj, (it + self.first) * 5 + 5)
                        self.gate_act(act, it + 1)

            def tail_act(self, act, it):
                L = self
                act.wait_ge(L.turned_out, (it + self.first) + 1)
                for n in range(L.chunks // 2):
                    a = act.activation(attn_t[:, 2 * n:2 * n + 2, :], bank[5 - n][:, :].rearrange("p (c t) -> p c t", c=2), ACT.Copy)
                a.then_inc(L.out_copied, 1)

            def gate_dve(self, dve, it):
                dve.wait_ge(self.tanh, (it + self.first) + 1)
                if isinstance(it, int) and it == 0:
                    dve.wait_ge(g_done, 4 * self.gate + 5)
                dve.scalar_tensor_tensor(out=hb[:, :, :], in0=hb[:, :, :], scalar=1.0,
                                         in1=G[:, G_SLOT[self.gate], :, DSZ(it * T, T)], op0=ALU.add, op1=ALU.mult)\
                   .then_inc(self.gated, 1)

            def front_dve(self, dve, it):
                L = self
                dve.wait_ge(L.proj, (it + self.first) * 5 + 1)
                vv = v_sb[:, :, :].rearrange("p a b -> p (a b)")
                if L.biased:
                    dve.tensor_tensor(v_sb[:, :, :], bank[4][:, :].rearrange("p (a b) -> p a b", a=2),
                                      bias_v[:, :].unsqueeze(1).to_broadcast([P, 2, C]), ALU.add).then_inc(L.v_ready, 1)
                else:
                    dve.tensor_copy(vv, bank[4][:, :]).then_inc(L.v_ready, 1)
                if L.ropes is None:
                    return
                mask, tab = L.ropes
                cos = rope[:, tab, :].unsqueeze(1).to_broadcast([P, 2, T])
                sin = rope[:, tab + 1, :].unsqueeze(1).to_broadcast([P, 2, T])
                for n, pair in enumerate((0, 2, 1, 3)):
                    dst = qk[:, pair * 2:pair * 2 + 2, :]
                    at = it * 16 + 4 * n
                    if n:
                        dve.wait_ge(L.rope_step, at)
                    dve.wait_ge(L.copied, (it + self.first) * 4 + n + 1)
                    dve.tensor_tensor(rope_b[:, :, :], dst, cos, ALU.mult).then_inc(L.rope_step, 1)
                    dve.stream_shuffle(rope_a[:, :, :], dst, mask).then_inc(L.rope_step, 1)
                    dve.wait_ge(L.rope_step, at + 2)
                    dve.tensor_tensor(rope_a[:, :, :], rope_a[:, :, :], sin, ALU.mult).then_inc(L.rope_step, 1)
                    dve.wait_ge(L.rope_step, at + 3)
                    dve.tensor_tensor(dst, rope_a[:, :, :], rope_b[:, :, :], ALU.add).then_inc(L.rope_step, 1)

            def max_dve(self, dve, it, hd):
                L = self
                if L.capped:
                    dve.wait_ge(L.cap, it * HEADS + hd + 1)
                    v = probs[:, hd % 2, 0:512].rearrange("p (a b) -> p a b", a=2)[:, :, 0:P]
                    dve.tensor_tensor(v, v, capmask[:, :].unsqueeze(1).to_broadcast([P, 2, P]), ALU.add).then_inc(L.negmax, 1)
                    return
                dve.wait_ge(L.scores, (it + self.first) * HEADS + hd + 1)
                for q, col, keys in L.blocks():
                    r = dve.tensor_reduce(row_max[:, q * HEADS + hd:q * HEADS + hd + 1], bank[hd % 2][:, col:col + keys],
                                          AX.X, ALU.max, negate=True)
                r.then_inc(L.negmax, 1)

            def copy_dve(self, dve, it, hd):
                dve.wait_ge(self.turned, (it + self.first) * HEADS + hd + 1)
                dve.tensor_copy(probs_t[:, hd % 2, 0:self.width()], bank[2 + hd % 2][:, 0:self.width()]).then_inc(self.odd, 1)

            def heads_dve(self, dve, it, last):
                n = self.next_gate
                for hd in range(HEADS):
                    self.max_dve(dve, it, hd)
                    if hd >= 2 and hd % 2 == 0:
                        self.copy_dve(dve, it, hd - 1)
                    if n is not None:
                        if hd in (1, 2, 5, 6, 9):
                            gate_dve(dve, (1, 2, 5, 6, 9).index(hd), n, it)
                        if hd == 11:
                            gate_finish(dve, n, it, G_SLOT[n])
                    if hd == 8 and not last:
                        self.gate_dve(dve, it + 1)
                self.copy_dve(dve, it, HEADS - 1)

            def norm_dve(self, dve, it):
                L, d = self, self.d
                dve.wait_ge(L.mixed, (it + self.first) + 1)
                dve.reciprocal(row_inv[:, :], row_sum[:, :]).then_inc(L.norm, 1)
                dve.wait_ge(L.norm, (it + self.first) * 2 + 1)
                inv = row_inv[:, :].rearrange("p (q h) -> p q h", q=2)
                for q in range(2):
                    src = bank[6][:, q * C:q * C + C] if d == 16 else bank[6 + q][:, :]
                    if L.scrambled:
                        for tb in range(4):
                            r = dve.tensor_tensor(h[:, q, DSZ(it * 64 + tb * 256, 64)].rearrange("p (g e) -> p g e", g=4),
                                                  src.rearrange("p (g t e) -> p t g e", g=4, t=4)[:, tb],
                                                  inv[:, q, :].rearrange("p (g t) -> p t g", g=4)[:, tb].unsqueeze(2).to_broadcast([P, 4, 16]),
                                                  ALU.mult)
                    else:
                        r = dve.tensor_tensor(attn[:, q, 0:HEADS * d].rearrange("p (g e) -> p g e", g=HEADS),
                                              src.rearrange("p (g e) -> p g e", g=HEADS),
                                              inv[:, q, :].unsqueeze(2).to_broadcast([P, HEADS, d]), ALU.mult)
                r.then_inc(L.norm, 1)

            def tail_dve(self, dve, it):
                L, bias = self, self.bias
                dve.wait_ge(L.out, (it + self.first) + 1)
                for m in range(KC):
                    xs = x[:, m, DSZ(it * T, T)]
                    y = bank[6][:, m * T:m * T + T]
                    if bias is None:
                        r = dve.tensor_tensor(xs, y, xs, ALU.add)
                    else:
                        r = dve.scalar_tensor_tensor(out=xs, in0=y, scalar=bias_attn[:, bias + m:bias + m + 1], in1=xs,
                                                     op0=ALU.add, op1=ALU.add)
                r.then_inc(L.x_done, 1)

            def pe(self, pe):
                L = self
                attn_src = lambda q, ch: attn[:, q, ch * P:ch * P + P]
                pe.wait_ge(attn_w[L.name], 32)
                if L.name == "L0":
                    pe.wait_ge(const_p, 11)
                L.front_pe(pe, 0)
                with pe.Fori(0, B - 1) as it:
                    L.heads_pe(pe, it)
                    L.front_pe(pe, it + 1)
                    if not L.scrambled:
                        L.tail_pe(pe, it, attn_src, True)
                L.heads_pe(pe, B - 1)
                if not L.scrambled:
                    L.tail_pe(pe, B - 1, attn_src, False)
                else:
                    for tb in range(B):
                        L.tail_pe(pe, tb, lambda q, ch: h[:, q, tb * C + ch * P:tb * C + ch * P + P], False)

            def act(self, act):
                L = self
                if L.name == "L0":
                    act.wait_ge(misc_in, 16 * 8)
                L.gate_act(act, 0)
                L.front_act(act, 0)
                with act.Fori(0, B - 1) as it:
                    L.heads_act(act, it, False)
                    L.front_act(act, it + 1)
                    if not L.scrambled:
                        L.tail_act(act, it)
                L.heads_act(act, B - 1, True)
                for tb in range(0 if L.scrambled else B - 1, B):
                    L.tail_act(act, tb)

            def dve(self, dve):
                L = self
                if L.name == "L0":
                    dve.wait_ge(misc_in, 16 * 8)
                    dve.wait_ge(const_p, 11)
                L.gate_dve(dve, 0)
                L.front_dve(dve, 0)
                with dve.Fori(0, B - 1) as it:
                    L.heads_dve(dve, it, False)
                    L.norm_dve(dve, it)
                    L.front_dve(dve, it + 1)
                    if not L.scrambled:
                        L.tail_dve(dve, it)
                L.heads_dve(dve, B - 1, True)
                L.norm_dve(dve, B - 1)
                for tb in range(0 if L.scrambled else B - 1, B):
                    L.tail_dve(dve, tb)

        ffn_sems = [
            sem("ffn_tanh"),
            sem("ffn_gated"),
            sem("ffn_hi"),
            sem("ffn_lo"),
            sem("ffn_logits"),
            sem("ffn_c_turned"),
            sem("ffn_c_copied"),
            sem("ffn_c_out"),
            sem("ffn_summed"),
            sem("ffn_x_done"),
        ]

        class Experts:
            def __init__(self, name, gate, chunks, experts, reps, next_gates, x_ready, x_value, route_at, sources, before, k):
                self.before = before
                self.name, self.gate, self.chunks, self.E, self.reps = name, gate, chunks, experts, reps
                self.next_gates, self.x_ready, self.x_value, self.route_at = next_gates, x_ready, x_value, route_at
                self.sources = sources
                s = lambda n: sem(f"{name}_ffn_{n}")
                self.tanh, self.gated, self.hi, self.lo, self.logits, self.c_turned, self.c_copied, self.c_out, self.summed, self.x_done = ffn_sems
                self.r_step, self.r_act = s("r_step"), s("r_act")
                self.w_in, self.c_in = [s("w_in0"), s("w_in1")], [s("c_in0"), s("c_in1")]
                self.gu_hi, self.gu_lo = s("gu_hi"), s("gu_lo")
                self.d_hi, self.d_lo = s("d_hi"), s("d_lo")
                self.gate_mm, self.up_mm, self.down = s("gate_mm"), s("up_mm"), s("down")
                self.silu, self.act_hi = s("silu"), s("act_hi")
                self.mul, self.scaled, self.act_lo = s("mul"), s("scaled"), s("act_lo")
                self.k = k

            def load_w(self, sp, src, slot):
                sp.dma_start(w_raw[:, slot, :], src).then_inc(self.w_in[slot], 16)

            def load_c(self, sp, c, slot):
                src = c_dram[self.name][DSZ(c * GRANULES, GRANULES), :].unsqueeze(1).to_broadcast([GRANULES, EXPERT_ROWS, N])
                sp.dma_start(c_rows[:, slot, :], src).then_inc(self.c_in[slot], 16)

            def prefetch_sp(self, sp):
                if self.before is not None:
                    sp.wait_ge(self.before.d_lo, self.before.chunks)
                    sp.wait_ge(self.before.gu_lo, self.before.chunks + 1)
                for c in (0, 1):
                    self.load_w(sp, self.sources(c), c)

            def sp(self, sp):
                n = self.chunks
                sp.wait_ge(self.c_copied, 2 * self.k + 2)
                sp.dma_start(c_dram[self.name][0:self.E * self.reps, :].rearrange("(e r) t -> e r t", r=self.reps),
                             c_t[0:self.E, :].unsqueeze(1).to_broadcast([self.E, self.reps, N])).then_inc(self.c_out, 16)
                sp.wait_ge(self.c_out, 16 * self.k + 16)
                if self.name == "L0":
                    sp.wait_ge(ones_out, 16)
                for c in (0, 1):
                    self.load_c(sp, c, c)

                def load(c, slot, src, rows=True):
                    sp.wait_ge(self.d_lo, c - 1)
                    self.load_w(sp, src, slot)
                    if rows:
                        sp.wait_ge(self.scaled, c * 2 - 2)
                        self.load_c(sp, c, slot)

                c = 2
                while not isinstance(self.sources(c), tuple):
                    load(c, c % 2, self.sources(c))
                    c += 1
                dram = self.sources(c)[0]
                with sp.Fori(0, (n - c) // 2) as i:
                    for k in range(2):
                        load(i * 2 + (c + k), (c + k) % 2, dram[DSZ(i * 2 + (c + k), 1)].rearrange("a p k -> (a p) k"))
                if (n - c) % 2:
                    load(n - 1, (n - 1) % 2, dram[n - 1])
                load(n, n % 2, dram[n], rows=False)

            def three(self, pe, o, w_hi, w_lo, r_hi, r_lo, start, stop):
                pe.matmul(o, w_hi, r_hi, start=start, stop=False)
                pe.matmul(o, w_lo, r_hi, start=False, stop=False)
                return pe.matmul(o, w_hi, r_lo, start=False, stop=stop)

            def gate_up_pe(self, pe, c, slot, half, first):
                L = self
                if not first:
                    pe.wait_ge(L.silu, c * 2 - 1 + half)
                    pe.wait_ge(L.mul, c * 2 - 1 + half)
                tok = slice(half * HALF, half * HALF + HALF)
                for n, done in enumerate((L.gate_mm, L.up_mm)):
                    for kc in range(KC):
                        w = slice((2 * n + kc) * P, (2 * n + kc) * P + P)
                        mm = L.three(pe, bank[2 * half + n][:, :], w_gu_hi[:, slot, w], w_gu_lo[:, slot, w],
                                     h_hi[:, kc, tok], h_lo[:, kc, tok], kc == 0, kc == KC - 1)
                    mm.then_inc(done, 1)

            def down_pe(self, pe, c, slot, half):
                L = self
                if half == 0:
                    pe.wait_ge(L.d_lo, c + 1)
                pe.wait_ge(L.act_lo, c * 2 + half + 1)
                for m in range(KC):
                    w = slice(m * P, m * P + P)
                    mm = L.three(pe, bank[4 + 2 * m + half][:, :], w_d_hi[:, slot, w], w_d_lo[:, slot, w],
                                 act_hi[:, half, :], act_lo[:, half, :], False, False)
                mm.then_inc(L.down, 1)

            def step_pe(self, pe, c, slot, first=False):
                pe.wait_ge(self.gu_lo, c + 1)
                for half in range(2):
                    self.gate_up_pe(pe, c, slot, half, first)
                    if not first:
                        self.down_pe(pe, c - 1, 1 - slot, half)

            def loops(self, eng, body, extra=None):
                rounds = (self.chunks - 1) // 2
                if self.next_gates:
                    with eng.Fori(0, len(self.next_gates)) as g:
                        with eng.Fori(0, B) as b:
                            for k in range(2):
                                body(g * 8 + b * 2 + (k + 1), (k + 1) % 2, (g + self.next_gates[0], b, k, g))
                else:
                    with eng.Fori(0, rounds) as i:
                        for k in range(2):
                            body(i * 2 + (k + 1), (k + 1) % 2, None)
                if (self.chunks - 1) % 2:
                    body(self.chunks - 1, (self.chunks - 1) % 2, None)

            def pe(self, pe):
                L, E = self, self.E
                pe.wait_ge(L.gated, 2 * L.k + 2)
                for tt in range(TILES):
                    for kc in range(KC):
                        mm = pe.matmul(bank[4][:, tt * E:tt * E + E], h[:, kc, tt * P:tt * P + P],
                                       w_route[:, L.route_at, kc, 0:E], start=(kc == 0), stop=(kc == KC - 1))
                mm.then_inc(L.logits, 1)
                pe.wait_ge(L.lo, 2 * L.k + 2)
                L.step_pe(pe, 0, 0, first=True)
                pe.wait_ge(L.r_step, L.route_steps)
                for half in range(2):
                    for tt in range(4):
                        mm = pe.transpose(bank[5 + half][0:E, tt * P:tt * P + P],
                                          route[:, 0, (half * 4 + tt) * E:(half * 4 + tt + 1) * E], ident[:, :])
                    mm.then_inc(L.c_turned, 1)
                pe.wait_ge(L.c_copied, 2 * L.k + 2)
                for i in range(4):
                    pe.matmul(bank[4 + i][:, :], zeros_bf[:, 0:P], zeros_bf[:, :], start=True, stop=False)
                L.loops(pe, lambda c, slot, _: L.step_pe(pe, c, slot))
                for half in range(2):
                    L.down_pe(pe, L.chunks - 1, (L.chunks - 1) % 2, half)
                for i in range(4):
                    mm = pe.matmul(bank[4 + i][:, :], zeros_bf[:, 0:P], zeros_bf[:, :], start=False, stop=True)
                mm.then_inc(L.summed, 1)

            def split_gu_act(self, act, c, slot, wait_up):
                act.wait_ge(self.w_in[slot], wait_up[0])
                if wait_up[1] is not None:
                    act.wait_ge(self.up_mm, wait_up[1])
                act.activation(w_gu_hi[:, slot, :], w_raw[:, slot, 0:512], ACT.Copy).then_inc(self.gu_hi, 1)

            def split_d_act(self, act, c, slot):
                act.activation(w_d_hi[:, slot, :], w_raw[:, slot, 512:768], ACT.Copy).then_inc(self.d_hi, 1)

            def step_act(self, act, c, slot, loaded, gate, first=False):
                L = self
                for half in range(2):
                    act.wait_ge(L.gate_mm, c * 2 + half + 1)
                    act.activation(act_s[:, half, :], bank[2 * half][:, :], ACT.Silu).then_inc(L.silu, 1)
                    if half == 0:
                        L.split_gu_act(act, c + 1, 1 - slot, (loaded, None if first else c * 2))
                        if first:
                            L.split_d_act(act, 0, 0)
                    act.wait_ge(L.scaled, c * 2 + half + 1)
                    if not first:
                        act.wait_ge(L.down, c * 2 - 1 + half)
                    act.activation(act_hi[:, half, :], act_a[:, half, :], ACT.Copy).then_inc(L.act_hi, 1)
                    if half == 0 and gate is not None and gate[2] == 0:
                        gate_act(act, gate[0], gate[1])
                if not first:
                    L.split_d_act(act, c, slot)

            def act(self, act):
                L = self
                act.wait_ge(L.x_ready, L.x_value)
                if L.name == "L0":
                    act.wait_ge(wq_done, 3)
                for half in range(2):
                    tok = slice(half * HALF, half * HALF + HALF)
                    act.activation(h[:, :, tok], x[:, :, tok], ACT.Tanh, scale=0.5).then_inc(L.tanh, 1)
                for half in range(2):
                    tok = slice(half * HALF, half * HALF + HALF)
                    act.wait_ge(L.gated, 2 * L.k + half + 1)
                    act.activation(h_hi[:, :, tok], h[:, :, tok], ACT.Copy).then_inc(L.hi, 1)
                L.split_gu_act(act, 0, 0, (16, None))
                L.route_act(act)
                for half in range(2):
                    act.wait_ge(L.c_turned, 2 * L.k + half + 1)
                    act.activation(c_t[0:L.E, half * HALF:half * HALF + HALF], bank[5 + half][0:L.E, :], ACT.Copy).then_inc(L.c_copied, 1)
                L.step_act(act, 0, 0, 16, None, first=True)

                def body(c, slot, gate):
                    L.step_act(act, c, slot, L.loads(c + 1, 1 - slot), gate)
                L.loops(act, body)

            def loads(self, c, slot):
                return (c - slot) * 8 + 16

            def pool(self, pool):
                L = self

                def gu(c, slot):
                    pool.wait_ge(L.gu_hi, c + 1)
                    pool.tensor_tensor(w_gu_lo[:, slot, :], w_raw[:, slot, 0:512], w_gu_hi[:, slot, :].bitcast(F32), ALU.subtract)\
                        .then_inc(L.gu_lo, 1)

                def d(c, slot):
                    pool.wait_ge(L.d_hi, c + 1)
                    pool.tensor_tensor(w_d_lo[:, slot, :], w_raw[:, slot, 512:768], w_d_hi[:, slot, :].bitcast(F32), ALU.subtract)\
                        .then_inc(L.d_lo, 1)

                gu(0, 0)
                gu(1, 1)
                d(0, 0)

                def body(c, slot, gate):
                    if gate is not None and gate[2] == 0:
                        gate_pool(pool, gate[0], gate[1])
                    gu(c + 1, 1 - slot)
                    d(c, slot)
                L.loops(pool, body)

            def step_dve(self, dve, c, slot, loaded, gate):
                L = self
                for half in range(2):
                    tok = slice(half * HALF, half * HALF + HALF)
                    n = c * 2 + half + 1
                    dve.wait_ge(L.silu, n)
                    dve.wait_ge(L.up_mm, n)
                    dve.tensor_tensor(act_m[:, half, :], bank[2 * half + 1][:, :], act_s[:, half, :], ALU.mult).then_inc(L.mul, 1)
                    if half == 0:
                        dve.wait_ge(L.c_in[slot], loaded)
                    dve.wait_ge(L.mul, n)
                    dve.tensor_tensor(act_a[:, half, :], act_m[:, half, :], c_rows[:, slot, tok], ALU.mult).then_inc(L.scaled, 1)
                    if gate is not None:
                        g, b, k, local = gate
                        for part in ((0, 1), (2, 3)) [half] if k == 0 else ((4,), ())[half]:
                            gate_dve(dve, part, g, b)
                        if k == 1 and half == 1:
                            L.gate_finish_dve(dve, g, b, local)
                    dve.wait_ge(L.act_hi, n)
                    dve.tensor_tensor(act_lo[:, half, :], act_a[:, half, :], act_hi[:, half, :].bitcast(F32), ALU.subtract)\
                       .then_inc(L.act_lo, 1)

            def gate_finish_dve(self, dve, n, b, local):
                s = n * 4 + b
                dve.wait_ge(wkv_inv, s + 1)
                dve.scalar_tensor_tensor(out=G_run(G_SLOT[self.next_gates[0]], local, b), in0=wkv_num[:, :, :], scalar=gscale[:, DSZ(b, 1)],
                                         in1=wkv_rec[:, :, :], op0=ALU.mult, op1=ALU.mult).then_inc(g_done, 1)

            def dve(self, dve):
                L = self
                for half in range(2):
                    tok = slice(half * HALF, half * HALF + HALF)
                    dve.wait_ge(L.tanh, 2 * L.k + half + 1)
                    if half == 0:
                        dve.wait_ge(g_done, 4 * L.gate + 5)
                    dve.scalar_tensor_tensor(out=h[:, :, tok], in0=h[:, :, tok], scalar=1.0, in1=G[:, G_SLOT[L.gate], :, tok],
                                             op0=ALU.add, op1=ALU.mult).then_inc(L.gated, 1)
                for half in range(2):
                    tok = slice(half * HALF, half * HALF + HALF)
                    dve.wait_ge(L.gated, 2 * L.k + 2)
                    dve.wait_ge(L.hi, 2 * L.k + half + 1)
                    dve.tensor_tensor(h_lo[:, :, tok], h[:, :, tok], h_hi[:, :, tok].bitcast(F32), ALU.subtract).then_inc(L.lo, 1)
                L.route_dve(dve)
                L.step_dve(dve, 0, 0, 16, None)
                L.loops(dve, lambda c, slot, gate: L.step_dve(dve, c, slot, L.loads(c, slot), gate))
                dve.wait_ge(L.summed, 1 * L.k + 1)
                for half in range(2):
                    for m in range(KC):
                        xs = x[:, m, half * HALF:half * HALF + HALF]
                        dve.tensor_tensor(xs, bank[4 + 2 * m + half][:, :], xs, ALU.add).then_inc(L.x_done, 1)

            def tab(self, i):
                return route[:, i, 0:TILES * self.E].rearrange("p (t e) -> p t e", e=self.E)

            def rank_dve(self, dve, do, src, dst):
                E = self.E
                big = lambda t: t[:, :, :].rearrange("p a b -> p (a b)")[:, 0:4 * E * E].rearrange("p (t i j) -> p t i j", i=E, j=E)
                for half in range(2):
                    v = src[:, 4 * half:4 * half + 4, :]
                    vj = v.unsqueeze(2).to_broadcast([P, 4, E, E])
                    vi = v.unsqueeze(3).to_broadcast([P, 4, E, E])
                    do(dve.tensor_tensor(big(act_s), vj, vi, ALU.is_ge))
                    do(dve.tensor_tensor(big(act_m), vj, vi, ALU.is_gt))
                    do(dve.tensor_tensor(big(act_s), big(act_s), earlier[:, 0:E, 0:E].unsqueeze(1).to_broadcast([P, 4, E, E]), ALU.mult))
                    do(dve.tensor_tensor(big(act_s), big(act_s), big(act_m), ALU.max))
                    do(dve.tensor_reduce(dst[:, 4 * half:4 * half + 4, :], big(act_s), AX.X, ALU.add))

            def route_dve(self, dve):
                L, E = self, self.E
                steps = [0]

                def do(ins):
                    steps[0] += 1
                    ins.then_inc(L.r_step, 1)
                    dve.wait_ge(L.r_step, steps[0])

                def sync():
                    L.act_turns.append(steps[0])
                    dve.wait_ge(L.r_act, len(L.act_turns))

                L.act_turns = []
                tb, bc = L.tab, lambda i: route_s[:, i, :].unsqueeze(2).to_broadcast([P, TILES, E])
                dve.wait_ge(L.logits, 1 * L.k + 1)
                do(dve.tensor_copy(route[:, 1, 0:TILES * E], bank[4][:, 0:TILES * E]))
                lg = tb(1)
                if L.name == "L0":
                    L.rank_dve(dve, do, lg, tb(2))
                    do(dve.tensor_scalar(tb(2), tb(2), 5.5, None, ALU.is_lt))
                    do(dve.tensor_reduce(route_s[:, 0, :], lg, AX.X, ALU.max))
                    do(dve.tensor_tensor(tb(3), lg, bc(0), ALU.subtract))
                    sync()
                    do(dve.tensor_reduce(route_s[:, 1, :], tb(3), AX.X, ALU.add))
                    do(dve.reciprocal(route_s[:, 2, :], route_s[:, 1, :]))
                    do(dve.tensor_tensor(tb(3), tb(3), bc(2), ALU.mult))
                    do(dve.tensor_tensor(tb(4), tb(3), tb(2), ALU.mult))
                    do(dve.tensor_reduce(route_s[:, 3, :], tb(4), AX.X, ALU.add))
                    do(dve.tensor_scalar(route_s[:, 3, :], route_s[:, 3, :], 1e-20, None, ALU.add))
                    do(dve.reciprocal(route_s[:, 4, :], route_s[:, 3, :]))
                    do(dve.tensor_tensor(tb(0), tb(4), bc(4), ALU.mult))
                elif L.name == "L1":
                    L.rank_dve(dve, do, lg, tb(2))
                    do(dve.tensor_scalar(tb(3), tb(2), 0.5, None, ALU.is_lt))
                    do(dve.tensor_scalar(tb(4), tb(2), 1.0, None, ALU.is_equal))
                    do(dve.tensor_tensor(tb(4), tb(4), tb(3), ALU.subtract))
                    do(dve.tensor_tensor(tb(4), tb(4), lg, ALU.mult))
                    do(dve.tensor_reduce(route_s[:, 0, :], tb(4), AX.X, ALU.add))
                    sync()
                    do(dve.tensor_scalar(route_s[:, 1, :], route_s[:, 0, :], 1.0, None, ALU.add))
                    do(dve.reciprocal(route_s[:, 2, :], route_s[:, 1, :]))
                    do(dve.tensor_tensor(tb(0), tb(3), bc(2), ALU.mult))
                else:
                    center = float(1.0 / np.e)
                    lower = float(0.5 - np.log(4.0 / 3.0))
                    do(dve.reciprocal(temp[:, 1:2], temp[:, 0:1]))
                    do(dve.tensor_scalar(lg, lg, temp[:, 1:2], None, ALU.mult))
                    sync()
                    do(dve.tensor_scalar(tb(2), tb(2), 0.5, 0.5, ALU.mult, ALU.add))
                    do(dve.tensor_scalar(tb(3), tb(2), lower, None, ALU.is_ge))
                    do(dve.tensor_scalar(tb(4), tb(2), 0.5, None, ALU.is_le))
                    do(dve.tensor_tensor(tb(3), tb(3), tb(4), ALU.mult))
                    do(dve.tensor_scalar(tb(4), tb(2), -1.0, center, ALU.mult, ALU.add))
                    do(dve.scalar_tensor_tensor(out=tb(2), in0=tb(2), scalar=center, in1=tb(4), op0=ALU.subtract, op1=ALU.max))
                    sync()
                    do(dve.tensor_tensor(tb(4), tb(4), tb(3), ALU.mult))
                    do(dve.tensor_reduce(route_s[:, 0, :], tb(4), AX.X, ALU.add))
                    do(dve.tensor_scalar(route_s[:, 1, :], route_s[:, 0, :], 1e-8, None, ALU.is_lt))
                    L.rank_dve(dve, do, tb(5), tb(6))
                    do(dve.tensor_scalar(tb(6), tb(6), 1.5, None, ALU.is_lt))
                    do(dve.tensor_tensor(tb(5), tb(5), tb(6), ALU.mult))
                    do(dve.tensor_reduce(route_s[:, 2, :], tb(5), AX.X, ALU.add))
                    do(dve.tensor_scalar(route_s[:, 2, :], route_s[:, 2, :], 1e-8, None, ALU.max))
                    do(dve.reciprocal(route_s[:, 3, :], route_s[:, 2, :]))
                    do(dve.tensor_tensor(tb(5), tb(5), bc(3), ALU.mult))
                    do(dve.tensor_tensor(tb(5), tb(5), bc(1), ALU.mult))
                    do(dve.tensor_scalar(route_s[:, 4, :], route_s[:, 1, :], -1.0, 1.0, ALU.mult, ALU.add))
                    do(dve.tensor_tensor(tb(4), tb(4), bc(4), ALU.mult))
                    do(dve.tensor_tensor(tb(4), tb(4), tb(5), ALU.add))
                    do(dve.tensor_reduce(route_s[:, 0, :], tb(4), AX.X, ALU.add))
                    do(dve.tensor_scalar(route_s[:, 0, :], route_s[:, 0, :], 1e-8, None, ALU.max))
                    do(dve.reciprocal(route_s[:, 5, :], route_s[:, 0, :]))
                    do(dve.tensor_tensor(tb(0), tb(4), bc(5), ALU.mult))
                assert steps[0] == L.route_steps, steps

            def route_act(self, act):
                L, tb = self, self.tab
                turns = dict(L0=(18 - 4,), L1=(16,), L3=(3, 9))[L.name]
                for n, at in enumerate(turns):
                    act.wait_ge(L.r_step, at)
                    if L.name == "L0":
                        a = act.activation(tb(3), tb(3), ACT.Exp)
                    elif L.name == "L1":
                        a = act.activation(route_s[:, 0, :], route_s[:, 0, :], ACT.Exp)
                    elif n == 0:
                        a = act.activation(tb(2), tb(1), ACT.Tanh, scale=0.5)
                    else:
                        act.activation(tb(4), tb(2), ACT.Exp, scale=-1.0 / 0.1)
                        a = act.activation(tb(5), tb(2), ACT.Exp, scale=-1.0 / 0.3)
                    a.then_inc(L.r_act, 1)
                L.turns_used = turns

            @property
            def route_steps(self):
                return dict(L0=22, L1=19, L3=36)[self.name]

        def G_run(first, local, b):
            return G[:, :, :, :].rearrange("p s c t -> p c s t")[:, :, DSZ(local + first, 1), DSZ(b * T, T)].rearrange("p c s t -> p c (s t)")

        cd_w = sem("cd_w")
        mixer_tanh = sem("mixer_tanh")
        mixer_gated = sem("mixer_gated")
        mixer_mm = sem("mixer_mm")
        mixer_sig = sem("mixer_sig")
        mixer_step = sem("mixer_step")
        mixer_x = sem("mixer_x")
        C_B, D_B, LOG_DELTA, DECAY, AB = (slice(KC * i, KC * i + KC) for i in range(5))

        def mixer_pe(pe):
            pe.wait_ge(cd_w, 16)
            for half in range(2):
                tok = slice(half * HALF, half * HALF + HALF)
                pe.wait_ge(mixer_gated, half + 1)
                for m in range(KC):
                    for col, first in ((C, 4), (0, 0)):
                        for kc in range(KC):
                            mm = pe.matmul(bank[first + 2 * m + half][:, :], w_attn[:, kc, col + m * P:col + m * P + P],
                                           h[:, kc, tok], start=(kc == 0), stop=(kc == KC - 1))
                        mm.then_inc(mixer_mm, 1)

        def mixer_act(act):
            act.wait_ge(F1.x_done, 8)
            for half in range(2):
                tok = slice(half * HALF, half * HALF + HALF)
                act.activation(h[:, :, tok], x[:, :, tok], ACT.Tanh, scale=0.5).then_inc(mixer_tanh, 1)
            act.activation(scan_c[:, DECAY], scan_c[:, LOG_DELTA], ACT.Sigmoid, scale=-1.0).then_inc(mixer_sig, 1)
            for half in range(2):
                for m in range(KC):
                    act.wait_ge(mixer_mm, 4 * half + 2 * m + 1)
                    act.activation(c_rows[:, m, half * HALF:half * HALF + HALF], bank[4 + 2 * m + half][:, :], ACT.Sigmoid,
                                   bias=scan_c[:, D_B][:, m:m + 1]).then_inc(mixer_sig, 1)

        def mixer_dve(dve):
            dve.tensor_tensor(ab_in[:, 0, :, :], ab_in[:, 0, :, :], ab_in[:, 1, :, :], ALU.mult).then_inc(mixer_step, 1)
            dve.wait_ge(mixer_step, 1)
            dve.tensor_reduce(scan_c[:, AB], ab_in[:, 0, :, :], AX.X, ALU.add).then_inc(mixer_step, 1)
            for half in range(2):
                tok = slice(half * HALF, half * HALF + HALF)
                dve.wait_ge(mixer_tanh, half + 1)
                dve.scalar_tensor_tensor(out=h[:, :, tok], in0=h[:, :, tok], scalar=1.0, in1=G[:, G_SLOT[4], :, tok],
                                         op0=ALU.add, op1=ALU.mult).then_inc(mixer_gated, 1)
            for half in range(2):
                tok = slice(half * HALF, half * HALF + HALF)
                for m in range(KC):
                    dve.wait_ge(mixer_mm, 4 * half + 2 * m + 2)
                    dve.wait_ge(mixer_sig, 2 * half + m + 2)
                    dve.scalar_tensor_tensor(out=c_rows[:, m, tok], in0=bank[2 * m + half][:, :], scalar=scan_c[:, C_B][:, m:m + 1],
                                             in1=c_rows[:, m, tok], op0=ALU.add, op1=ALU.mult).then_inc(mixer_step, 1)
                dve.wait_ge(mixer_step, 2 + 6 * half + 2)
                for b in (2 * half, 2 * half + 1):
                    for m in range(KC):
                        dve.tensor_tensor_scan(h[:, m, b * T:b * T + T], scan_c[:, DECAY][:, m:m + 1].to_broadcast([P, T]),
                                               c_rows[:, m, b * T:b * T + T], 0.0, ALU.mult, ALU.add).then_inc(mixer_step, 1)
                dve.wait_ge(mixer_step, 2 + 6 * half + 6)
                for b in (2 * half, 2 * half + 1):
                    for m in range(KC):
                        xs = x[:, m, b * T:b * T + T]
                        dve.scalar_tensor_tensor(out=xs, in0=h[:, m, b * T:b * T + T], scalar=scan_c[:, AB][:, m:m + 1], in1=xs,
                                                 op0=ALU.mult, op1=ALU.add).then_inc(mixer_x, 1)

        ln_in = sem("ln_in")
        bit_tanh = sem("bit_tanh")
        bit_gated = sem("bit_gated")
        bit_turned = sem("bit_turned")
        bit_step = sem("bit_step")
        bit_q = sem("bit_q")
        bit_q_turned = sem("bit_q_turned")
        bit_q_copied = sem("bit_q_copied")
        bit_gate = sem("bit_gate")
        bit_up = sem("bit_up")
        bit_silu = sem("bit_silu")
        bit_mid = sem("bit_mid")
        bit_sq = sem("bit_sq")
        bit_var = sem("bit_var")
        bit_rstd = sem("bit_rstd")
        bit_norm = sem("bit_norm")
        bit_q2 = sem("bit_q2")
        bit_q2_turned = sem("bit_q2_turned")
        bit_q2_copied = sem("bit_q2_copied")
        bit_down = sem("bit_down")
        bit_scaled = sem("bit_scaled")
        bit_back = sem("bit_back")
        bit_x = sem("bit_x")
        AMAX, INV, DQ, DQ_G, DQ_U, SQ, VAR, RSTD, AMAX2, AMAX2C, INV2, Q2, DQ2 = range(13)

        def tile_loop(eng, body):
            with eng.Fori(0, 2) as g:
                with eng.Fori(0, B) as b:
                    body(g * 4 + b, g, b)

        def bit_pe(pe):
            for tt in range(TILES):
                pe.wait_ge(bit_gated, tt // 4 + 1)
                for kc in range(KC):
                    mm = pe.transpose(bank[tt // 2][:, (tt % 2) * C + kc * P:(tt % 2) * C + kc * P + P],
                                      h[:, kc, tt * P:tt * P + P], ident[:, :])
                if tt % 2:
                    mm.then_inc(bit_turned, 1)
            for half in range(2):
                pe.wait_ge(bit_q, half + 1)
                for kc in range(KC):
                    for i in range(4):
                        mm = pe.transpose(bank[4 + half][:, :].bitcast(BF16)[:, kc * HALF + i * P:kc * HALF + i * P + P],
                                          hq_bf[:, half * 4 + i, kc * P:kc * P + P], ident_bf[:, :])
                mm.then_inc(bit_q_turned, 1)
            pe.wait_ge(bit_q_copied, 2)
            pe.wait_ge(wq_done, 3)

            def tile(t, g, b):
                for n, w, done in ((0, wq_g, bit_gate), (1, wq_u, bit_up)):
                    for half in range(2):
                        for kc in range(KC):
                            mm = pe.matmul(bank[2 * n + half][:, :], hq_t[:, kc, DSZ(t * P, P)], w[:, kc, half * 512:half * 512 + 512],
                                           start=(kc == 0), stop=(kc == KC - 1))
                        mm.then_inc(done, 1)
                pe.wait_ge(bit_q2, t + 1)
                for ch in range(L2I // P):
                    mm = pe.transpose(bank[4][:, :].bitcast(BF16)[:, ch * P:ch * P + P], h2_bf[:, ch * P:ch * P + P], ident_bf[:, :])
                mm.then_inc(bit_q2_turned, 1)
                pe.wait_ge(bit_q2_copied, t + 1)
                for ch in range(L2I // P):
                    mm = pe.matmul(bank[5][:, 0:C], h2_t[:, ch, :], wq_d[:, ch, :], start=(ch == 0), stop=(ch == L2I // P - 1))
                mm.then_inc(bit_down, 1)
                pe.wait_ge(bit_scaled, t + 1)
                for m in range(KC):
                    mm = pe.transpose(bank[6][:, m * P:m * P + P], y_sb[:, m * P:m * P + P], ident[:, :])
                mm.then_inc(bit_back, 1)
            tile_loop(pe, tile)

        def bit_act(act):
            for half in range(2):
                tok = slice(half * HALF, half * HALF + HALF)
                act.wait_ge(mixer_x, 8)
                act.activation(h[:, :, tok], x[:, :, tok], ACT.Tanh, scale=0.5).then_inc(bit_tanh, 1)
            for half in range(2):
                act.wait_ge(bit_q_turned, half + 1)
                act.activation(hq_t[:, :, half * HALF:half * HALF + HALF],
                               bank[4 + half][:, :].bitcast(BF16).rearrange("p (k t) -> p k t", k=KC), ACT.Copy).then_inc(bit_q_copied, 1)

            def tile(t, g, b):
                act.wait_ge(bit_gate, t * 2 + 2)
                act.wait_ge(bit_q_copied, 2)
                for half in range(2):
                    act.activation(act_s[:, half, :], bank[half][:, :], ACT.Silu, scale=bstat[:, DQ_G, DSZ(t, 1)]).then_inc(bit_silu, 1)
                act.wait_ge(bit_mid, t * 2 + 2)
                act.wait_ge(bit_q_copied, 2)
                act.activation(act_a[:, :, :], act_m[:, :, :], ACT.Square, accum_out=bstat[:, SQ, DSZ(t, 1)]).then_inc(bit_sq, 1)
                gate_act(act, g + 6, b)
                act.wait_ge(bit_q2_turned, t + 1)
                act.activation(h2_t[:, :, :].rearrange("p a b -> p (a b)"), bank[4][:, :].bitcast(BF16), ACT.Copy).then_inc(bit_q2_copied, 1)
                act.wait_ge(bit_down, t + 1)
                act.wait_ge(bit_q_copied, 2)
                act.activation(y_sb[:, :], bank[5][:, 0:C], ACT.Identity, scale=bstat[:, DQ2, DSZ(t, 1)]).then_inc(bit_scaled, 1)
            tile_loop(act, tile)

        def bit_pool(pool):
            def tile(t, g, b):
                gate_pool(pool, g + 6, b)
                pool.wait_ge(bit_var, t + 1)
                pool.tensor_tensor(bstat[:, RSTD, DSZ(t, 1)], bstat[:, VAR, DSZ(t, 1)], half_c[:, 0:1], ALU.pow).then_inc(bit_rstd, 1)
            tile_loop(pool, tile)

        def bit_dve(dve):
            for half in range(2):
                tok = slice(half * HALF, half * HALF + HALF)
                dve.wait_ge(bit_tanh, half + 1)
                dve.scalar_tensor_tensor(out=h[:, :, tok], in0=h[:, :, tok], scalar=1.0, in1=G[:, G_SLOT[5], :, tok],
                                         op0=ALU.add, op1=ALU.mult).then_inc(bit_gated, 1)
            for pair in range(4):
                dve.wait_ge(bit_turned, pair + 1)
                dve.tensor_reduce(bstat[:, AMAX, 2 * pair:2 * pair + 2], bank[pair][:, :].rearrange("p (a c) -> p a c", a=2),
                                  AX.X, ALU.max, apply_absolute_value=True).then_inc(bit_step, 1)
            dve.wait_ge(bit_step, 4)
            dve.tensor_scalar(bstat[:, AMAX, :], bstat[:, AMAX, :], 1e-5, None, ALU.max).then_inc(bit_step, 1)
            dve.wait_ge(bit_step, 5)
            dve.reciprocal(bstat[:, INV, :], bstat[:, AMAX, :]).then_inc(bit_step, 1)
            dve.tensor_scalar(bstat[:, DQ_G, :], bstat[:, AMAX, :], wq_stat[:, 0, 1:2], 1.0 / 127.0, ALU.mult, ALU.mult).then_inc(bit_step, 1)
            dve.tensor_scalar(bstat[:, DQ_U, :], bstat[:, AMAX, :], wq_stat[:, 1, 1:2], 1.0 / 127.0, ALU.mult, ALU.mult).then_inc(bit_step, 1)
            dve.wait_ge(bit_step, 6)
            dve.tensor_scalar(bstat[:, INV, :], bstat[:, INV, :], 127.0, None, ALU.mult).then_inc(bit_step, 1)
            dve.wait_ge(bit_step, 9)
            for half, buf in enumerate((act_s, act_m)):
                flat = buf[:, :, :].rearrange("p a b -> p (a b)")
                for i in range(4):
                    tt = half * 4 + i
                    dve.tensor_scalar(flat[:, i * C:i * C + C], bank[tt // 2][:, (tt % 2) * C:(tt % 2) * C + C],
                                      bstat[:, INV, tt:tt + 1], MAGIC, ALU.mult, ALU.add).then_inc(bit_step, 1)
                dve.wait_ge(bit_step, 9 + 4 * half + 4)
                dve.tensor_scalar(hq_bf[:, half * 4:half * 4 + 4, :].rearrange("p a b -> p (a b)"), flat, -MAGIC, 127.0,
                                  ALU.add, ALU.min).then_inc(bit_q, 1)

            dve.wait_ge(ln_in, 16)
            mid = act_m[:, :, :].rearrange("p a b -> p (a b)")
            scaled = act_s[:, :, :].rearrange("p a b -> p (a b)")

            def tile(t, g, b):
                st = lambda i: bstat[:, i, DSZ(t, 1)]
                for half in range(2):
                    dve.wait_ge(bit_silu, t * 2 + half + 1)
                    dve.wait_ge(bit_up, t * 2 + half + 1)
                    dve.scalar_tensor_tensor(out=act_m[:, half, :], in0=bank[2 + half][:, :], scalar=st(DQ_U), in1=act_s[:, half, :],
                                             op0=ALU.mult, op1=ALU.mult).then_inc(bit_mid, 1)
                dve.wait_ge(bit_mid, t * 2 + 2)
                dve.tensor_tensor(scaled, mid, ln_bc, ALU.mult).then_inc(bit_norm, 1)
                dve.wait_ge(bit_sq, t + 1)
                dve.tensor_scalar(st(VAR), st(SQ), 1.0 / L2I, 1e-6, ALU.mult, ALU.add).then_inc(bit_var, 1)
                dve.wait_ge(bit_norm, t * 7 + 1)
                dve.tensor_reduce(st(AMAX2), scaled, AX.X, ALU.max, apply_absolute_value=True).then_inc(bit_norm, 1)
                gate_dve(dve, 0, g + 6, b)
                dve.wait_ge(bit_rstd, t + 1)
                dve.wait_ge(bit_norm, t * 7 + 2)
                dve.tensor_scalar(st(AMAX2C), st(AMAX2), st(RSTD), 1e-5, ALU.mult, ALU.max).then_inc(bit_norm, 1)
                dve.wait_ge(bit_norm, t * 7 + 3)
                dve.reciprocal(st(INV2), st(AMAX2C)).then_inc(bit_norm, 1)
                dve.tensor_scalar(st(DQ2), st(AMAX2C), wq_stat[:, 2, 1:2], 1.0 / 127.0, ALU.mult, ALU.mult).then_inc(bit_norm, 1)
                dve.wait_ge(bit_norm, t * 7 + 4)
                dve.tensor_scalar(st(Q2), st(INV2), st(RSTD), 127.0, ALU.mult, ALU.mult).then_inc(bit_norm, 1)
                dve.wait_ge(bit_norm, t * 7 + 6)
                dve.tensor_scalar(mid, scaled, st(Q2), MAGIC, ALU.mult, ALU.add).then_inc(bit_norm, 1)
                dve.wait_ge(bit_norm, t * 7 + 7)
                dve.tensor_scalar(h2_bf[:, :], mid, -MAGIC, 127.0, ALU.add, ALU.min).then_inc(bit_q2, 1)
                for part in range(1, 5):
                    gate_dve(dve, part, g + 6, b)
                dve.wait_ge(bit_back, t + 1)
                xs = x[:, :, DSZ(t * P, P)]
                dve.tensor_tensor(xs, bank[6][:, 0:C].rearrange("p (m t) -> p m t", m=KC), xs, ALU.add).then_inc(bit_x, 1)
                s = (g + 6) * 4 + b
                dve.wait_ge(wkv_inv, s + 1)
                dve.scalar_tensor_tensor(out=G_run(G_SLOT[6], g, b), in0=wkv_num[:, :, :], scalar=gscale[:, DSZ(b, 1)],
                                         in1=wkv_rec[:, :, :], op0=ALU.mult, op1=ALU.mult).then_inc(g_done, 1)
            tile_loop(dve, tile)

        ROPE4 = [2, 3, 0, 1] + list(range(4, 32))
        ROPE32 = list(range(16, 32)) + list(range(16))
        A0 = Attention("L0", 0, 1, True, 1.0, False, (ROPE4, 0), True, 2 * GROUPS, 16, 16, False, x_in, 16, 0, sem("rope_step_0"))
        F0 = Experts("L0", 1, 25, 16, 11, [2, 3, 4], A0.x_done, 4, 0,
                     lambda c: io["L0_w"][c] if c < 2 else (io["L0_w"],), None, 0)
        A1 = Attention("L1", 2, 5, False, 0.25, False, None, False, 2 * GROUPS + KC, 16, 16, True, F0.x_done, 4, 4, None)
        F1 = Experts("L1", 3, 11, 8, 11, [], A1.x_done, 8, 1,
                     lambda c: io["L1_w"][c] if c < 2 else (io["L1_w"],), F0, 1)
        A3 = Attention("L3", 6, None, True, 1.0, True, (ROPE32, 2), False, None, 32, 8, False, bit_x, TILES, 8, sem("rope_step_3"))
        F3 = Experts("L3", 7, 16, 8, 16, [], A3.x_done, 12, 2,
                     lambda c: lora_dram[c] if c < 4 else (io["L3_w"],), F1, 2)
        out_done = sem("out_done")

        block = ctx.enter_context(nc.Block())

        @block.sync
        def _(sp):
            setup_sp(sp)
            sp.wait_ge(lora_out, 64)
            F0.prefetch_sp(sp)
            sp.wait_ge(A0.out, B)
            sp.dma_start(w_attn[:, :, :], io["L1_w_attn"]).then_inc(attn_w["L1"], 16)
            sp.dma_start(w_out[:, 0:KC, :], io["L1_w_out"]).then_inc(attn_w["L1"], 16)
            F0.sp(sp)
            F1.prefetch_sp(sp)
            sp.wait_ge(A1.out, 2 * B)
            sp.dma_start(w_attn[:, :, 0:2 * C], io["L2_cd"]).then_inc(cd_w, 16)
            sp.dma_start(ln_bc, io["L2_ln"].unsqueeze(0).to_broadcast([P, L2I])).then_inc(ln_in, 16)
            F1.sp(sp)
            F3.prefetch_sp(sp)
            sp.wait_ge(mixer_mm, 8)
            sp.dma_start(w_attn[:, :, :], io["L3_w_attn"]).then_inc(attn_w["L3"], 16)
            sp.dma_start(w_out[:, :, :], io["L3_w_out"]).then_inc(attn_w["L3"], 16)
            F3.sp(sp)
            sp.wait_ge(F3.x_done, 12)
            sp.dma_start(out, x[:, :, :]).then_inc(out_done, 16)
            sp.wait_ge(out_done, 16)

        @block.scalar
        def _(act):
            setup_act(act)
            A0.act(act)
            F0.act(act)
            A1.act(act)
            F1.act(act)
            mixer_act(act)
            bit_act(act)
            A3.act(act)
            F3.act(act)

        @block.vector
        def _(dve):
            setup_dve(dve)
            A0.dve(dve)
            F0.dve(dve)
            A1.dve(dve)
            F1.dve(dve)
            mixer_dve(dve)
            bit_dve(dve)
            A3.dve(dve)
            F3.dve(dve)

        @block.tensor
        def _(pe):
            setup_pe(pe)
            A0.pe(pe)
            F0.pe(pe)
            A1.pe(pe)
            F1.pe(pe)
            mixer_pe(pe)
            bit_pe(pe)
            A3.pe(pe)
            F3.pe(pe)

        @block.gpsimd
        def _(pool):
            setup_pool(pool)
            F0.pool(pool)
            with pool.Fori(0, B) as b:
                gate_pool(pool, A1.next_gate, b)
            F1.pool(pool)
            bit_pool(pool)
            F3.pool(pool)


def halves(w):
    return w.reshape(-1, P, w.shape[-1]).transpose(1, 0, 2)


def padded_heads(w):
    full = np.zeros((w.shape[0], HEADS, SLOT), w.dtype)
    full[:, :, :w.shape[2]] = w
    return full.reshape(w.shape[0], HEADS * SLOT)


def expert_chunks(gate, up, down):
    rows = gate.shape[0]
    chunks = -(-rows // P)
    out = np.zeros((chunks + 1, P, 768), gate.dtype)
    for n, w in enumerate((gate, up)):
        full = np.zeros((chunks * P, C), w.dtype)
        full[:rows] = w
        out[:chunks, :, n * 256:n * 256 + 256] = full.reshape(chunks, P, KC, P).transpose(0, 3, 2, 1).reshape(chunks, P, 256)
    full = np.zeros((chunks * P, C), down.dtype)
    full[:rows] = down
    out[:chunks, :, 512:] = full.reshape(chunks, P, C)
    return out


def rope_tables():
    tab = np.zeros((SLOT, 4, T), np.float32)
    tab[:, 0] = 1.0
    for first, dims in ((0, 4), (2, 32)):
        freq = (1.0 / np.float32(10000.0) ** (np.arange(0, dims, 2, dtype=np.float32) / np.float32(dims))).astype(np.float32)
        angle = (np.arange(T, dtype=np.float32)[None, :] * freq[:, None]).astype(np.float32)
        half = dims // 2
        tab[0:half, first], tab[half:dims, first] = np.cos(angle), np.cos(angle)
        tab[0:half, first + 1], tab[half:dims, first + 1] = -np.sin(angle), np.sin(angle)
    return np.tile(tab, (P // SLOT, 1, 1))


def kernel(**inputs):
    import concourse.bacc as bacc
    from concourse.bass_utils import run_bass_kernel_spmd

    v = {name: np.asarray(a) for name, a in inputs.items()}
    f32 = np.float32
    arrays = {}
    arrays["x"] = halves(v["x"].reshape(N, C).T)
    arrays["side"] = halves(v["fside_BxSxS_0"].reshape(N, C).T)
    arrays["cond"] = v["cond_512"]
    gates = [f"L{l}_{c}" for l in range(4) for c in ("cond", "cond2")]
    wu = np.stack([np.stack([v[f"{g}_{k}"] for g in gates], -1) for k in "wu"])
    arrays["wu"] = wu.reshape(2, KC, P, CONDS).transpose(2, 0, 1, 3)

    qkv0 = v["L0_attn_w_qkv"].reshape(C, HEADS, 3, 16)
    qkv1 = v["L1_attn_Wqkv"].T.reshape(C, HEADS, 3, 16)
    for name, qkv in (("L0", qkv0), ("L1", qkv1)):
        arrays[f"{name}_w_attn"] = halves(np.concatenate(
            [padded_heads(qkv[:, :, 0]), padded_heads(qkv[:, :, 1]), qkv[:, :, 2].reshape(C, C)], 1))
    wk = np.repeat(v["L3_attn_Wk"].reshape(C, 8, 32), 2, axis=1).reshape(C, 512)
    arrays["L3_w_attn"] = halves(np.concatenate([v["L3_attn_Wq"], wk, v["L3_attn_Wv"]], 1))
    arrays["L0_w_out"] = halves(v["L0_attn_w_out"])
    arrays["L1_w_out"] = halves(v["L1_attn_Wproj"].T)
    arrays["L3_w_out"] = halves(v["L3_attn_Wo"])
    b0 = v["L0_attn_b_qkv"].reshape(1, HEADS, 3, 16)
    arrays["attn_bias"] = np.concatenate(
        [padded_heads(b0[:, :, 0]).reshape(GROUPS, P).T, padded_heads(b0[:, :, 1]).reshape(GROUPS, P).T,
         v["L0_attn_b_out"].reshape(KC, P).T, v["L1_attn_bproj"].reshape(KC, P).T], 1)
    arrays["L0_bias_v"] = b0[0, :, 2].reshape(C)
    arrays["rope"] = rope_tables()
    arrays["earlier"] = np.tile(np.tril(np.ones((16, 16), f32), -1)[None], (P, 1, 1))
    route = np.zeros((P, 3, KC, 16), f32)
    route[:, 0] = halves(v["L0_ffn_gate_w"].T)
    route[:, 1, :, 0:8] = halves(v["L1_ffn_router_w"].T)
    route[:, 2, :, 0:8] = halves(v["L3_ffn_Wr"])
    arrays["w_route"] = route
    arrays["temp"] = v["L3_ffn_temperature"].reshape(1)
    arrays["scan_c"] = np.concatenate([v[f"L2_attn_{n}"].reshape(KC, P).T for n in ("C_b", "D_b", "log_delta")], 1)
    arrays["scan_ab"] = np.stack([halves(v["L2_attn_A"]), halves(v["L2_attn_B"])], 1)
    arrays["L2_cd"] = np.concatenate([halves(v["L2_attn_C_w"].T), halves(v["L2_attn_D_w"].T)], 2)
    arrays["L2_ln"] = v["L2_ffn_ln_weight"]
    arrays["L2_w_gate"] = halves(v["L2_ffn_w_gate"].T)
    arrays["L2_w_up"] = halves(v["L2_ffn_w_up"].T)
    arrays["L2_w_down"] = halves(v["L2_ffn_w_down"].T).reshape(P, KC, L2I)

    half = 176
    w13, sw13 = v["L0_ffn_w13"], v["L0_ffn_sw13"]
    arrays["L0_w"] = expert_chunks(
        np.concatenate([w13[:, :half].reshape(-1, C), sw13[:2 * half]]),
        np.concatenate([w13[:, half:].reshape(-1, C), sw13[2 * half:]]),
        np.concatenate([v["L0_ffn_w2"].transpose(0, 2, 1).reshape(-1, C), v["L0_ffn_sw2"].T]))
    arrays["L1_w"] = expert_chunks(v["L1_ffn_gate_w"].reshape(-1, C), v["L1_ffn_up_w"].reshape(-1, C),
                                   v["L1_ffn_down_w"].transpose(0, 2, 1).reshape(-1, C))
    arrays["L3_w"] = expert_chunks(v["L3_ffn_Wg"].transpose(0, 2, 1).reshape(-1, C),
                                   v["L3_ffn_Wu"].transpose(0, 2, 1).reshape(-1, C), v["L3_ffn_Wd"].reshape(-1, C))
    arrays["lora"] = np.concatenate(
        [v["L3_ffn_Ga"].transpose(0, 2, 1), v["L3_ffn_Gb"], v["L3_ffn_Ua"].transpose(0, 2, 1), v["L3_ffn_Ub"],
         v["L3_ffn_Da"].transpose(0, 2, 1), v["L3_ffn_Db"]], 2).reshape(2, 64, 2, 768)
    arrays = {name: np.ascontiguousarray(a) for name, a in arrays.items()}

    nc = bacc.Bacc("TRN2", target_bir_lowering=False, num_devices=1)
    io = {name: nc.dram_tensor(f"in_{name}", a.shape, mybir.dt.from_np(a.dtype), kind="ExternalInput").ap() for name, a in arrays.items()}
    out = nc.dram_tensor("out", (P, KC, N), F32, kind="ExternalOutput").ap()
    build(nc, io, out)
    r = run_bass_kernel_spmd(nc, [{f"in_{name}": a for name, a in arrays.items()}], core_ids=[0])
    y = r.results[0]["out"]
    return np.ascontiguousarray(y.transpose(1, 0, 2).reshape(C, N).T.reshape(B, T, C))
```

```python
from contextlib import ExitStack

import numpy as np

import concourse.bass as bass
from concourse import mybir

F32 = mybir.dt.float32
F32R = mybir.dt.float32r
BF16 = mybir.dt.bfloat16
ALU = mybir.AluOpType
ACT = mybir.ActivationFunctionType
AX = mybir.AxisListType

P = 128
B, T, C = 4, 256, 256
N = B * T
KC = C // P
HALF = N // 2
HEADS, SLOT = 16, 32
GROUPS = HEADS * SLOT // P
CONDS = 8
EXPERT_ROWS = 16
GRANULES = P // EXPERT_ROWS
E30 = float(np.exp(np.float32(30.0)))
MAGIC = float(1.5 * 2 ** 23)
DEEP = 4
NEG = -1.0e30
CAP = 50.0
L2I = 1024
TILES = N // P

ATTN_COLS = 2 * GROUPS * P + C
G_SLOT = (0, 3, 1, 0, 2, 3, 1, 2)
G_READY = (4, 12, 12, 16, 24, 24, 28, 32)
DSZ = bass.ds


def build(nc, io, out):
    ctx = ExitStack()
    with ctx:
        def sb(name, shape, dt=F32):
            return ctx.enter_context(nc.sbuf_tensor(name, shape, dt))

        def sem(name):
            return ctx.enter_context(nc.semaphore(name))

        bank = [ctx.enter_context(nc.psum_tensor(f"bank{i}", [P, 512], F32)) for i in range(8)]

        score_bank = (bank[0], bank[1], bank[4], bank[5])

        x = sb("x", [P, KC, N])
        work = sb("work", [P, 4, N])
        h = work[:, 0:2, :]
        h_hi = sb("h_hi", [P, KC, N], F32R)
        h_lo = sb("h_lo", [P, KC, N], F32R)
        G = sb("G", [P, 4, KC, N])
        side = sb("side", [P, KC, N])
        ek = sb("ek", [P, KC, N])
        wkv_in = sb("wkv_in", [P, 2, KC, T])
        wu = sb("wu", [P, 2, KC, CONDS])
        cond_bc = sb("cond_bc", [P, B, 64])
        tf4 = sb("tf4", [P, 4, B])
        ew = sb("ew", [P, 2, KC * CONDS])
        decay = sb("decay", [P, KC, CONDS * B])
        gscale = sb("gscale", [P, B])
        scan_f = sb("scan_f", [P, 2, KC, T])
        scan_b = sb("scan_b", [P, 2, KC, T])
        euk = sb("euk", [P, KC, T])
        wkv_num = sb("wkv_num", [P, KC, T])
        wkv_rec = euk
        ident = sb("ident", [P, P])
        ident_bf = sb("ident_bf", [P, P], BF16)
        negmask = sb("negmask", [P, P], BF16)
        capmask = sb("capmask", [P, P])
        zeros_bf = sb("zeros_bf", [P, 512], BF16)
        ones = sb("ones", [P, P])
        earlier = sb("earlier", [P, 16, 16])
        rope = sb("rope", [P, 4, T])
        w_attn = sb("w_attn", [P, KC, ATTN_COLS])
        w_out = sb("w_out", [P, 4, C])
        bias_attn = sb("bias_attn", [P, 8 + KC + KC])
        bias_v = sb("bias_v", [P, C])
        hb = sb("hb", [P, KC, T])
        q_head = sb("q_head", [P, 2, 2, T])
        head_mask = sb("head_mask", [P, 4])
        v_sb = sb("v_sb", [P, 2, HEADS * SLOT])
        probs = sb("probs", [P, DEEP, 512])
        probs_t = sb("probs_t", [P, 2, 512])
        row_max = sb("row_max", [P, 2 * HEADS])
        row_sum = sb("row_sum", [P, 2 * HEADS])
        row_inv = sb("row_inv", [P, 2 * HEADS])
        attn_t = sb("attn_t", [P, 4, T])
        w_raw = sb("w_raw", [P, 2, 768])
        w_gu_hi = sb("w_gu_hi", [P, 2, 512], F32R)
        w_gu_lo = sb("w_gu_lo", [P, 2, 512], F32R)
        w_d_hi = sb("w_d_hi", [P, 2, 256], F32R)
        w_d_lo = sb("w_d_lo", [P, 2, 256], F32R)
        c_rows = sb("c_rows", [P, 2, N])
        act_s = sb("act_s", [P, 2, 512])
        act_m = work[:, 2, :].rearrange("p (h t) -> p h t", h=2)
        act_a = work[:, 3, :].rearrange("p (h t) -> p h t", h=2)
        act_hi = sb("act_hi", [P, 2, 512], F32R)
        act_lo = sb("act_lo", [P, 2, 512], F32R)
        w_route = sb("w_route", [P, 3, KC, 16])
        route_s = sb("route_s", [P, 6, TILES])
        temp = sb("temp", [P, 2])
        scan_c = sb("scan_c", [P, 4 * KC + 2 * KC])
        ab_in = sb("ab_in", [P, 2, KC, 64])
        wq_g = sb("wq_g", [P, KC, L2I], BF16)
        wq_u = sb("wq_u", [P, KC, L2I], BF16)
        wq_d = sb("wq_d", [P, L2I // P, C], BF16)
        wq_stat = sb("wq_stat", [P, 3, 4])
        bstat = sb("bstat", [P, 13, TILES])
        half_c = sb("half_c", [P, 2])
        route = q_head[:, :, :, :].rearrange("p a b t -> p (a b t)")[:, 0:7 * TILES * 16].rearrange("p (i c) -> p i c", i=7)
        qk = c_rows[:, :, :].rearrange("p a (b t) -> p (a b) t", t=T)
        rope_a = act_s[:, 0, :].rearrange("p (g t) -> p g t", g=2)
        rope_b = act_s[:, 1, :].rearrange("p (g t) -> p g t", g=2)
        c_t = act_a[0:16, :, :].rearrange("p a b -> p (a b)")
        ln_bc = attn_t[:, :, :].rearrange("p a b -> p (a b)")
        hq_bf = probs[:, 0:2, :].rearrange("p a b -> p (a b)").bitcast(BF16).rearrange("p (t c) -> p t c", c=C)
        hq_t = probs_t[:, :, :].rearrange("p a b -> p (a b)").bitcast(BF16).rearrange("p (k t) -> p k t", k=KC)
        h2_bf = probs[:, 2, :].bitcast(BF16)
        h2_t = probs[:, 3, :].bitcast(BF16).rearrange("p (c t) -> p c t", t=P)
        y_sb = v_sb[:, 0, 0:C]
        ctx_all = work

        c_dram = {l: nc.dram_tensor(f"c_granules_{l}", (g, N), F32).ap() for l, g in (("L0", 200), ("L1", 88), ("L3", 128))}
        lora_dram = nc.dram_tensor("lora_chunks", (4, P, 768), F32).ap()

        side_in = sem("side_in")
        cond_in = sem("cond_in")
        x_in = sem("x_in")
        wkv_put = sem("wkv_put")
        scan_done = sem("scan_done")
        euk_done = sem("euk_done")
        wkv_step = sem("wkv_step")
        wkv_inv = sem("wkv_inv")
        g_done = sem("g_done")
        setup_v = sem("setup_v")
        setup_a = sem("setup_a")
        const_p = sem("const_p")

        def gate_dve(dve, part, n, b, o, euk_of=None):
            e = euk[:, :, :] if euk_of is None else euk_of[:, :, DSZ(b * T, T)]
            tok = DSZ(b * T, T)
            if part in (0, 1):
                ch = part
                if part == 0:
                    dve.wait_ge(g_done, o + 1)
                    dve.wait_ge(wkv_put, o + 1)
                d = decay[:, ch, DSZ(n * B + b, 1)]
                for i in range(2):
                    dve.tensor_tensor_scan(scan_f[:, i, ch, :], d.to_broadcast([P, T]), wkv_in[:, i, ch, :], 0.0,
                                           ALU.mult, ALU.add)
                    last = dve.tensor_tensor_scan(scan_b[:, i, ch, 0:T - 1][:, ::-1],
                                                  wkv_in[:, i, ch, 1:T][:, ::-1],
                                                  d.to_broadcast([P, T - 1]), 0.0, ALU.add, ALU.mult)
                if part == 1:
                    last.then_inc(scan_done, 1)
            if part == 2:
                dve.wait_ge(scan_done, o + 2)
                dve.tensor_tensor(scan_f[:, :, :, :], scan_f[:, :, :, :], scan_b[:, :, :, :], ALU.add).then_inc(wkv_step, 1)
                dve.wait_ge(euk_done, o + 1)
                dve.scalar_tensor_tensor(out=wkv_num[:, :, :], in0=e, scalar=E30, in1=side[:, :, tok],
                                         op0=ALU.min, op1=ALU.mult).then_inc(wkv_step, 1)
            if part == 3:
                dve.wait_ge(wkv_step, o * 5 + 2)
                dve.scalar_tensor_tensor(out=scan_f[:, 1, :, :], in0=e, scalar=E30, in1=scan_f[:, 1, :, :],
                                         op0=ALU.min, op1=ALU.add).then_inc(wkv_step, 1)
                dve.tensor_tensor(wkv_num[:, :, :], wkv_num[:, :, :], scan_f[:, 0, :, :], ALU.add).then_inc(wkv_step, 1)
            if part == 4:
                dve.wait_ge(wkv_step, o * 5 + 3)
                dve.tensor_scalar(scan_f[:, 1, :, :], scan_f[:, 1, :, :], 1e-8, None, ALU.max).then_inc(wkv_step, 1)
                dve.wait_ge(wkv_step, o * 5 + 5)
                dve.reciprocal(wkv_rec[:, 0, :], scan_f[:, 1, 0, :]).then_inc(wkv_inv, 1)
            if part == 5:
                dve.reciprocal(wkv_rec[:, 1, :], scan_f[:, 1, 1, :]).then_inc(wkv_inv, 1)

        def gate_finish(dve, n, b, o):
            dve.wait_ge(wkv_inv, 2 * o + 2)
            dve.scalar_tensor_tensor(out=G[:, G_SLOT[n], :, DSZ(b * T, T)], in0=wkv_num[:, :, :], scalar=gscale[:, DSZ(b, 1)],
                                     in1=wkv_rec[:, :, :], op0=ALU.mult, op1=ALU.mult).then_inc(g_done, 1)

        def gate_pool(pool, b, o, waited=False):
            tok = DSZ(b * T, T)
            if not waited:
                pool.wait_ge(side_in, 16)
                pool.wait_ge(scan_done, o + 1)
            pool.tensor_tensor(wkv_in[:, 0, :, :], ek[:, :, tok], side[:, :, tok], ALU.mult)
            pool.tensor_tensor(wkv_in[:, 1, :, :], ek[:, :, tok], ones[:, 0:1].unsqueeze(2).to_broadcast([P, KC, T]), ALU.mult).then_inc(wkv_put, 1)

        def gate_act(act, n, b, o, waited=False):
            if not waited:
                act.wait_ge(side_in, 16)
                act.wait_ge(scan_done, o + 2)
            for ch in range(KC):
                last = act.activation(euk[:, ch, :], side[:, ch, DSZ(b * T, T)], ACT.Exp, bias=wu[:, 1, ch, DSZ(n, 1)])
            last.then_inc(euk_done, 1)

        lora_in = sem("lora_in")
        lora_raw = [sem("lora_raw0"), sem("lora_raw1")]
        lora_mm = sem("lora_mm")
        lora_add = sem("lora_add")
        lora_out = sem("lora_out")
        ones_out = sem("ones_out")
        wq_in = [sem(f"wq_in{i}") for i in range(3)]
        wq_abs = sem("wq_abs")
        wq_sum = sem("wq_sum")
        wq_scale = sem("wq_scale")
        wq_step = sem("wq_step")
        wq_done = sem("wq_done")
        misc_in = sem("misc_in")
        lora_sb = G[0:64, 0, :, 0:768]
        wq_raw = (h[:, :, :], G[:, 1, :, :], G[:, 2, :, :])

        def setup_sp(sp):
            sp.dma_start(side[:, :, :], io["side"]).then_inc(side_in, 16)
            sp.dma_start(wu[:, :, :, :], io["wu"]).then_inc(cond_in, 16)
            sp.dma_start(cond_bc[:, :, :], io["cond"].unsqueeze(0).to_broadcast([P, B, 64])).then_inc(cond_in, 16)
            sp.dma_start(x[:, :, :], io["x"]).then_inc(x_in, 16)
            sp.dma_start(w_attn[:, :, :], io["L0_w_attn"]).then_inc(attn_w["L0"], 16)
            sp.dma_start(w_out[:, :, :], io["L0_w_out"]).then_inc(attn_w["L0"], 16)
            sp.dma_start(bias_attn[:, :], io["attn_bias"]).then_inc(misc_in, 16)
            sp.dma_start(bias_v[:, :], io["L0_bias_v"].unsqueeze(0).to_broadcast([P, C])).then_inc(misc_in, 16)
            sp.dma_start(rope[:, :, :], io["rope"]).then_inc(misc_in, 16)
            sp.dma_start(earlier[:, :, :], io["earlier"]).then_inc(misc_in, 16)
            sp.dma_start(w_route[:, :, :, :], io["w_route"]).then_inc(misc_in, 16)
            sp.dma_start(temp[:, 0:1], io["temp"].unsqueeze(0).to_broadcast([P, 1])).then_inc(misc_in, 16)
            sp.dma_start(scan_c[:, 0:3 * KC], io["scan_c"]).then_inc(misc_in, 16)
            sp.dma_start(ab_in[:, :, :, :], io["scan_ab"]).then_inc(misc_in, 16)
            for i, name in enumerate(("L2_w_gate", "L2_w_up", "L2_w_down")):
                sp.dma_start(wq_raw[i], io[name]).then_inc(wq_in[i], 16)
            sp.wait_ge(const_p, 3)
            sp.dma_start(c_dram["L0"][176:200, :].rearrange("g (a n) -> g a n", a=8), ones[0:24, :].unsqueeze(1).to_broadcast([24, 8, P])).then_inc(ones_out, 16)

        def lora_sp(sp, e):
            sp.dma_start(lora_sb, io["lora"][e]).then_inc(lora_in, 16)
            for f in range(2):
                sp.dma_start(w_raw[:, f, :], io["L3_w"][2 * e + f]).then_inc(lora_raw[f], 16)

        def lora_out_sp(sp, e):
            sp.wait_ge(lora_add, 10 * e + 10)
            for f in range(2):
                sp.dma_start(lora_dram[2 * e + f], w_raw[:, f, :]).then_inc(lora_out, 16)
            sp.wait_ge(lora_out, 32 * e + 32)

        def setup_pool(pool):
            pool.memset(ident[:, :], 0.0).then_inc(const_p, 1)
            pool.memset(ident_bf[:, :], 0.0).then_inc(const_p, 1)
            pool.memset(ones[:, :], 1.0).then_inc(const_p, 1)
            pool.memset(negmask[:, :], 0.0).then_inc(const_p, 1)
            pool.memset(capmask[:, :], 0.0).then_inc(const_p, 1)
            pool.memset(zeros_bf[:, :], 0.0).then_inc(const_p, 1)
            pool.memset(half_c[:, :], -0.5).then_inc(const_p, 1)
            pool.memset(head_mask[:, :], 0.0).then_inc(const_p, 1)
            pool.wait_ge(const_p, 8)
            for j in range(4):
                pool.memset(head_mask[SLOT * j:SLOT * j + SLOT, j:j + 1], 1.0).then_inc(const_p, 1)
            pool.wait_ge(const_p, 12)
            for m in (ident, ident_bf):
                pool.affine_select(out=m[:, :], in_=m[:, :], compare_op=ALU.not_equal, fill=1.0, base=0,
                                   pattern=[[-1, P]], channel_multiplier=1).then_inc(const_p, 1)
            for m, fill in ((negmask, NEG), (capmask, -1000.0)):
                pool.affine_select(out=m[:, :], in_=m[:, :], compare_op=ALU.is_ge, fill=fill, base=0,
                                   pattern=[[-1, P]], channel_multiplier=1).then_inc(const_p, 1)
            pool.wait_ge(side_in, 16)
            pool.wait_ge(setup_a, 4)
            with pool.Fori(0, B) as b:
                gate_pool(pool, b, b)
        def ternary_dve(dve, i, dst):
            raw = wq_raw[i].rearrange("p a b -> p (a b)")
            dve.wait_ge(wq_scale, 3 * i + 3)
            dve.tensor_scalar(raw, raw, wq_stat[:, i, 2:3], MAGIC, ALU.mult, ALU.add).then_inc(wq_step, 1)
            dve.wait_ge(wq_step, 2 * i + 1)
            dve.tensor_scalar(raw, raw, -MAGIC, 1.0, ALU.add, ALU.min).then_inc(wq_step, 1)
            dve.wait_ge(wq_step, 2 * i + 2)
            dve.tensor_scalar(dst[:, :, :].rearrange("p a b -> p (a b)"), raw, -1.0, None, ALU.max).then_inc(wq_done, 1)

        def setup_act(act):
            act.wait_ge(cond_in, 32)
            act.activation(ew[:, 0, :], wu[:, 0, :, :].rearrange("p c n -> p (c n)"), ACT.Exp).then_inc(setup_a, 1)
            act.wait_ge(setup_a, 1)
            act.activation(ew[:, 1, :], ew[:, 0, :], ACT.Exp, scale=-1.0).then_inc(setup_a, 1)
            act.wait_ge(setup_v, 1)
            act.activation(tf4[:, 1, :], tf4[:, 0, :], ACT.Tanh, scale=0.5).then_inc(setup_a, 1)
            act.wait_ge(setup_v, 2)
            act.activation(ek[:, :, :], ek[:, :, :], ACT.Exp).then_inc(setup_a, 1)
            with act.Fori(0, B) as b:
                gate_act(act, 0, b, b)

        def setup_dve(dve):
            dve.memset(scan_b[:, :, :, T - 1:T], 0.0).then_inc(g_done, 1)
            dve.memset(v_sb[:, :, :], 0.0).then_inc(scan_done, 1)
            dve.wait_ge(cond_in, 32)
            dve.tensor_reduce(tf4[:, 0, :], cond_bc[:, :, :], AX.X, ALU.add).then_inc(setup_v, 1)
            dve.wait_ge(side_in, 16)
            dve.tensor_scalar(ek[:, :, :], side[:, :, :], 30.0, None, ALU.min).then_inc(setup_v, 1)
            dve.wait_ge(setup_a, 3)
            dve.tensor_scalar(tf4[:, 2, :], tf4[:, 1, :], 0.25, 0.75, ALU.mult, ALU.add).then_inc(setup_v, 1)
            dve.tensor_scalar(gscale[:, :], tf4[:, 1, :], 0.05, 0.45, ALU.mult, ALU.add).then_inc(setup_v, 1)
            dve.wait_ge(setup_v, 4)
            dve.tensor_tensor(decay[:, :, :].rearrange("p c (n b) -> p (c n) b", b=B),
                              ew[:, 1, :].unsqueeze(2).to_broadcast([P, KC * CONDS, B]),
                              tf4[:, 2, :].unsqueeze(1).to_broadcast([P, KC * CONDS, B]), ALU.mult).then_inc(setup_v, 1)
            dve.wait_ge(setup_v, 5)
            with dve.Fori(0, B) as b:
                for part in range(6):
                    gate_dve(dve, part, 0, b, b)
                gate_finish(dve, 0, b, b)
            for i in range(3):
                dve.wait_ge(wq_in[i], 16)
                dve.tensor_reduce(wq_stat[:, i, 0:1], wq_raw[i].rearrange("p a b -> p (a b)"), AX.X, ALU.add,
                                  apply_absolute_value=True).then_inc(wq_abs, 1)
                dve.wait_ge(wq_sum, i + 1)
                dve.tensor_scalar(wq_stat[:, i, 1:2], bank[6][:, i:i + 1], 1.0 / (C * L2I), 1e-5, ALU.mult, ALU.max)\
                   .then_inc(wq_scale, 1)
                dve.wait_ge(wq_scale, 3 * i + 1)
                dve.reciprocal(wq_stat[:, i, 2:3], wq_stat[:, i, 1:2]).then_inc(wq_scale, 2)
                ternary_dve(dve, i, (wq_g, wq_u, wq_d)[i])

        def lora_dve(dve, e):
            for f in range(2):
                dve.wait_ge(lora_raw[f], 16 * (e + 1))
            dve.wait_ge(lora_mm, 6 * e + 6)
            for n in range(2 * KC):
                for f in range(2):
                    o = w_raw[:, f, n * P:n * P + P]
                    dve.tensor_tensor(o, lora_bank(n)[:, f * P:f * P + P], o, ALU.add).then_inc(lora_add, 1)
            for f in range(2):
                o = w_raw[:, f, 512:768]
                dve.tensor_tensor(o, lora_bank(4 + f), o, ALU.add).then_inc(lora_add, 1)

        def lora_pe(pe, e):
            pe.wait_ge(lora_in, 16 * (e + 1))
            if e:
                pe.wait_ge(mixer_step, 10)
            for n in range(2 * KC):
                a, b = (n // KC) * 2 * C, ((n // KC) * 2 + 1) * C
                pe.matmul(lora_bank(n), lora_at(a + n % KC * P, P), lora_at(b, C), start=True, stop=True).then_inc(lora_mm, 1)
            for f in range(2):
                pe.matmul(lora_bank(4 + f), lora_at(4 * C + f * P, P), lora_at(5 * C, C), start=True, stop=True).then_inc(lora_mm, 1)

        def lora_bank(n):
            return bank[n // 2][:, (n % 2) * C:(n % 2) * C + C]

        def setup_pe(pe):
            pe.wait_ge(const_p, 3)
            for i in range(3):
                pe.wait_ge(wq_abs, i + 1)
                pe.matmul(bank[6][:, i:i + 1], ones[:, :], wq_stat[:, i, 0:1], start=True, stop=True).then_inc(wq_sum, 1)

        def lora_at(col, width):
            return lora_sb[:, col // 768, col % 768:col % 768 + width]

        attn_w = {l: sem(f"{l}_attn_w") for l in ("L0", "L1", "L3")}

        attn_sems = [
            sem("attn_tanh"),
            sem("attn_gated"),
            sem("attn_proj"),
            sem("attn_copied"),
            sem("attn_v_ready"),
            sem("attn_scores"),
            sem("attn_negmax"),
            sem("attn_probs"),
            sem("attn_turned"),
            sem("attn_even"),
            sem("attn_odd"),
            sem("attn_mixed"),
            sem("attn_q_head"),
            sem("attn_inv"),
            sem("attn_normed"),
            sem("attn_out_copied"),
            sem("attn_out"),
            sem("attn_x_done"),
        ]
        attn_cap = sem("attn_cap")

        class Attention:
            def __init__(self, name, gate, next_gates, made, causal, q_scale, capped, ropes, biased, bias, d, v_heads, scrambled, x_ready, x_value, first, rope_step):
                self.name, self.gate, self.next_gates, self.made, self.bias = name, gate, next_gates, made, bias
                self.causal, self.q_scale, self.capped, self.ropes = causal, q_scale, capped, ropes
                self.biased, self.d, self.v_heads, self.scrambled = biased, d, v_heads, scrambled
                self.x_ready, self.x_value = x_ready, x_value
                self.first = first
                (self.tanh, self.gated, self.proj, self.copied, self.v_ready, self.scores, self.negmax, self.probs,
                 self.turned, self.even, self.odd, self.mixed, self.q_head, self.inv, self.normed, self.out_copied, self.out,
                 self.x_done) = attn_sems
                self.rope_step = rope_step
                self.cap = attn_cap

            def order(self, it, i):
                return it * len(self.next_gates) + (self.made + i)

            def blocks(self):
                return [(0, 0, P), (1, P, T)] if self.causal else [(0, 0, T), (1, T, T)]

            def width(self):
                return 384 if self.causal else 512

            def corners(self):
                at, out = 0, []
                for k in range(2):
                    for q, col, keys in self.blocks():
                        if k * P < keys:
                            out.append((q, k, at, col + k * P))
                            at += P
                return out

            def front_pe(self, pe, it):
                L = self
                pe.wait_ge(L.gated, (it + self.first) + 1)
                for tt in range(2):
                    for kc in range(KC):
                        mm = pe.matmul(bank[4][:, tt * C:tt * C + C], hb[:, kc, tt * P:tt * P + P],
                                       w_attn[:, kc, 2 * GROUPS * P:ATTN_COLS], start=(kc == 0), stop=(kc == KC - 1))
                mm.then_inc(L.proj, 1)
                for n, pair in enumerate((0, 2, 1, 3)):
                    if n == 1:
                        pe.wait_ge(L.v_ready, (it + self.first) + 1)
                    if n >= 2:
                        pe.wait_ge(L.copied, (it + self.first) * 4 + n - 1)
                    for g in range(2):
                        for kc in range(KC):
                            mm = pe.matmul(bank[5 - n % 2][:, g * T:g * T + T],
                                           w_attn[:, kc, (pair * 2 + g) * P:(pair * 2 + g + 1) * P], hb[:, kc, :],
                                           start=(kc == 0), stop=(kc == KC - 1))
                    mm.then_inc(L.proj, 1)

            def qk_ready(self, eng, it, pairs):
                if self.ropes is not None:
                    eng.wait_ge(self.rope_step, it * 16 + 4 * pairs)
                else:
                    eng.wait_ge(self.copied, (it + self.first) * 4 + pairs)

            def scores_pe(self, pe, it, hd):
                L, g = self, hd // 4
                if hd in (0, HEADS // 2):
                    L.qk_ready(pe, it, 2 if hd == 0 else 4)
                if hd == 2:
                    pe.wait_ge(L.copied, (it + self.first) * 4 + 4)
                if hd % 2 == 0:
                    pe.wait_ge(L.q_head, (it + L.first) * 8 + hd // 2 + 1)
                for q, col, keys in L.blocks():
                    mm = pe.matmul(score_bank[hd % DEEP][:, col:col + keys], q_head[:, hd // 2 % 2, hd % 2, q * P:q * P + P],
                                   qk[:, GROUPS + g, 0:keys], start=True, stop=not (L.causal and not L.capped))
                    if L.causal and not L.capped:
                        mm = pe.matmul(score_bank[hd % DEEP][:, col + keys - P:col + keys], ident_bf[:, :], negmask[:, :],
                                       start=False, stop=True)
                mm.then_inc(L.scores, 1)

            def turn_pe(self, pe, it, hd):
                L = self
                pe.wait_ge(L.normed, (it + self.first) * HEADS + hd + 1)
                if hd >= 2:
                    pe.wait_ge(L.odd if hd % 2 else L.even, (it + self.first) * 8 + hd // 2)
                for q, k, at, col in L.corners():
                    mm = pe.transpose(bank[2 + hd % 2][:, at:at + P], probs[:, hd % DEEP, col:col + P], ident[:, :])
                mm.then_inc(L.turned, 1)

            def mix_pe(self, pe, it, hd):
                L = self
                pe.wait_ge(L.odd if hd % 2 else L.even, (it + self.first) * 8 + hd // 2 + 1)
                if hd == 0 and L.scrambled:
                    pe.wait_ge(L.out_copied, it + self.first)
                vh = hd * L.v_heads // HEADS * SLOT
                g, j = hd // 4, hd % 4
                rows, first = slice(SLOT * j, SLOT * j + SLOT), g % 2 * T
                for k in range(2):
                    at, q0 = next((at, q * P) for q, kk, at, col in L.corners() if kk == k)
                    mm = pe.matmul(bank[6 + g // 2][rows, first + q0:first + T], v_sb[:, k, vh:vh + SLOT],
                                   probs_t[:, hd % 2, at:at + T - q0], start=(k == 0), stop=(k == 1),
                                   tile_position=(0, SLOT * j))
                if hd == HEADS - 1:
                    mm.then_inc(L.mixed, 1)

            def heads_pe(self, pe, it):
                for hd in range(DEEP):
                    self.scores_pe(pe, it, hd)
                for hd in range(HEADS):
                    self.turn_pe(pe, it, hd)
                    if hd + DEEP < HEADS:
                        self.scores_pe(pe, it, hd + DEEP)
                    if hd >= 1:
                        self.mix_pe(pe, it, hd - 1)
                self.mix_pe(pe, it, HEADS - 1)

            def tail_pe(self, pe, it, src):
                L = self
                pe.wait_ge(L.out_copied, self.first + B if L.scrambled else (it + self.first) + 1)
                if L.scrambled and it:
                    pe.wait_ge(L.x_done, (it + self.first))
                for m in range(KC):
                    for ch in range(GROUPS):
                        mm = pe.matmul(bank[6][:, m * T:m * T + T], w_out[:, ch, m * P:m * P + P], src(ch),
                                       start=(ch == 0), stop=(ch == GROUPS - 1))
                mm.then_inc(L.out, 1)

            def gate_act(self, act, it):
                act.wait_ge(self.x_ready, self.x_value)
                act.activation(hb[:, :, :], x[:, :, DSZ(it * T, T)], ACT.Tanh, scale=0.5).then_inc(self.tanh, 1)

            def front_act(self, act, it):
                L = self
                for n, pair in enumerate((0, 2, 1, 3)):
                    act.wait_ge(L.proj, (it + self.first) * 5 + n + 2)
                    src = bank[5 - n % 2]
                    dst = qk[:, pair * 2:pair * 2 + 2, :]
                    if L.biased:
                        for g in range(2):
                            a = act.activation(dst[:, g, :], src[:, g * T:g * T + T], ACT.Identity,
                                               bias=bias_attn[:, pair * 2 + g:pair * 2 + g + 1])
                    else:
                        a = act.activation(dst, src[:, :].rearrange("p (g t) -> p g t", g=2), ACT.Copy,
                                           scale=L.q_scale if pair < 2 else 1.0)
                    a.then_inc(L.copied, 1)

            def cap_act(self, act, it, hd):
                act.wait_ge(self.scores, (it + self.first) * HEADS + hd + 1)
                act.activation(probs[:, hd % DEEP, 0:self.width()], score_bank[hd % DEEP][:, 0:self.width()], ACT.Tanh,
                               scale=1.0 / (16.0 * CAP)).then_inc(self.cap, 1)

            def softmax_act(self, act, it, hd):
                L = self
                if L.capped and hd + 1 < HEADS:
                    L.cap_act(act, it, hd + 1)
                act.wait_ge(L.negmax, (it + self.first) * HEADS + hd + 1)
                for q, col, keys in L.blocks():
                    src = probs[:, hd % DEEP, col:col + keys] if L.capped else score_bank[hd % DEEP][:, col:col + keys]
                    a = act.activation(probs[:, hd % DEEP, col:col + keys], src, ACT.Exp, scale=CAP if L.capped else 1.0,
                                       bias=0.0 if L.capped else row_max[:, q * HEADS + hd:q * HEADS + hd + 1],
                                       accum_out=row_sum[:, q * HEADS + hd:q * HEADS + hd + 1])
                a.then_inc(L.probs, 1)

            def copied_by_act(self, hd):
                return hd % 2 == 0 or not self.capped

            def copy_act(self, act, it, hd):
                act.wait_ge(self.turned, (it + self.first) * HEADS + hd + 1)
                act.activation(probs_t[:, hd % 2, 0:self.width()], bank[2 + hd % 2][:, 0:self.width()], ACT.Copy)\
                   .then_inc(self.odd if hd % 2 else self.even, 1)

            def heads_act(self, act, it, last):
                for hd in range(HEADS):
                    if self.capped and hd == 0:
                        self.cap_act(act, it, 0)
                    self.softmax_act(act, it, hd)
                    for i, n in enumerate(self.next_gates):
                        if hd == 2 + 8 * i:
                            act.wait_ge(scan_done, self.order(it, i) + 2)
                    if hd >= 2 and self.copied_by_act(hd - 2):
                        self.copy_act(act, it, hd - 2)
                    for i, n in enumerate(self.next_gates):
                        if hd == 2 + 8 * i:
                            gate_act(act, n, it, self.order(it, i), True)
                    if hd == 8 and not last:
                        act.wait_ge(self.proj, (it + self.first) * 5 + 5)
                        self.gate_act(act, it + 1)
                for hd in (HEADS - 2, HEADS - 1):
                    if self.copied_by_act(hd):
                        self.copy_act(act, it, hd)

            def context_act(self, act, it):
                L = self
                act.wait_ge(L.mixed, (it + self.first) + 1)
                act.wait_ge(L.x_ready, L.x_value)
                dst = ctx_all[:, DSZ(it, 1), :] if L.scrambled else attn_t[:, :, :].rearrange("p (o g) t -> p o (g t)", o=1)
                for n in range(2):
                    a = act.activation(dst[:, :, n * 512:n * 512 + 512], bank[6 + n][:, :].unsqueeze(1), ACT.Copy)
                a.then_inc(L.out_copied, 1)

            def gate_dve(self, dve, it):
                dve.wait_ge(self.tanh, (it + self.first) + 1)
                if isinstance(it, int) and it == 0:
                    dve.wait_ge(g_done, G_READY[self.gate] + 1)
                dve.scalar_tensor_tensor(out=hb[:, :, :], in0=hb[:, :, :], scalar=1.0,
                                         in1=G[:, G_SLOT[self.gate], :, DSZ(it * T, T)], op0=ALU.add, op1=ALU.mult)\
                   .then_inc(self.gated, 1)

            def front_dve(self, dve, it):
                L = self
                dve.wait_ge(L.proj, (it + self.first) * 5 + 1)
                if L.v_heads == HEADS:
                    dst = v_sb[:, :, :].rearrange("p t (h s) -> p t h s", s=SLOT)[:, :, :, 0:16]
                    src = bank[4][:, :].rearrange("p (t h e) -> p t h e", t=2, e=16)
                else:
                    dst, src = v_sb[:, :, 0:C], bank[4][:, :].rearrange("p (t c) -> p t c", t=2)
                if L.biased:
                    for tt in range(2):
                        v = dve.tensor_tensor(dst[:, tt], src[:, tt], bias_v[:, :].rearrange("p (h e) -> p h e", e=16), ALU.add)
                else:
                    for tt in range(2):
                        v = dve.tensor_copy(dst[:, tt], src[:, tt])
                v.then_inc(L.v_ready, 1)
                if L.ropes is None:
                    return
                mask, tab = L.ropes
                cos = rope[:, tab, :].unsqueeze(1).to_broadcast([P, 2, T])
                sin = rope[:, tab + 1, :].unsqueeze(1).to_broadcast([P, 2, T])
                for n, pair in enumerate((0, 2, 1, 3)):
                    dst = qk[:, pair * 2:pair * 2 + 2, :]
                    at = it * 16 + 4 * n
                    if n:
                        dve.wait_ge(L.rope_step, at)
                    dve.wait_ge(L.copied, (it + self.first) * 4 + n + 1)
                    dve.tensor_tensor(rope_b[:, :, :], dst, cos, ALU.mult).then_inc(L.rope_step, 1)
                    dve.stream_shuffle(rope_a[:, :, :], dst, mask).then_inc(L.rope_step, 1)
                    dve.wait_ge(L.rope_step, at + 2)
                    dve.tensor_tensor(rope_a[:, :, :], rope_a[:, :, :], sin, ALU.mult).then_inc(L.rope_step, 1)
                    dve.wait_ge(L.rope_step, at + 3)
                    dve.tensor_tensor(dst, rope_a[:, :, :], rope_b[:, :, :], ALU.add).then_inc(L.rope_step, 1)

            def max_dve(self, dve, it, hd):
                L = self
                if L.capped:
                    dve.wait_ge(L.cap, it * HEADS + hd + 1)
                    v = probs[:, hd % DEEP, 0:512].rearrange("p (a b) -> p a b", a=2)[:, :, 0:P]
                    dve.tensor_tensor(v, v, capmask[:, :].unsqueeze(1).to_broadcast([P, 2, P]), ALU.add).then_inc(L.negmax, 1)
                    return
                dve.wait_ge(L.scores, (it + self.first) * HEADS + hd + 1)
                for q, col, keys in L.blocks():
                    r = dve.tensor_reduce(row_max[:, q * HEADS + hd:q * HEADS + hd + 1], score_bank[hd % DEEP][:, col:col + keys],
                                          AX.X, ALU.max, negate=True)
                r.then_inc(L.negmax, 1)

            def copy_dve(self, dve, it, hd):
                dve.wait_ge(self.turned, (it + self.first) * HEADS + hd + 1)
                dve.tensor_copy(probs_t[:, hd % 2, 0:self.width()], bank[2 + hd % 2][:, 0:self.width()]).then_inc(self.odd, 1)

            def heads_dve(self, dve, it, last):
                self.max_dve(dve, it, 0)
                for hd in range(HEADS):
                    if hd + 1 < HEADS:
                        self.max_dve(dve, it, hd + 1)
                    if self.capped:
                        self.inv_dve(dve, it, hd)
                    elif hd >= 1:
                        self.inv_dve(dve, it, hd - 1)
                    if hd >= 2 and not self.copied_by_act(hd - 2):
                        self.copy_dve(dve, it, hd - 2)
                    for i, n in enumerate(self.next_gates):
                        if 0 <= hd - 1 - 8 * i < 6:
                            gate_dve(dve, hd - 1 - 8 * i, n, it, self.order(it, i))
                        if hd - 1 - 8 * i == 6:
                            gate_finish(dve, n, it, self.order(it, i))
                    if hd == 8 and not last:
                        self.gate_dve(dve, it + 1)
                if not self.capped:
                    self.inv_dve(dve, it, HEADS - 1)
                if not self.copied_by_act(HEADS - 1):
                    self.copy_dve(dve, it, HEADS - 1)

            def inv_dve(self, dve, it, hd):
                dve.wait_ge(self.probs, (it + self.first) * HEADS + hd + 1)
                dve.reciprocal(row_inv[:, :].rearrange("p (q h) -> p q h", q=2)[:, :, hd],
                               row_sum[:, :].rearrange("p (q h) -> p q h", q=2)[:, :, hd]).then_inc(self.inv, 1)

            def q_head_pool(self, pool, it, pair):
                g, j = pair // 2, pair % 2 * 2
                pool.tensor_tensor(q_head[:, pair % 2, :, :], qk[:, g, :].unsqueeze(1).to_broadcast([P, 2, T]),
                                   head_mask[:, j:j + 2].unsqueeze(2).to_broadcast([P, 2, T]), ALU.mult).then_inc(self.q_head, 1)

            def pool(self, pool):
                L = self
                with pool.Fori(0, B) as it:
                    gate_pool(pool, it, L.order(it, 0))
                    L.qk_ready(pool, it, 1)
                    L.q_head_pool(pool, it, 0)
                    L.q_head_pool(pool, it, 1)
                    for hd in range(HEADS):
                        if hd % 2 == 0 and hd + 4 < HEADS:
                            if hd == 4:
                                L.qk_ready(pool, it, 3)
                            pool.wait_ge(L.scores, (it + self.first) * HEADS + hd + 2)
                            L.q_head_pool(pool, it, hd // 2 + 2)
                        if hd == 7 and len(L.next_gates) == 2:
                            pool.wait_ge(scan_done, L.order(it, 1) + 1)
                        pool.wait_ge(L.inv, (it + self.first) * HEADS + hd + 1)
                        for q, col, keys in L.blocks():
                            p = probs[:, hd % DEEP, col:col + keys]
                            n = pool.tensor_tensor(p, p, row_inv[:, q * HEADS + hd:q * HEADS + hd + 1].to_broadcast([P, keys]), ALU.mult)
                        n.then_inc(L.normed, 1)
                        if hd == 7 and len(L.next_gates) == 2:
                            gate_pool(pool, it, L.order(it, 1), True)

            def tail_dve(self, dve, it):
                L, bias = self, self.bias
                dve.wait_ge(L.out, (it + self.first) + 1)
                for m in range(KC):
                    xs = x[:, m, DSZ(it * T, T)]
                    y = bank[6][:, m * T:m * T + T]
                    if bias is None:
                        r = dve.tensor_tensor(xs, y, xs, ALU.add)
                    else:
                        r = dve.scalar_tensor_tensor(out=xs, in0=y, scalar=bias_attn[:, bias + m:bias + m + 1], in1=xs,
                                                     op0=ALU.add, op1=ALU.add)
                r.then_inc(L.x_done, 1)

            def pe(self, pe):
                L = self
                attn_src = lambda ch: attn_t[:, ch, :]
                pe.wait_ge(attn_w[L.name], 32)
                if L.name == "L0":
                    pe.wait_ge(const_p, 16)
                L.front_pe(pe, 0)
                with pe.Fori(0, B - 1) as it:
                    L.heads_pe(pe, it)
                    L.front_pe(pe, it + 1)
                    if not L.scrambled:
                        L.tail_pe(pe, it, attn_src)
                L.heads_pe(pe, B - 1)
                if not L.scrambled:
                    L.tail_pe(pe, B - 1, attn_src)
                else:
                    for tb in range(B):
                        L.tail_pe(pe, tb, lambda b: ctx_all[:, b, tb * T:tb * T + T])

            def act(self, act):
                L = self
                if L.name == "L0":
                    act.wait_ge(misc_in, 16 * 8)
                L.gate_act(act, 0)
                L.front_act(act, 0)
                with act.Fori(0, B - 1) as it:
                    L.heads_act(act, it, False)
                    L.context_act(act, it)
                    L.front_act(act, it + 1)
                L.heads_act(act, B - 1, True)
                L.context_act(act, B - 1)

            def dve(self, dve):
                L = self
                if L.name == "L0":
                    dve.wait_ge(misc_in, 16 * 8)
                    dve.wait_ge(const_p, 16)
                L.gate_dve(dve, 0)
                L.front_dve(dve, 0)
                with dve.Fori(0, B - 1) as it:
                    L.heads_dve(dve, it, False)
                    L.front_dve(dve, it + 1)
                    if not L.scrambled:
                        L.tail_dve(dve, it)
                L.heads_dve(dve, B - 1, True)
                for tb in range(0 if L.scrambled else B - 1, B):
                    L.tail_dve(dve, tb)

        ffn_sems = [
            sem("ffn_tanh"),
            sem("ffn_gated"),
            sem("ffn_hi"),
            sem("ffn_lo"),
            sem("ffn_logits"),
            sem("ffn_c_turned"),
            sem("ffn_c_copied"),
            sem("ffn_c_out"),
            sem("ffn_summed"),
            sem("ffn_x_done"),
        ]

        class Experts:
            def __init__(self, name, gate, chunks, experts, reps, next_gate, x_ready, x_value, route_at, sources, before, k):
                self.before = before
                self.name, self.gate, self.chunks, self.E, self.reps = name, gate, chunks, experts, reps
                self.next_gate, self.x_ready, self.x_value, self.route_at = next_gate, x_ready, x_value, route_at
                self.sources = sources
                s = lambda n: sem(f"{name}_ffn_{n}")
                self.tanh, self.gated, self.hi, self.lo, self.logits, self.c_turned, self.c_copied, self.c_out, self.summed, self.x_done = ffn_sems
                self.r_step, self.r_act = s("r_step"), s("r_act")
                self.w_in, self.c_in = [s("w_in0"), s("w_in1")], [s("c_in0"), s("c_in1")]
                self.gu_hi, self.gu_lo = s("gu_hi"), s("gu_lo")
                self.d_hi, self.d_lo = s("d_hi"), s("d_lo")
                self.gate_mm, self.up_mm, self.down = s("gate_mm"), s("up_mm"), s("down")
                self.silu, self.act_hi = s("silu"), s("act_hi")
                self.mul, self.act_lo = s("mul"), s("act_lo")
                self.weighted = s("weighted")
                self.k = k

            def load_w(self, sp, src, slot):
                sp.dma_start(w_raw[:, slot, :], src).then_inc(self.w_in[slot], 16)

            def load_c(self, sp, c, slot):
                src = c_dram[self.name][DSZ(c * GRANULES, GRANULES), :].unsqueeze(1).to_broadcast([GRANULES, EXPERT_ROWS, N])
                sp.dma_start(c_rows[:, slot, :], src).then_inc(self.c_in[slot], 16)

            def prefetch_sp(self, sp):
                if self.before is not None:
                    sp.wait_ge(self.before.d_lo, self.before.chunks)
                    sp.wait_ge(self.before.gu_lo, self.before.chunks + 1)
                for c in (0, 1):
                    self.load_w(sp, self.sources(c), c)

            def sp(self, sp):
                n = self.chunks
                sp.wait_ge(self.c_copied, 2 * self.k + 2)
                sp.dma_start(c_dram[self.name][0:self.E * self.reps, :].rearrange("(e r) t -> e r t", r=self.reps),
                             c_t[0:self.E, :].unsqueeze(1).to_broadcast([self.E, self.reps, N])).then_inc(self.c_out, 16)
                sp.wait_ge(self.c_out, 16 * self.k + 16)
                if self.name == "L0":
                    sp.wait_ge(ones_out, 16)
                for c in (0, 1):
                    self.load_c(sp, c, c)

                def load(c, slot, src, rows=True):
                    sp.wait_ge(self.d_lo, c - 1)
                    self.load_w(sp, src, slot)
                    if rows:
                        sp.wait_ge(self.weighted, c * 2 - 2)
                        self.load_c(sp, c, slot)

                c = 2
                while not isinstance(self.sources(c), tuple):
                    load(c, c % 2, self.sources(c))
                    c += 1
                dram = self.sources(c)[0]
                with sp.Fori(0, (n - c) // 2) as i:
                    for k in range(2):
                        load(i * 2 + (c + k), (c + k) % 2, dram[DSZ(i * 2 + (c + k), 1)].rearrange("a p k -> (a p) k"))
                if (n - c) % 2:
                    load(n - 1, (n - 1) % 2, dram[n - 1])
                load(n, n % 2, dram[n], rows=False)

            def three(self, pe, o, w_hi, w_lo, r_hi, r_lo, start, stop):
                pe.matmul(o, w_hi, r_hi, start=start, stop=False)
                pe.matmul(o, w_lo, r_hi, start=False, stop=False)
                return pe.matmul(o, w_hi, r_lo, start=False, stop=stop)

            def gate_up_pe(self, pe, c, slot, half, first):
                L = self
                if not first:
                    pe.wait_ge(L.silu, c * 2 - 1 + half)
                    pe.wait_ge(L.mul, c * 2 - 1 + half)
                tok = slice(half * HALF, half * HALF + HALF)
                for n, done in enumerate((L.gate_mm, L.up_mm)):
                    for kc in range(KC):
                        w = slice((2 * n + kc) * P, (2 * n + kc) * P + P)
                        mm = L.three(pe, bank[2 * half + n][:, :], w_gu_hi[:, slot, w], w_gu_lo[:, slot, w],
                                     h_hi[:, kc, tok], h_lo[:, kc, tok], kc == 0, kc == KC - 1)
                    mm.then_inc(done, 1)

            def down_pe(self, pe, c, slot, half):
                L = self
                if half == 0:
                    pe.wait_ge(L.d_lo, c + 1)
                pe.wait_ge(L.act_lo, c * 2 + half + 1)
                for m in range(KC):
                    w = slice(m * P, m * P + P)
                    mm = L.three(pe, bank[4 + 2 * m + half][:, :], w_d_hi[:, slot, w], w_d_lo[:, slot, w],
                                 act_hi[:, half, :], act_lo[:, half, :], False, False)
                mm.then_inc(L.down, 1)

            def step_pe(self, pe, c, slot, first=False):
                pe.wait_ge(self.gu_lo, c + 1)
                for half in range(2):
                    self.gate_up_pe(pe, c, slot, half, first)
                    if not first:
                        self.down_pe(pe, c - 1, 1 - slot, half)

            def loops(self, eng, body, extra=None):
                done = 2 * B if self.next_gate is not None else 0
                rounds = (self.chunks - 1 - done) // 2
                if done:
                    with eng.Fori(0, B) as b:
                        for k in range(2):
                            body(b * 2 + (k + 1), (k + 1) % 2, (b, k))
                if rounds > 1:
                    with eng.Fori(0, rounds) as i:
                        for k in range(2):
                            body(i * 2 + (done + k + 1), (k + 1) % 2, None)
                for c in range(done + 1 + 2 * (rounds if rounds > 1 else 0), self.chunks):
                    body(c, c % 2, None)

            def pe(self, pe):
                L, E = self, self.E
                pe.wait_ge(L.gated, 2 * L.k + 2)
                for tt in range(TILES):
                    for kc in range(KC):
                        mm = pe.matmul(bank[4][:, tt * E:tt * E + E], h[:, kc, tt * P:tt * P + P],
                                       w_route[:, L.route_at, kc, 0:E], start=(kc == 0), stop=(kc == KC - 1))
                mm.then_inc(L.logits, 1)
                pe.wait_ge(L.lo, 2 * L.k + 2)
                L.step_pe(pe, 0, 0, first=True)
                pe.wait_ge(L.r_step, L.route_steps)
                for half in range(2):
                    for tt in range(4):
                        mm = pe.transpose(bank[5 + half][0:E, tt * P:tt * P + P],
                                          route[:, 0, (half * 4 + tt) * E:(half * 4 + tt + 1) * E], ident[:, :])
                    mm.then_inc(L.c_turned, 1)
                pe.wait_ge(L.c_copied, 2 * L.k + 2)
                for i in range(4):
                    pe.matmul(bank[4 + i][:, :], zeros_bf[:, 0:P], zeros_bf[:, :], start=True, stop=False)
                L.loops(pe, lambda c, slot, _: L.step_pe(pe, c, slot))
                for half in range(2):
                    L.down_pe(pe, L.chunks - 1, (L.chunks - 1) % 2, half)
                for i in range(4):
                    mm = pe.matmul(bank[4 + i][:, :], zeros_bf[:, 0:P], zeros_bf[:, :], start=False, stop=True)
                mm.then_inc(L.summed, 1)

            def split_gu_act(self, act, c, slot, wait_up):
                act.wait_ge(self.w_in[slot], wait_up[0])
                if wait_up[1] is not None:
                    act.wait_ge(self.up_mm, wait_up[1])
                act.activation(w_gu_hi[:, slot, :], w_raw[:, slot, 0:512], ACT.Copy).then_inc(self.gu_hi, 1)

            def split_d_act(self, act, c, slot):
                act.activation(w_d_hi[:, slot, :], w_raw[:, slot, 512:768], ACT.Copy).then_inc(self.d_hi, 1)

            def step_act(self, act, c, slot, loaded, gate, first=False):
                L = self
                for half in range(2):
                    act.wait_ge(L.gate_mm, c * 2 + half + 1)
                    act.activation(act_s[:, half, :], bank[2 * half][:, :], ACT.Silu).then_inc(L.silu, 1)
                    if half == 0:
                        L.split_gu_act(act, c + 1, 1 - slot, (loaded, None if first else c * 2))
                        if first:
                            L.split_d_act(act, 0, 0)
                    act.wait_ge(L.mul, c * 2 + half + 1)
                    if not first:
                        act.wait_ge(L.down, c * 2 - 1 + half)
                    act.activation(act_hi[:, half, :], act_a[:, half, :], ACT.Copy).then_inc(L.act_hi, 1)
                    if half == 0 and not first:
                        L.split_d_act(act, c, slot)

            def act(self, act):
                L = self
                act.wait_ge(L.x_ready, L.x_value)
                if L.name == "L0":
                    act.wait_ge(wq_done, 3)
                for half in range(2):
                    tok = slice(half * HALF, half * HALF + HALF)
                    act.activation(h[:, :, tok], x[:, :, tok], ACT.Tanh, scale=0.5).then_inc(L.tanh, 1)
                for half in range(2):
                    tok = slice(half * HALF, half * HALF + HALF)
                    act.wait_ge(L.gated, 2 * L.k + half + 1)
                    act.activation(h_hi[:, :, tok], h[:, :, tok], ACT.Copy).then_inc(L.hi, 1)
                L.split_gu_act(act, 0, 0, (16, None))
                if L.next_gate is not None:
                    for ch in range(KC):
                        last = act.activation(G[:, G_SLOT[L.next_gate], ch, :], side[:, ch, :], ACT.Exp,
                                              bias=wu[:, 1, ch, L.next_gate:L.next_gate + 1])
                    last.then_inc(euk_done, B)
                L.route_act(act)
                for half in range(2):
                    act.wait_ge(L.c_turned, 2 * L.k + half + 1)
                    act.activation(c_t[0:L.E, half * HALF:half * HALF + HALF], bank[5 + half][0:L.E, :], ACT.Copy).then_inc(L.c_copied, 1)
                L.step_act(act, 0, 0, 16, None, first=True)

                def body(c, slot, gate):
                    L.step_act(act, c, slot, L.loads(c + 1, 1 - slot), gate)
                L.loops(act, body)

            def loads(self, c, slot):
                return (c - slot) * 8 + 16

            def pool(self, pool):
                L = self

                def gu(c, slot):
                    pool.wait_ge(L.gu_hi, c + 1)
                    pool.tensor_tensor(w_gu_lo[:, slot, :], w_raw[:, slot, 0:512], w_gu_hi[:, slot, :].bitcast(F32), ALU.subtract)\
                        .then_inc(L.gu_lo, 1)

                def d(c, slot):
                    pool.wait_ge(L.d_hi, c + 1)
                    pool.tensor_tensor(w_d_lo[:, slot, :], w_raw[:, slot, 512:768], w_d_hi[:, slot, :].bitcast(F32), ALU.subtract)\
                        .then_inc(L.d_lo, 1)

                def weigh(c, slot, half):
                    if half == 0:
                        pool.wait_ge(L.c_in[slot], L.loads(c, slot))
                    pool.wait_ge(L.silu, c * 2 + half + 1)
                    pool.tensor_tensor(act_s[:, half, :], act_s[:, half, :], c_rows[:, slot, half * HALF:half * HALF + HALF],
                                       ALU.mult).then_inc(L.weighted, 1)

                gu(0, 0)
                weigh(0, 0, 0)
                gu(1, 1)
                weigh(0, 0, 1)
                d(0, 0)

                def body(c, slot, gate):
                    weigh(c, slot, 0)
                    gu(c + 1, 1 - slot)
                    weigh(c, slot, 1)
                    if gate is not None and gate[1] == 0:
                        gate_pool(pool, gate[0], gate[0] + (G_READY[L.next_gate] - B))
                    d(c, slot)
                L.loops(pool, body)

            def step_dve(self, dve, c, gate):
                L = self
                for half in range(2):
                    n = c * 2 + half + 1
                    dve.wait_ge(L.weighted, n)
                    dve.wait_ge(L.up_mm, n)
                    dve.tensor_tensor(act_a[:, half, :], bank[2 * half + 1][:, :], act_s[:, half, :], ALU.mult).then_inc(L.mul, 1)
                    dve.wait_ge(L.act_hi, n)
                    dve.tensor_tensor(act_lo[:, half, :], act_a[:, half, :], act_hi[:, half, :].bitcast(F32), ALU.subtract)\
                       .then_inc(L.act_lo, 1)
                    if gate is not None:
                        b, k = gate
                        o = b + (G_READY[L.next_gate] - B)
                        for part in (((), (0, 1)), ((2,), (3, 4)))[k][half]:
                            gate_dve(dve, part, L.next_gate, b, o, G[:, G_SLOT[L.next_gate], :, :])
                if gate is not None and gate[1] == 1:
                    gate_dve(dve, 5, L.next_gate, b, o)
                    gate_finish(dve, L.next_gate, b, o)

            def dve(self, dve):
                L = self
                for half in range(2):
                    tok = slice(half * HALF, half * HALF + HALF)
                    dve.wait_ge(L.tanh, 2 * L.k + half + 1)
                    if half == 0:
                        dve.wait_ge(g_done, G_READY[L.gate] + 1)
                    dve.scalar_tensor_tensor(out=h[:, :, tok], in0=h[:, :, tok], scalar=1.0, in1=G[:, G_SLOT[L.gate], :, tok],
                                             op0=ALU.add, op1=ALU.mult).then_inc(L.gated, 1)
                for half in range(2):
                    tok = slice(half * HALF, half * HALF + HALF)
                    dve.wait_ge(L.gated, 2 * L.k + 2)
                    dve.wait_ge(L.hi, 2 * L.k + half + 1)
                    dve.tensor_tensor(h_lo[:, :, tok], h[:, :, tok], h_hi[:, :, tok].bitcast(F32), ALU.subtract).then_inc(L.lo, 1)
                L.route_dve(dve)
                L.step_dve(dve, 0, None)
                L.loops(dve, lambda c, slot, gate: L.step_dve(dve, c, gate))
                dve.wait_ge(L.summed, 1 * L.k + 1)
                for half in range(2):
                    for m in range(KC):
                        xs = x[:, m, half * HALF:half * HALF + HALF]
                        dve.tensor_tensor(xs, bank[4 + 2 * m + half][:, :], xs, ALU.add).then_inc(L.x_done, 1)

            def tab(self, i):
                return route[:, i, 0:TILES * self.E].rearrange("p (t e) -> p t e", e=self.E)

            def rank_dve(self, dve, do, src, dst):
                E = self.E
                big = lambda t: t[:, :, :].rearrange("p a b -> p (a b)")[:, 0:4 * E * E].rearrange("p (t i j) -> p t i j", i=E, j=E)
                for half in range(2):
                    v = src[:, 4 * half:4 * half + 4, :]
                    vj = v.unsqueeze(2).to_broadcast([P, 4, E, E])
                    vi = v.unsqueeze(3).to_broadcast([P, 4, E, E])
                    do(dve.tensor_tensor(big(act_s), vj, vi, ALU.is_ge))
                    do(dve.tensor_tensor(big(act_m), vj, vi, ALU.is_gt))
                    do(dve.tensor_tensor(big(act_s), big(act_s), earlier[:, 0:E, 0:E].unsqueeze(1).to_broadcast([P, 4, E, E]), ALU.mult))
                    do(dve.tensor_tensor(big(act_s), big(act_s), big(act_m), ALU.max))
                    do(dve.tensor_reduce(dst[:, 4 * half:4 * half + 4, :], big(act_s), AX.X, ALU.add))

            def route_dve(self, dve):
                L, E = self, self.E
                steps = [0]

                def do(ins):
                    steps[0] += 1
                    ins.then_inc(L.r_step, 1)
                    dve.wait_ge(L.r_step, steps[0])

                def sync():
                    L.act_turns.append(steps[0])
                    dve.wait_ge(L.r_act, len(L.act_turns))

                L.act_turns = []
                tb, bc = L.tab, lambda i: route_s[:, i, :].unsqueeze(2).to_broadcast([P, TILES, E])
                dve.wait_ge(L.logits, 1 * L.k + 1)
                do(dve.tensor_copy(route[:, 1, 0:TILES * E], bank[4][:, 0:TILES * E]))
                lg = tb(1)
                if L.name == "L0":
                    L.rank_dve(dve, do, lg, tb(2))
                    do(dve.tensor_scalar(tb(2), tb(2), 5.5, None, ALU.is_lt))
                    do(dve.tensor_reduce(route_s[:, 0, :], lg, AX.X, ALU.max))
                    do(dve.tensor_tensor(tb(3), lg, bc(0), ALU.subtract))
                    sync()
                    do(dve.tensor_reduce(route_s[:, 1, :], tb(3), AX.X, ALU.add))
                    do(dve.reciprocal(route_s[:, 2, :], route_s[:, 1, :]))
                    do(dve.tensor_tensor(tb(3), tb(3), bc(2), ALU.mult))
                    do(dve.tensor_tensor(tb(4), tb(3), tb(2), ALU.mult))
                    do(dve.tensor_reduce(route_s[:, 3, :], tb(4), AX.X, ALU.add))
                    do(dve.tensor_scalar(route_s[:, 3, :], route_s[:, 3, :], 1e-20, None, ALU.add))
                    do(dve.reciprocal(route_s[:, 4, :], route_s[:, 3, :]))
                    do(dve.tensor_tensor(tb(0), tb(4), bc(4), ALU.mult))
                elif L.name == "L1":
                    L.rank_dve(dve, do, lg, tb(2))
                    do(dve.tensor_scalar(tb(3), tb(2), 0.5, None, ALU.is_lt))
                    do(dve.tensor_scalar(tb(4), tb(2), 1.0, None, ALU.is_equal))
                    do(dve.tensor_tensor(tb(4), tb(4), tb(3), ALU.subtract))
                    do(dve.tensor_tensor(tb(4), tb(4), lg, ALU.mult))
                    do(dve.tensor_reduce(route_s[:, 0, :], tb(4), AX.X, ALU.add))
                    sync()
                    do(dve.tensor_scalar(route_s[:, 1, :], route_s[:, 0, :], 1.0, None, ALU.add))
                    do(dve.reciprocal(route_s[:, 2, :], route_s[:, 1, :]))
                    do(dve.tensor_tensor(tb(0), tb(3), bc(2), ALU.mult))
                else:
                    center = float(1.0 / np.e)
                    lower = float(0.5 - np.log(4.0 / 3.0))
                    do(dve.reciprocal(temp[:, 1:2], temp[:, 0:1]))
                    do(dve.tensor_scalar(lg, lg, temp[:, 1:2], None, ALU.mult))
                    sync()
                    do(dve.tensor_scalar(tb(2), tb(2), 0.5, 0.5, ALU.mult, ALU.add))
                    do(dve.tensor_scalar(tb(3), tb(2), lower, None, ALU.is_ge))
                    do(dve.tensor_scalar(tb(4), tb(2), 0.5, None, ALU.is_le))
                    do(dve.tensor_tensor(tb(3), tb(3), tb(4), ALU.mult))
                    do(dve.tensor_scalar(tb(4), tb(2), -1.0, center, ALU.mult, ALU.add))
                    do(dve.scalar_tensor_tensor(out=tb(2), in0=tb(2), scalar=center, in1=tb(4), op0=ALU.subtract, op1=ALU.max))
                    sync()
                    do(dve.tensor_tensor(tb(4), tb(4), tb(3), ALU.mult))
                    do(dve.tensor_reduce(route_s[:, 0, :], tb(4), AX.X, ALU.add))
                    do(dve.tensor_scalar(route_s[:, 1, :], route_s[:, 0, :], 1e-8, None, ALU.is_lt))
                    L.rank_dve(dve, do, tb(5), tb(6))
                    do(dve.tensor_scalar(tb(6), tb(6), 1.5, None, ALU.is_lt))
                    do(dve.tensor_tensor(tb(5), tb(5), tb(6), ALU.mult))
                    do(dve.tensor_reduce(route_s[:, 2, :], tb(5), AX.X, ALU.add))
                    do(dve.tensor_scalar(route_s[:, 2, :], route_s[:, 2, :], 1e-8, None, ALU.max))
                    do(dve.reciprocal(route_s[:, 3, :], route_s[:, 2, :]))
                    do(dve.tensor_tensor(tb(5), tb(5), bc(3), ALU.mult))
                    do(dve.tensor_tensor(tb(5), tb(5), bc(1), ALU.mult))
                    do(dve.tensor_scalar(route_s[:, 4, :], route_s[:, 1, :], -1.0, 1.0, ALU.mult, ALU.add))
                    do(dve.tensor_tensor(tb(4), tb(4), bc(4), ALU.mult))
                    do(dve.tensor_tensor(tb(4), tb(4), tb(5), ALU.add))
                    do(dve.tensor_reduce(route_s[:, 0, :], tb(4), AX.X, ALU.add))
                    do(dve.tensor_scalar(route_s[:, 0, :], route_s[:, 0, :], 1e-8, None, ALU.max))
                    do(dve.reciprocal(route_s[:, 5, :], route_s[:, 0, :]))
                    do(dve.tensor_tensor(tb(0), tb(4), bc(5), ALU.mult))
                assert steps[0] == L.route_steps, steps

            def route_act(self, act):
                L, tb = self, self.tab
                turns = dict(L0=(18 - 4,), L1=(16,), L3=(3, 9))[L.name]
                for n, at in enumerate(turns):
                    act.wait_ge(L.r_step, at)
                    if L.name == "L0":
                        a = act.activation(tb(3), tb(3), ACT.Exp)
                    elif L.name == "L1":
                        a = act.activation(route_s[:, 0, :], route_s[:, 0, :], ACT.Exp)
                    elif n == 0:
                        a = act.activation(tb(2), tb(1), ACT.Tanh, scale=0.5)
                    else:
                        act.activation(tb(4), tb(2), ACT.Exp, scale=-1.0 / 0.1)
                        a = act.activation(tb(5), tb(2), ACT.Exp, scale=-1.0 / 0.3)
                    a.then_inc(L.r_act, 1)
                L.turns_used = turns

            @property
            def route_steps(self):
                return dict(L0=22, L1=19, L3=36)[self.name]

        cd_w = sem("cd_w")
        mixer_tanh = sem("mixer_tanh")
        mixer_gated = sem("mixer_gated")
        mixer_mm = sem("mixer_mm")
        mixer_sig = sem("mixer_sig")
        mixer_step = sem("mixer_step")
        mixer_x = sem("mixer_x")
        C_B, D_B, LOG_DELTA, DECAY, AB = (slice(KC * i, KC * i + KC) for i in range(5))

        def mixer_pe(pe):
            pe.wait_ge(cd_w, 16)
            for half in range(2):
                tok = slice(half * HALF, half * HALF + HALF)
                pe.wait_ge(mixer_gated, half + 1)
                for m in range(KC):
                    for col, first in ((C, 4), (0, 0)):
                        for kc in range(KC):
                            mm = pe.matmul(bank[first + 2 * m + half][:, :], w_attn[:, kc, col + m * P:col + m * P + P],
                                           h[:, kc, tok], start=(kc == 0), stop=(kc == KC - 1))
                        mm.then_inc(mixer_mm, 1)

        def mixer_act(act):
            act.wait_ge(F1.x_done, 8)
            for half in range(2):
                tok = slice(half * HALF, half * HALF + HALF)
                act.activation(h[:, :, tok], x[:, :, tok], ACT.Tanh, scale=0.5).then_inc(mixer_tanh, 1)
            act.activation(scan_c[:, DECAY], scan_c[:, LOG_DELTA], ACT.Sigmoid, scale=-1.0).then_inc(mixer_sig, 1)
            for half in range(2):
                for m in range(KC):
                    act.wait_ge(mixer_mm, 4 * half + 2 * m + 1)
                    act.activation(c_rows[:, m, half * HALF:half * HALF + HALF], bank[4 + 2 * m + half][:, :], ACT.Sigmoid,
                                   bias=scan_c[:, D_B][:, m:m + 1]).then_inc(mixer_sig, 1)

        def mixer_dve(dve):
            dve.tensor_tensor(ab_in[:, 0, :, :], ab_in[:, 0, :, :], ab_in[:, 1, :, :], ALU.mult).then_inc(mixer_step, 1)
            dve.wait_ge(mixer_step, 1)
            dve.tensor_reduce(scan_c[:, AB], ab_in[:, 0, :, :], AX.X, ALU.add).then_inc(mixer_step, 1)
            for half in range(2):
                tok = slice(half * HALF, half * HALF + HALF)
                dve.wait_ge(mixer_tanh, half + 1)
                dve.scalar_tensor_tensor(out=h[:, :, tok], in0=h[:, :, tok], scalar=1.0, in1=G[:, G_SLOT[4], :, tok],
                                         op0=ALU.add, op1=ALU.mult).then_inc(mixer_gated, 1)
            for half in range(2):
                tok = slice(half * HALF, half * HALF + HALF)
                for m in range(KC):
                    dve.wait_ge(mixer_mm, 4 * half + 2 * m + 2)
                    dve.wait_ge(mixer_sig, 2 * half + m + 2)
                    dve.scalar_tensor_tensor(out=c_rows[:, m, tok], in0=bank[2 * m + half][:, :], scalar=scan_c[:, C_B][:, m:m + 1],
                                             in1=c_rows[:, m, tok], op0=ALU.add, op1=ALU.mult).then_inc(mixer_step, 1)
                dve.wait_ge(mixer_step, 2 + 6 * half + 2)
                for b in (2 * half, 2 * half + 1):
                    for m in range(KC):
                        dve.tensor_tensor_scan(h[:, m, b * T:b * T + T], scan_c[:, DECAY][:, m:m + 1].to_broadcast([P, T]),
                                               c_rows[:, m, b * T:b * T + T], 0.0, ALU.mult, ALU.add).then_inc(mixer_step, 1)
                dve.wait_ge(mixer_step, 2 + 6 * half + 6)
                for b in (2 * half, 2 * half + 1):
                    for m in range(KC):
                        xs = x[:, m, b * T:b * T + T]
                        dve.scalar_tensor_tensor(out=xs, in0=h[:, m, b * T:b * T + T], scalar=scan_c[:, AB][:, m:m + 1], in1=xs,
                                                 op0=ALU.mult, op1=ALU.add).then_inc(mixer_x, 1)

        ln_in = sem("ln_in")
        bit_tanh = sem("bit_tanh")
        bit_gated = sem("bit_gated")
        bit_turned = sem("bit_turned")
        bit_step = sem("bit_step")
        bit_q = sem("bit_q")
        bit_q_turned = sem("bit_q_turned")
        bit_q_copied = sem("bit_q_copied")
        bit_gate = sem("bit_gate")
        bit_up = sem("bit_up")
        bit_silu = sem("bit_silu")
        bit_mid = sem("bit_mid")
        bit_sq = sem("bit_sq")
        bit_var = sem("bit_var")
        bit_rstd = sem("bit_rstd")
        bit_norm = sem("bit_norm")
        bit_q2 = sem("bit_q2")
        bit_q2_turned = sem("bit_q2_turned")
        bit_q2_copied = sem("bit_q2_copied")
        bit_down = sem("bit_down")
        bit_scaled = sem("bit_scaled")
        bit_back = sem("bit_back")
        bit_x = sem("bit_x")
        mid_flat = act_m[:, :, :].rearrange("p a b -> p (a b)")
        AMAX, INV, DQ, DQ_G, DQ_U, SQ, VAR, RSTD, AMAX2, AMAX2C, INV2, Q2, DQ2 = range(13)

        def tile_loop(eng, ahead, body):
            ahead(0)
            body(0, lambda: ahead(1))
            with eng.Fori(0, TILES - 2) as i:
                body(i + 1, lambda: ahead(i + 2))
            body(TILES - 1, lambda: None)

        def bit_pe(pe):
            for tt in range(TILES):
                pe.wait_ge(bit_gated, tt // 4 + 1)
                for kc in range(KC):
                    mm = pe.transpose(bank[tt // 2][:, (tt % 2) * C + kc * P:(tt % 2) * C + kc * P + P],
                                      h[:, kc, tt * P:tt * P + P], ident[:, :])
                if tt % 2:
                    mm.then_inc(bit_turned, 1)
            for half in range(2):
                pe.wait_ge(bit_q, half + 1)
                for kc in range(KC):
                    for i in range(4):
                        mm = pe.transpose(bank[4 + half][:, :].bitcast(BF16)[:, kc * HALF + i * P:kc * HALF + i * P + P],
                                          hq_bf[:, half * 4 + i, kc * P:kc * P + P], ident_bf[:, :])
                mm.then_inc(bit_q_turned, 1)
            pe.wait_ge(bit_q_copied, 2)
            pe.wait_ge(wq_done, 3)

            def gate_up(t):
                if not (isinstance(t, int) and t == 0):
                    pe.wait_ge(bit_mid, t * 2)
                for n, w, done in ((0, wq_g, bit_gate), (1, wq_u, bit_up)):
                    for half in range(2):
                        for kc in range(KC):
                            mm = pe.matmul(bank[2 * n + half][:, :], hq_t[:, kc, DSZ(t * P, P)], w[:, kc, half * 512:half * 512 + 512],
                                           start=(kc == 0), stop=(kc == KC - 1))
                        mm.then_inc(done, 1)

            def tile(t, ahead):
                ahead()
                pe.wait_ge(bit_q2, t + 1)
                for ch in range(L2I // P):
                    mm = pe.transpose(bank[4][:, :].bitcast(BF16)[:, ch * P:ch * P + P], h2_bf[:, ch * P:ch * P + P], ident_bf[:, :])
                mm.then_inc(bit_q2_turned, 1)
                pe.wait_ge(bit_q2_copied, t + 1)
                for ch in range(L2I // P):
                    mm = pe.matmul(bank[5][:, 0:C], h2_t[:, ch, :], wq_d[:, ch, :], start=(ch == 0), stop=(ch == L2I // P - 1))
                mm.then_inc(bit_down, 1)
                pe.wait_ge(bit_scaled, t + 1)
                if not (isinstance(t, int) and t == 0):
                    pe.wait_ge(bit_x, t)
                for m in range(KC):
                    mm = pe.transpose(bank[6][:, m * P:m * P + P], y_sb[:, m * P:m * P + P], ident[:, :])
                mm.then_inc(bit_back, 1)
            tile_loop(pe, gate_up, tile)

        def bit_act(act):
            for half in range(2):
                tok = slice(half * HALF, half * HALF + HALF)
                act.wait_ge(mixer_x, 8)
                act.activation(h[:, :, tok], x[:, :, tok], ACT.Tanh, scale=0.5).then_inc(bit_tanh, 1)
            for half in range(2):
                act.wait_ge(bit_q_turned, half + 1)
                act.activation(hq_t[:, :, half * HALF:half * HALF + HALF],
                               bank[4 + half][:, :].bitcast(BF16).rearrange("p (k t) -> p k t", k=KC), ACT.Copy).then_inc(bit_q_copied, 1)

            def silu(t):
                act.wait_ge(bit_gate, t * 2 + 2)
                act.wait_ge(bit_q_copied, 2)
                for half in range(2):
                    act.activation(act_s[:, half, :], bank[half][:, :], ACT.Silu, scale=bstat[:, DQ_G, DSZ(t, 1)]).then_inc(bit_silu, 1)

            def squares(t):
                act.wait_ge(bit_mid, t * 2 + 2)
                act.wait_ge(bit_q_copied, 2)
                act.activation(h[:, 0, :], mid_flat, ACT.Square, accum_out=bstat[:, SQ, DSZ(t, 1)]).then_inc(bit_sq, 1)

            def tile(t, ahead):
                if isinstance(t, int) and t == 0:
                    squares(0)
                ahead()
                act.wait_ge(bit_q2_turned, t + 1)
                act.activation(h2_t[:, :, :].rearrange("p a b -> p (a b)"), bank[4][:, :].bitcast(BF16), ACT.Copy).then_inc(bit_q2_copied, 1)
                if not (isinstance(t, int) and t == TILES - 1):
                    squares(t + 1)
                act.wait_ge(bit_down, t + 1)
                act.wait_ge(bit_q_copied, 2)
                act.activation(y_sb[:, :], bank[5][:, 0:C], ACT.Identity, scale=bstat[:, DQ2, DSZ(t, 1)]).then_inc(bit_scaled, 1)
            tile_loop(act, silu, tile)

        def bit_pool(pool):
            with pool.Fori(0, TILES) as t:
                pool.wait_ge(bit_var, t + 1)
                pool.tensor_tensor(bstat[:, RSTD, DSZ(t, 1)], bstat[:, VAR, DSZ(t, 1)], half_c[:, 0:1], ALU.pow).then_inc(bit_rstd, 1)

        def bit_dve(dve):
            for half in range(2):
                tok = slice(half * HALF, half * HALF + HALF)
                dve.wait_ge(bit_tanh, half + 1)
                dve.scalar_tensor_tensor(out=h[:, :, tok], in0=h[:, :, tok], scalar=1.0, in1=G[:, G_SLOT[5], :, tok],
                                         op0=ALU.add, op1=ALU.mult).then_inc(bit_gated, 1)
            for pair in range(4):
                dve.wait_ge(bit_turned, pair + 1)
                dve.tensor_reduce(bstat[:, AMAX, 2 * pair:2 * pair + 2], bank[pair][:, :].rearrange("p (a c) -> p a c", a=2),
                                  AX.X, ALU.max, apply_absolute_value=True).then_inc(bit_step, 1)
            dve.wait_ge(bit_step, 4)
            dve.tensor_scalar(bstat[:, AMAX, :], bstat[:, AMAX, :], 1e-5, None, ALU.max).then_inc(bit_step, 1)
            dve.wait_ge(bit_step, 5)
            dve.reciprocal(bstat[:, INV, :], bstat[:, AMAX, :]).then_inc(bit_step, 1)
            dve.tensor_scalar(bstat[:, DQ_G, :], bstat[:, AMAX, :], wq_stat[:, 0, 1:2], 1.0 / 127.0, ALU.mult, ALU.mult).then_inc(bit_step, 1)
            dve.tensor_scalar(bstat[:, DQ_U, :], bstat[:, AMAX, :], wq_stat[:, 1, 1:2], 1.0 / 127.0, ALU.mult, ALU.mult).then_inc(bit_step, 1)
            dve.wait_ge(bit_step, 6)
            dve.tensor_scalar(bstat[:, INV, :], bstat[:, INV, :], 127.0, None, ALU.mult).then_inc(bit_step, 1)
            dve.wait_ge(bit_step, 9)
            for half, buf in enumerate((act_s, act_m)):
                flat = buf[:, :, :].rearrange("p a b -> p (a b)")
                for i in range(4):
                    tt = half * 4 + i
                    dve.tensor_scalar(flat[:, i * C:i * C + C], bank[tt // 2][:, (tt % 2) * C:(tt % 2) * C + C],
                                      bstat[:, INV, tt:tt + 1], MAGIC, ALU.mult, ALU.add).then_inc(bit_step, 1)
                dve.wait_ge(bit_step, 9 + 4 * half + 4)
                dve.tensor_scalar(hq_bf[:, half * 4:half * 4 + 4, :].rearrange("p a b -> p (a b)"), flat, -MAGIC, 127.0,
                                  ALU.add, ALU.min).then_inc(bit_q, 1)

            dve.wait_ge(ln_in, 16)
            mid = act_m[:, :, :].rearrange("p a b -> p (a b)")
            scaled = act_a[:, :, :].rearrange("p a b -> p (a b)")

            def middle(t):
                for half in range(2):
                    dve.wait_ge(bit_silu, t * 2 + half + 1)
                    dve.wait_ge(bit_up, t * 2 + half + 1)
                    dve.scalar_tensor_tensor(out=act_m[:, half, :], in0=bank[2 + half][:, :], scalar=bstat[:, DQ_U, DSZ(t, 1)],
                                             in1=act_s[:, half, :], op0=ALU.mult, op1=ALU.mult).then_inc(bit_mid, 1)

            def to_stream(t):
                dve.wait_ge(bit_back, t + 1)
                xs = x[:, :, DSZ(t * P, P)]
                dve.tensor_tensor(xs, bank[6][:, 0:C].rearrange("p (m t) -> p m t", m=KC), xs, ALU.add).then_inc(bit_x, 1)

            def tile(t, ahead):
                st = lambda i: bstat[:, i, DSZ(t, 1)]
                dve.wait_ge(bit_mid, t * 2 + 2)
                dve.tensor_tensor(scaled, mid, ln_bc, ALU.mult).then_inc(bit_norm, 1)
                dve.wait_ge(bit_norm, t * 7 + 1)
                dve.tensor_reduce(st(AMAX2), scaled, AX.X, ALU.max, apply_absolute_value=True).then_inc(bit_norm, 1)
                dve.wait_ge(bit_sq, t + 1)
                dve.tensor_scalar(st(VAR), st(SQ), 1.0 / L2I, 1e-6, ALU.mult, ALU.add).then_inc(bit_var, 1)
                dve.wait_ge(bit_rstd, t + 1)
                dve.wait_ge(bit_norm, t * 7 + 2)
                dve.tensor_scalar(st(AMAX2C), st(AMAX2), st(RSTD), 1e-5, ALU.mult, ALU.max).then_inc(bit_norm, 1)
                dve.wait_ge(bit_norm, t * 7 + 3)
                dve.reciprocal(st(INV2), st(AMAX2C)).then_inc(bit_norm, 1)
                dve.tensor_scalar(st(DQ2), st(AMAX2C), wq_stat[:, 2, 1:2], 1.0 / 127.0, ALU.mult, ALU.mult).then_inc(bit_norm, 1)
                dve.wait_ge(bit_norm, t * 7 + 4)
                dve.tensor_scalar(st(Q2), st(INV2), st(RSTD), 127.0, ALU.mult, ALU.mult).then_inc(bit_norm, 1)
                dve.wait_ge(bit_norm, t * 7 + 6)
                dve.tensor_scalar(mid, scaled, st(Q2), MAGIC, ALU.mult, ALU.add).then_inc(bit_norm, 1)
                dve.wait_ge(bit_norm, t * 7 + 7)
                dve.tensor_scalar(h2_bf[:, :], mid, -MAGIC, 127.0, ALU.add, ALU.min).then_inc(bit_q2, 1)
                dve.wait_ge(bit_q2, t + 1)
                ahead()
                if not (isinstance(t, int) and t == 0):
                    to_stream(t - 1)
            tile_loop(dve, middle, tile)
            to_stream(TILES - 1)

        ROPE4 = [2, 3, 0, 1] + list(range(4, 32))
        ROPE32 = list(range(16, 32)) + list(range(16))
        A0 = Attention("L0", 0, [1, 2], 4, True, 1.0, False, (ROPE4, 0), True, 2 * GROUPS, 16, 16, False, x_in, 16, 0, sem("rope_step_0"))
        F0 = Experts("L0", 1, 25, 16, 11, 3, A0.x_done, 4, 0,
                     lambda c: io["L0_w"][c] if c < 2 else (io["L0_w"],), None, 0)
        A1 = Attention("L1", 2, [4, 5], 16, False, 0.25, False, None, False, 2 * GROUPS + KC, 16, 16, True, F0.x_done, 4, 4, None)
        F1 = Experts("L1", 3, 11, 8, 11, 6, A1.x_done, 8, 1,
                     lambda c: io["L1_w"][c] if c < 2 else (io["L1_w"],), F0, 1)
        A3 = Attention("L3", 6, [7], 28, True, 1.0, True, (ROPE32, 2), False, None, 32, 8, False, bit_x, TILES, 8, sem("rope_step_3"))
        F3 = Experts("L3", 7, 16, 8, 16, None, A3.x_done, 12, 2,
                     lambda c: lora_dram[c] if c < 4 else (io["L3_w"],), F1, 2)
        out_done = sem("out_done")

        block = ctx.enter_context(nc.Block())

        @block.sync
        def _(sp):
            setup_sp(sp)
            F0.prefetch_sp(sp)
            sp.wait_ge(A0.out, B)
            sp.dma_start(w_attn[:, :, :], io["L1_w_attn"]).then_inc(attn_w["L1"], 16)
            sp.dma_start(w_out[:, :, :], io["L1_w_out"]).then_inc(attn_w["L1"], 16)
            F0.sp(sp)
            F1.prefetch_sp(sp)
            sp.wait_ge(A1.out, 2 * B)
            sp.dma_start(w_attn[:, :, 0:2 * C], io["L2_cd"]).then_inc(cd_w, 16)
            sp.dma_start(ln_bc, io["L2_ln"].unsqueeze(0).to_broadcast([P, L2I])).then_inc(ln_in, 16)
            F1.sp(sp)
            sp.wait_ge(F1.d_lo, F1.chunks)
            sp.wait_ge(F1.gu_lo, F1.chunks + 1)
            lora_sp(sp, 0)
            lora_out_sp(sp, 0)
            lora_sp(sp, 1)
            sp.wait_ge(mixer_mm, 8)
            sp.dma_start(w_attn[:, :, :], io["L3_w_attn"]).then_inc(attn_w["L3"], 16)
            sp.dma_start(w_out[:, :, :], io["L3_w_out"]).then_inc(attn_w["L3"], 16)
            lora_out_sp(sp, 1)
            F3.prefetch_sp(sp)
            F3.sp(sp)
            sp.wait_ge(F3.x_done, 12)
            sp.dma_start(out, x[:, :, :]).then_inc(out_done, 16)
            sp.wait_ge(out_done, 16)

        @block.scalar
        def _(act):
            setup_act(act)
            A0.act(act)
            F0.act(act)
            A1.act(act)
            F1.act(act)
            mixer_act(act)
            bit_act(act)
            A3.act(act)
            F3.act(act)

        @block.vector
        def _(dve):
            setup_dve(dve)
            A0.dve(dve)
            F0.dve(dve)
            A1.dve(dve)
            F1.dve(dve)
            lora_dve(dve, 0)
            mixer_dve(dve)
            lora_dve(dve, 1)
            bit_dve(dve)
            A3.dve(dve)
            F3.dve(dve)

        @block.tensor
        def _(pe):
            setup_pe(pe)
            A0.pe(pe)
            F0.pe(pe)
            A1.pe(pe)
            F1.pe(pe)
            lora_pe(pe, 0)
            mixer_pe(pe)
            lora_pe(pe, 1)
            bit_pe(pe)
            A3.pe(pe)
            F3.pe(pe)

        @block.gpsimd
        def _(pool):
            setup_pool(pool)
            A0.pool(pool)
            F0.pool(pool)
            A1.pool(pool)
            F1.pool(pool)
            bit_pool(pool)
            A3.pool(pool)
            F3.pool(pool)


def halves(w):
    return w.reshape(-1, P, w.shape[-1]).transpose(1, 0, 2)


def padded_heads(w):
    full = np.zeros((w.shape[0], HEADS, SLOT), w.dtype)
    full[:, :, :w.shape[2]] = w
    return full.reshape(w.shape[0], HEADS * SLOT)


def expert_chunks(gate, up, down):
    rows = gate.shape[0]
    chunks = -(-rows // P)
    out = np.zeros((chunks + 1, P, 768), gate.dtype)
    for n, w in enumerate((gate, up)):
        full = np.zeros((chunks * P, C), w.dtype)
        full[:rows] = w
        out[:chunks, :, n * 256:n * 256 + 256] = full.reshape(chunks, P, KC, P).transpose(0, 3, 2, 1).reshape(chunks, P, 256)
    full = np.zeros((chunks * P, C), down.dtype)
    full[:rows] = down
    out[:chunks, :, 512:] = full.reshape(chunks, P, C)
    return out


def rope_tables():
    tab = np.zeros((SLOT, 4, T), np.float32)
    tab[:, 0] = 1.0
    for first, dims in ((0, 4), (2, 32)):
        freq = (1.0 / np.float32(10000.0) ** (np.arange(0, dims, 2, dtype=np.float32) / np.float32(dims))).astype(np.float32)
        angle = (np.arange(T, dtype=np.float32)[None, :] * freq[:, None]).astype(np.float32)
        half = dims // 2
        tab[0:half, first], tab[half:dims, first] = np.cos(angle), np.cos(angle)
        tab[0:half, first + 1], tab[half:dims, first + 1] = -np.sin(angle), np.sin(angle)
    return np.tile(tab, (P // SLOT, 1, 1))


def kernel(**inputs):
    import concourse.bacc as bacc
    from concourse.bass_utils import run_bass_kernel_spmd

    v = {name: np.asarray(a) for name, a in inputs.items()}
    f32 = np.float32
    arrays = {}
    arrays["x"] = halves(v["x"].reshape(N, C).T)
    arrays["side"] = halves(v["fside_BxSxS_0"].reshape(N, C).T)
    arrays["cond"] = v["cond_512"]
    gates = [f"L{l}_{c}" for l in range(4) for c in ("cond", "cond2")]
    wu = np.stack([np.stack([v[f"{g}_{k}"] for g in gates], -1) for k in "wu"])
    arrays["wu"] = wu.reshape(2, KC, P, CONDS).transpose(2, 0, 1, 3)

    qkv0 = v["L0_attn_w_qkv"].reshape(C, HEADS, 3, 16)
    qkv1 = v["L1_attn_Wqkv"].T.reshape(C, HEADS // 4, 4, 3, 16).transpose(0, 2, 1, 3, 4).reshape(C, HEADS, 3, 16)
    for name, qkv in (("L0", qkv0), ("L1", qkv1)):
        arrays[f"{name}_w_attn"] = halves(np.concatenate(
            [padded_heads(qkv[:, :, 0]), padded_heads(qkv[:, :, 1]), qkv[:, :, 2].reshape(C, C)], 1))
    wk = np.repeat(v["L3_attn_Wk"].reshape(C, 8, 32), 2, axis=1).reshape(C, 512)
    arrays["L3_w_attn"] = halves(np.concatenate([v["L3_attn_Wq"], wk, v["L3_attn_Wv"]], 1))
    arrays["L0_w_out"] = halves(padded_heads(v["L0_attn_w_out"].T.reshape(C, HEADS, 16)).T)
    arrays["L1_w_out"] = halves(padded_heads(v["L1_attn_Wproj"].reshape(C, HEADS, 16)).T)
    arrays["L3_w_out"] = halves(v["L3_attn_Wo"])
    b0 = v["L0_attn_b_qkv"].reshape(1, HEADS, 3, 16)
    arrays["attn_bias"] = np.concatenate(
        [padded_heads(b0[:, :, 0]).reshape(GROUPS, P).T, padded_heads(b0[:, :, 1]).reshape(GROUPS, P).T,
         v["L0_attn_b_out"].reshape(KC, P).T, v["L1_attn_bproj"].reshape(KC, P).T], 1)
    arrays["L0_bias_v"] = b0[0, :, 2].reshape(C)
    arrays["rope"] = rope_tables()
    arrays["earlier"] = np.tile(np.tril(np.ones((16, 16), f32), -1)[None], (P, 1, 1))
    route = np.zeros((P, 3, KC, 16), f32)
    route[:, 0] = halves(v["L0_ffn_gate_w"].T)
    route[:, 1, :, 0:8] = halves(v["L1_ffn_router_w"].T)
    route[:, 2, :, 0:8] = halves(v["L3_ffn_Wr"])
    arrays["w_route"] = route
    arrays["temp"] = v["L3_ffn_temperature"].reshape(1)
    arrays["scan_c"] = np.concatenate([v[f"L2_attn_{n}"].reshape(KC, P).T for n in ("C_b", "D_b", "log_delta")], 1)
    arrays["scan_ab"] = np.stack([halves(v["L2_attn_A"]), halves(v["L2_attn_B"])], 1)
    arrays["L2_cd"] = np.concatenate([halves(v["L2_attn_C_w"].T), halves(v["L2_attn_D_w"].T)], 2)
    arrays["L2_ln"] = v["L2_ffn_ln_weight"]
    arrays["L2_w_gate"] = halves(v["L2_ffn_w_gate"].T)
    arrays["L2_w_up"] = halves(v["L2_ffn_w_up"].T)
    arrays["L2_w_down"] = halves(v["L2_ffn_w_down"].T).reshape(P, KC, L2I)

    half = 176
    w13, sw13 = v["L0_ffn_w13"], v["L0_ffn_sw13"]
    arrays["L0_w"] = expert_chunks(
        np.concatenate([w13[:, :half].reshape(-1, C), sw13[:2 * half]]),
        np.concatenate([w13[:, half:].reshape(-1, C), sw13[2 * half:]]),
        np.concatenate([v["L0_ffn_w2"].transpose(0, 2, 1).reshape(-1, C), v["L0_ffn_sw2"].T]))
    arrays["L1_w"] = expert_chunks(v["L1_ffn_gate_w"].reshape(-1, C), v["L1_ffn_up_w"].reshape(-1, C),
                                   v["L1_ffn_down_w"].transpose(0, 2, 1).reshape(-1, C))
    arrays["L3_w"] = expert_chunks(v["L3_ffn_Wg"].transpose(0, 2, 1).reshape(-1, C),
                                   v["L3_ffn_Wu"].transpose(0, 2, 1).reshape(-1, C), v["L3_ffn_Wd"].reshape(-1, C))
    arrays["lora"] = np.concatenate(
        [v["L3_ffn_Ga"].transpose(0, 2, 1), v["L3_ffn_Gb"], v["L3_ffn_Ua"].transpose(0, 2, 1), v["L3_ffn_Ub"],
         v["L3_ffn_Da"].transpose(0, 2, 1), v["L3_ffn_Db"]], 2).reshape(2, 64, 2, 768)
    arrays = {name: np.ascontiguousarray(a) for name, a in arrays.items()}

    nc = bacc.Bacc("TRN2", target_bir_lowering=False, num_devices=1)
    io = {name: nc.dram_tensor(f"in_{name}", a.shape, mybir.dt.from_np(a.dtype), kind="ExternalInput").ap() for name, a in arrays.items()}
    out = nc.dram_tensor("out", (P, KC, N), F32, kind="ExternalOutput").ap()
    build(nc, io, out)
    r = run_bass_kernel_spmd(nc, [{f"in_{name}": a for name, a in arrays.items()}], core_ids=[0])
    y = r.results[0]["out"]
    return np.ascontiguousarray(y.transpose(1, 0, 2).reshape(C, N).T.reshape(B, T, C))
```
